# Optimizing a Trainium2 kernel written in Bass

```python
import numpy as np
import jax
import jax.numpy as jnp

def _softmax(x, axis=-1):
    return jax.nn.softmax(x, axis=axis)

def _gelu(x):
    return jax.nn.gelu(x, approximate=True)

def _silu(x):
    return jax.nn.silu(x)

def _sigmoid(x):
    return jax.nn.sigmoid(x)

def _layernorm(x, axis=-1, eps=1e-05):
    m = jnp.mean(x, axis=axis, keepdims=True)
    v = jnp.var(x, axis=axis, keepdims=True)
    return (x - m) / jnp.sqrt(v + eps)

def _scatter_add(tgt, idx, src, axis=0):
    return tgt.at[idx].add(src)

def _segment_sum(src, seg, n):
    return jax.ops.segment_sum(src, seg, n)
kernel_name = 'mk_flamingo_gated_d2_seqx_r4_d16162'

def setup_inputs(seed: int=0):
    np.random.seed(seed)
    _w = jnp.asarray

    def _rec_inputs():
        import jax
        import jax.numpy as jnp
        _rk = jax.random.key(seed)
        x = -0.0002928 + 1 * jax.random.normal(jax.random.fold_in(_rk, 1), (4, 512, 512), jnp.float32)
        _lenS = 512 - jax.random.randint(jax.random.fold_in(_rk, 7), (4,), 0, max(1, 512 // 4) + 1, jnp.int32)
        _lenS2 = 512 - jax.random.randint(jax.random.fold_in(_rk, 8), (4,), 0, max(1, 512 // 4) + 1, jnp.int32)
        _ctx_2048P = jax.random.normal(jax.random.fold_in(_rk, 11), (4, 16, 512), jnp.float32)
        _ctx_2048c = jax.random.dirichlet(jax.random.fold_in(_rk, 511), 0.3 * jnp.ones((16,), jnp.float32), (4, 512))
        _ctx_2048t = jnp.einsum('bsk,bkd->bsd', _ctx_2048c, _ctx_2048P)
        _ctx_2048t = _ctx_2048t * jax.lax.rsqrt(jnp.mean(jnp.square(_ctx_2048t)) + 1e-12) * 0.953939
        ctx_2048 = -1.39393e-06 + 0.999914 * (_ctx_2048t + 0.3 * jax.random.normal(jax.random.fold_in(_rk, 611), (4, 512, 512), jnp.float32))
        _g = jax.random.normal(jax.random.fold_in(_rk, 9001), (2, 2), jnp.float32)
        _g = jnp.sign(_g) * jnp.maximum(jnp.abs(_g), 1.0) + (_g == 0) * 1.0
        g_xattn = _g[0]
        g_ffn = _g[1]
        return (x, ctx_2048, g_xattn, g_ffn)
    x, ctx_2048, g_xattn, g_ffn = _rec_inputs()

    def _L0_xattn_setup():
        import jax, jax.numpy as jnp
        import numpy as np
        B, S, E, NH = (2, 256, 512, 16)
        DH = E // NH
        EPS = 1e-06

        def _mlstm_forward(q, k, v, Wi, bi, Wf, bf, ln_scale):
            b, s, e = q.shape
            nh = Wi.shape[1]
            dh = e // nh
            x = jnp.concatenate([q, k, v], axis=-1)
            ig = (x @ Wi + bi).transpose(0, 2, 1)[..., None]
            fg = (x @ Wf + bf).transpose(0, 2, 1)[..., None]
            split = lambda t: t.reshape(b, s, nh, dh).transpose(0, 2, 1, 3)
            qh, kh, vh = (split(q), split(k), split(v))
            log_f = jax.nn.log_sigmoid(fg)
            log_f_cum = jnp.concatenate([jnp.zeros((b, nh, 1, 1), q.dtype), jnp.cumsum(log_f, axis=2)], axis=2)
            fg_mat = log_f_cum - jnp.transpose(log_f_cum, (0, 1, 3, 2))
            ltr = jnp.tril(jnp.ones((s, s), dtype=bool))
            log_fg = jnp.where(ltr, fg_mat[:, :, 1:, 1:], -jnp.inf)
            log_D = log_fg + jnp.transpose(ig, (0, 1, 3, 2))
            max_log_D = jnp.max(log_D, axis=-1, keepdims=True)
            D = jnp.exp(log_D - max_log_D)
            qk = jnp.einsum('bhsd,bhtd->bhst', qh, kh) / jnp.sqrt(jnp.asarray(dh, q.dtype))
            C = qk * D
            normalizer = jnp.maximum(jnp.abs(C.sum(-1, keepdims=True)), jnp.exp(-max_log_D))
            Cn = C / (normalizer + EPS)
            h = jnp.einsum('bhst,bhtd->bhsd', Cn, vh)
            mu = h.mean(-1, keepdims=True)
            var = ((h - mu) ** 2).mean(-1, keepdims=True)
            hn = (h - mu) * jax.lax.rsqrt(var + EPS)
            hn = hn * ln_scale.reshape(1, nh, 1, dh)
            return hn.transpose(0, 2, 1, 3).reshape(b, s, e)
        key = jax.random.key(seed)
        ks = jax.random.split(key, 6)
        q = jax.random.normal(ks[0], (B, S, E), dtype=jnp.float32)
        k = jax.random.normal(ks[1], (B, S, E), dtype=jnp.float32)
        v = jax.random.normal(ks[2], (B, S, E), dtype=jnp.float32)
        Wi = jax.random.normal(ks[3], (3 * E, NH), dtype=jnp.float32) * 0.02
        bi = jax.random.normal(ks[4], (NH,), dtype=jnp.float32) * 0.1
        Wf = jax.random.normal(ks[5], (3 * E, NH), dtype=jnp.float32) * 0.02
        bf = jnp.linspace(3.0, 6.0, NH, dtype=jnp.float32)
        ln_scale = jnp.ones((E,), dtype=jnp.float32)
        return {'q': q, 'k': k, 'v': v, 'Wi': Wi, 'bi': bi, 'Wf': Wf, 'bf': bf, 'ln_scale': ln_scale}
    _L0_xattn_all = _L0_xattn_setup()
    _L0_xattn_in = {k: v for k, v in _L0_xattn_all.items() if k in ('Wi', 'bi', 'Wf', 'bf', 'ln_scale')}
    del _L0_xattn_all

    def _L0_ffn_setup():
        import jax, jax.numpy as jnp
        import numpy as np
        HIDDEN = 512
        INTER = 2048
        COMPRESSION = 128.9

        def _n_ctrl(out_size, in_size):
            return max(16, int(out_size * in_size / COMPRESSION))

        def _catmull_rom_grid(n_ctrl, n_samples):
            t = np.linspace(0.0, n_ctrl - 1.0, n_samples, dtype=np.float64)
            i = np.clip(np.floor(t).astype(np.int64), 0, n_ctrl - 2)
            f = (t - i).astype(np.float32)
            idx = np.stack([np.clip(i + k, 0, n_ctrl - 1) for k in (-1, 0, 1, 2)], axis=0)
            return (jnp.asarray(idx.astype(np.int32)), jnp.asarray(f))

        def spline_reconstruct(control_points, out_size, in_size):
            n = out_size * in_size
            idx, f = _catmull_rom_grid(control_points.shape[0], n)
            p0, p1, p2, p3 = (control_points[idx[0]], control_points[idx[1]], control_points[idx[2]], control_points[idx[3]])
            f2 = f * f
            f3 = f2 * f
            w = 0.5 * (2.0 * p1 + (p2 - p0) * f + (2.0 * p0 - 5.0 * p1 + 4.0 * p2 - p3) * f2 + (3.0 * p1 - p0 - 3.0 * p2 + p3) * f3)
            return w.reshape(out_size, in_size)
        key = jax.random.key(seed)
        k0, k1, k2, k3 = jax.random.split(key, 4)
        hidden_states = jax.random.normal(k0, (4, 512, HIDDEN), dtype=jnp.float32)
        gate_cp = jax.random.normal(k1, (_n_ctrl(INTER, HIDDEN),), dtype=jnp.float32) * 0.02
        up_cp = jax.random.normal(k2, (_n_ctrl(INTER, HIDDEN),), dtype=jnp.float32) * 0.02
        down_cp = jax.random.normal(k3, (_n_ctrl(HIDDEN, INTER),), dtype=jnp.float32) * 0.02
        return {'hidden_states': hidden_states, 'gate_cp': gate_cp, 'up_cp': up_cp, 'down_cp': down_cp}
    _L0_ffn_all = _L0_ffn_setup()
    _L0_ffn_in = {k: v for k, v in _L0_ffn_all.items() if k in ('gate_cp', 'up_cp', 'down_cp')}
    del _L0_ffn_all

    def _L1_xattn_setup():
        import jax, jax.numpy as jnp
        import numpy as np
        import math
        N_HEADS = 8
        key = jax.random.key(seed)
        k1, k2, k3 = jax.random.split(key, 3)
        N, W, T, S = (4, 128, 512, 512)
        q = jax.random.normal(k1, (N, W, T), dtype=jnp.float32)
        k = jax.random.normal(k2, (N, W, S), dtype=jnp.float32)
        v = jax.random.normal(k3, (N, W, S), dtype=jnp.float32)
        return {'q': q, 'k': k, 'v': v}
    _L1_xattn_all = _L1_xattn_setup()
    _L1_xattn_in = {k: v for k, v in _L1_xattn_all.items() if k in ()}
    del _L1_xattn_all

    def _L1_ffn_setup():
        import jax, jax.numpy as jnp
        import numpy as np
        _FP8_MAX = 448.0
        _BLOCK = 32
        _EPS = 1e-30

        def _mx_dequant(t):
            rows, feat = t.shape
            blocks = t.reshape(rows, feat // _BLOCK, _BLOCK)
            max_abs = jnp.max(jnp.abs(blocks), axis=-1)
            scales = jnp.maximum(max_abs / _FP8_MAX, _EPS)
            q = (blocks / scales[..., None]).astype(jnp.float8_e4m3fn).astype(jnp.float32)
            return (q * scales[..., None]).reshape(rows, feat)

        def _mx_linear(x2d, w):
            return _mx_dequant(x2d) @ _mx_dequant(w).T
        key = jax.random.key(seed)
        k1, k2, k3, k4 = jax.random.split(key, 4)
        B, S, H, I = (2, 256, 512, 2048)
        return {'x': jax.random.normal(k1, (B, S, H), dtype=jnp.float32), 'gate_w': jax.random.normal(k2, (I, H), dtype=jnp.float32) * 0.02, 'up_w': jax.random.normal(k3, (I, H), dtype=jnp.float32) * 0.02, 'down_w': jax.random.normal(k4, (H, I), dtype=jnp.float32) * 0.02}
    _L1_ffn_all = _L1_ffn_setup()
    _L1_ffn_in = {k: v for k, v in _L1_ffn_all.items() if k in ('gate_w', 'up_w', 'down_w')}
    del _L1_ffn_all
    return {'x': x, 'ctx_2048': ctx_2048, 'g_xattn': g_xattn, 'g_ffn': g_ffn, 'L0_xattn_Wi': _L0_xattn_in['Wi'], 'L0_xattn_bi': _L0_xattn_in['bi'], 'L0_xattn_Wf': _L0_xattn_in['Wf'], 'L0_xattn_bf': _L0_xattn_in['bf'], 'L0_xattn_ln_scale': _L0_xattn_in['ln_scale'], 'L0_ffn_gate_cp': _L0_ffn_in['gate_cp'], 'L0_ffn_up_cp': _L0_ffn_in['up_cp'], 'L0_ffn_down_cp': _L0_ffn_in['down_cp'], 'L1_ffn_gate_w': _L1_ffn_in['gate_w'], 'L1_ffn_up_w': _L1_ffn_in['up_w'], 'L1_ffn_down_w': _L1_ffn_in['down_w']}

def reference(x, ctx_2048, g_xattn, g_ffn, L0_xattn_Wi, L0_xattn_bi, L0_xattn_Wf, L0_xattn_bf, L0_xattn_ln_scale, L0_ffn_gate_cp, L0_ffn_up_cp, L0_ffn_down_cp, L1_ffn_gate_w, L1_ffn_up_w, L1_ffn_down_w):
    import jax
    import jax.numpy as jnp

    def _L0_xattn_ref(q, k, v, Wi, bi, Wf, bf, ln_scale):
        import jax, jax.numpy as jnp
        import numpy as np
        B, S, E, NH = (2, 256, 512, 16)
        DH = E // NH
        EPS = 1e-06

        def _mlstm_forward(q, k, v, Wi, bi, Wf, bf, ln_scale):
            b, s, e = q.shape
            nh = Wi.shape[1]
            dh = e // nh
            x = jnp.concatenate([q, k, v], axis=-1)
            ig = (x @ Wi + bi).transpose(0, 2, 1)[..., None]
            fg = (x @ Wf + bf).transpose(0, 2, 1)[..., None]
            split = lambda t: t.reshape(b, s, nh, dh).transpose(0, 2, 1, 3)
            qh, kh, vh = (split(q), split(k), split(v))
            log_f = jax.nn.log_sigmoid(fg)
            log_f_cum = jnp.concatenate([jnp.zeros((b, nh, 1, 1), q.dtype), jnp.cumsum(log_f, axis=2)], axis=2)
            fg_mat = log_f_cum - jnp.transpose(log_f_cum, (0, 1, 3, 2))
            ltr = jnp.tril(jnp.ones((s, s), dtype=bool))
            log_fg = jnp.where(ltr, fg_mat[:, :, 1:, 1:], -jnp.inf)
            log_D = log_fg + jnp.transpose(ig, (0, 1, 3, 2))
            max_log_D = jnp.max(log_D, axis=-1, keepdims=True)
            D = jnp.exp(log_D - max_log_D)
            qk = jnp.einsum('bhsd,bhtd->bhst', qh, kh) / jnp.sqrt(jnp.asarray(dh, q.dtype))
            C = qk * D
            normalizer = jnp.maximum(jnp.abs(C.sum(-1, keepdims=True)), jnp.exp(-max_log_D))
            Cn = C / (normalizer + EPS)
            h = jnp.einsum('bhst,bhtd->bhsd', Cn, vh)
            mu = h.mean(-1, keepdims=True)
            var = ((h - mu) ** 2).mean(-1, keepdims=True)
            hn = (h - mu) * jax.lax.rsqrt(var + EPS)
            hn = hn * ln_scale.reshape(1, nh, 1, dh)
            return hn.transpose(0, 2, 1, 3).reshape(b, s, e)
        return _mlstm_forward(q, k, v, Wi, bi, Wf, bf, ln_scale)

    def _L0_ffn_ref(hidden_states, gate_cp, up_cp, down_cp):
        import jax, jax.numpy as jnp
        import numpy as np
        HIDDEN = 512
        INTER = 2048
        COMPRESSION = 128.9

        def _n_ctrl(out_size, in_size):
            return max(16, int(out_size * in_size / COMPRESSION))

        def _catmull_rom_grid(n_ctrl, n_samples):
            t = np.linspace(0.0, n_ctrl - 1.0, n_samples, dtype=np.float64)
            i = np.clip(np.floor(t).astype(np.int64), 0, n_ctrl - 2)
            f = (t - i).astype(np.float32)
            idx = np.stack([np.clip(i + k, 0, n_ctrl - 1) for k in (-1, 0, 1, 2)], axis=0)
            return (jnp.asarray(idx.astype(np.int32)), jnp.asarray(f))

        def spline_reconstruct(control_points, out_size, in_size):
            n = out_size * in_size
            idx, f = _catmull_rom_grid(control_points.shape[0], n)
            p0, p1, p2, p3 = (control_points[idx[0]], control_points[idx[1]], control_points[idx[2]], control_points[idx[3]])
            f2 = f * f
            f3 = f2 * f
            w = 0.5 * (2.0 * p1 + (p2 - p0) * f + (2.0 * p0 - 5.0 * p1 + 4.0 * p2 - p3) * f2 + (3.0 * p1 - p0 - 3.0 * p2 + p3) * f3)
            return w.reshape(out_size, in_size)
        gate_w = spline_reconstruct(gate_cp, INTER, HIDDEN)
        up_w = spline_reconstruct(up_cp, INTER, HIDDEN)
        down_w = spline_reconstruct(down_cp, HIDDEN, INTER)
        gate = jnp.einsum('bsh,ih->bsi', hidden_states, gate_w)
        up = jnp.einsum('bsh,ih->bsi', hidden_states, up_w)
        inter = jax.nn.silu(gate) * up
        return jnp.einsum('bsi,hi->bsh', inter, down_w)

    def _L1_xattn_ref(q, k, v):
        import jax, jax.numpy as jnp
        import numpy as np
        import math
        N_HEADS = 8
        bs, width, T = q.shape
        S = k.shape[-1]
        ch = width // N_HEADS
        qh = q.reshape(bs * N_HEADS, ch, T)
        kh = k.reshape(bs * N_HEADS, ch, S)
        vh = v.reshape(bs * N_HEADS, ch, S)
        scale = 1.0 / math.sqrt(ch)
        attn = jnp.einsum('bct,bcs->bts', qh * scale, kh * scale)
        attn = jax.nn.softmax(attn, axis=-1)
        out = jnp.einsum('bts,bcs->bct', attn, vh)
        return out.reshape(bs, width, T)

    def _L1_ffn_ref(x, gate_w, up_w, down_w):
        import jax, jax.numpy as jnp
        import numpy as np
        _FP8_MAX = 448.0
        _BLOCK = 32
        _EPS = 1e-30

        def _mx_dequant(t):
            rows, feat = t.shape
            blocks = t.reshape(rows, feat // _BLOCK, _BLOCK)
            max_abs = jnp.max(jnp.abs(blocks), axis=-1)
            scales = jnp.maximum(max_abs / _FP8_MAX, _EPS)
            q = (blocks / scales[..., None]).astype(jnp.float8_e4m3fn).astype(jnp.float32)
            return (q * scales[..., None]).reshape(rows, feat)

        def _mx_linear(x2d, w):
            return _mx_dequant(x2d) @ _mx_dequant(w).T
        B, S, H = x.shape
        x2d = x.reshape(B * S, H)
        gate = _mx_linear(x2d, gate_w)
        up = _mx_linear(x2d, up_w)
        h = jax.nn.silu(gate) * up
        out = _mx_linear(h, down_w)
        return out.reshape(B, S, H)
    x = x + jnp.tanh(g_xattn[0]) * _L0_xattn_ref(_layernorm(x, axis=-1), ctx_2048, ctx_2048, L0_xattn_Wi, L0_xattn_bi, L0_xattn_Wf, L0_xattn_bf, L0_xattn_ln_scale)
    x = x + jnp.tanh(g_ffn[0]) * _L0_ffn_ref(_layernorm(x, axis=-1), L0_ffn_gate_cp, L0_ffn_up_cp, L0_ffn_down_cp)
    x = x + jnp.tanh(g_xattn[1]) * _L1_xattn_ref(_layernorm(x, axis=-1), ctx_2048, ctx_2048)
    x = x + jnp.tanh(g_ffn[1]) * _L1_ffn_ref(_layernorm(x, axis=-1), L1_ffn_gate_w, L1_ffn_up_w, L1_ffn_down_w)
    return x

_drawn_inputs = setup_inputs


def setup_inputs(seed=0):
    import zlib

    import numpy as np

    out = dict(_drawn_inputs(seed))
    spreads = {'g_ffn': (-1.0, 0.6), 'L0_xattn_ln_scale': (1.0, 0.2)}
    factors = {'L0_xattn_bi': 64.0,
     'L0_ffn_gate_cp': 3.783,
     'L0_ffn_up_cp': 4.265,
     'L0_ffn_down_cp': 3.989}
    for name, (base, spread) in spreads.items():
        noise = np.random.default_rng([zlib.crc32(name.encode()), seed]).standard_normal(out[name].shape)
        drawn = base * np.exp(spread * noise) if base else spread * noise
        out[name] = jnp.asarray(drawn.astype(out[name].dtype))
    for name, factor in factors.items():
        out[name] = (out[name] * factor).astype(out[name].dtype)
    return out
```

```python
from contextlib import ExitStack

import concourse.bass as bass
from concourse import mybir
import numpy as np

F32 = mybir.dt.float32
F16 = mybir.dt.float16
BF16 = mybir.dt.bfloat16
U32 = mybir.dt.uint32
U8 = mybir.dt.uint8
ALU = mybir.AluOpType
ACT = mybir.ActivationFunctionType
AX = mybir.AxisListType
RMAX = bass.bass_isa.ReduceOp.max
ds = bass.ds

P = 128
B, S, D = 4, 512, 512
NC = S // P
KD = D // P
TILES = B * NC
NH, DH = 16, 32
HG = P // DH
VW = DH + 1
INTER = 2048
KI = INTER // P


class Tally:

    def __init__(self, eng, sem, it, per):
        self.eng, self.sem, self.it, self.per, self.n = eng, sem, it, per, 0

    def inc(self, ins):
        self.n += 1
        ins.then_inc(self.sem, 1)

    def wait(self):
        self.eng.wait_ge(self.sem, self.it * self.per + self.n)

    def done(self):
        assert self.n == self.per, self.n


def shape_constants():
    ident = np.eye(P, dtype=np.float32)
    t, s = np.mgrid[0:P, 0:P]
    future = np.where(t > s, np.float32(-1e30), np.float32(0))
    k, h = np.mgrid[0:P, 0:NH]
    pick = ((k % 32 == h) & (k < 96)).astype(np.float32)
    p, c = np.mgrid[0:P, 0:HG * VW]
    own = np.where(p // DH == c // VW, np.float32(DH ** -0.5), np.float32(0))
    return np.concatenate([ident, future, pick, own, np.arange(P)[:, None]], axis=1).astype(np.float32)


CST_W = P + P + NH + HG * VW + 1


def mlstm_phase(nc, A, X, tg, CST, idf, idb, stack):
    def sb(name, shape, dt=F32):
        return stack.enter_context(nc.sbuf_tensor(name, shape, dt))

    def ps(name):
        return stack.enter_context(nc.psum_tensor(name, [P, 512], F32))

    sem = nc.alloc_semaphore
    XN = sb("XN", [P, NC, D])
    CTX = sb("CTX", [P, NC, D])
    QT = sb("QT", [P, KD, S])
    KT = sb("KT", [P, KD, S])
    VA = sb("VA", [P, NC, NH, VW])
    OUT = sb("OUT", [P, NC, NH, VW])
    HN = sb("HN", [P, NC * NH, DH])
    SQ = sb("SQ", [P, NC * NH, DH])
    KU = sb("KU", [P, 6, D])
    SS = sb("SS", [P, 2, NC - 1, HG * VW])
    DD = sb("DD", [P, 2, S])
    CC = sb("CC", [P, 2, S])
    WG = sb("WG", [P, 12, 32])
    GS = sb("GS", [P, NC, 2, 96])
    TM = sb("TM", [P, 13, NH])
    ROW = sb("ROW", [96, 8, S])
    ZF, ZI, AZ, MZ, LF, FC, FM, EL = (ROW[:, i, :] for i in range(8))
    VV = sb("VV", [96, 2, S])
    RR = sb("RR", [96, 2, S])
    NP = sb("NP", [96, 2, S], BF16)
    T2 = sb("T2", [96, 2, S], BF16)
    UW = sb("UW", [NH, 13, P])
    ONE = sb("ONE", [96, S])
    BIAS = sb("BIAS", [96, 2])
    GLN = sb("GLN", [P, D])
    ST = sb("ST", [P, NC, 6])
    MV = sb("MV", [P, NC, 2])
    SD = sb("SD", [P, NC])
    RS = sb("RS", [P, NC])
    MU = sb("MU", [P, NC * NH])
    VR = sb("VR", [P, NC * NH])
    DN = sb("DN", [P, NC * NH])
    FUT = sb("FUT", [P, NC, P], BF16)
    PICK = sb("PICK", [P, NH], BF16)
    EPS = sb("EPS", [P, 3])
    T = [ps("T0"), ps("T1")]
    QK = [ps("QK0"), ps("QK1")]
    E = [ps("E0"), ps("E1")]
    O = [ps("O0"), ps("O1")]

    ctx_loaded, w_loaded, pre_dve, pre_act = (sem("a_" + n) for n in ("ctx_loaded", "w_loaded", "pre_dve", "pre_act"))
    pre_pool = sem("a_pre_pool")
    mv_ready, sd_ready, xn_ready, t_ready = (sem("a_" + n) for n in ("mv_ready", "sd_ready", "xn_ready", "t_ready"))
    t_taken = [sem("a_t_taken0"), sem("a_t_taken1")]
    va_ready, ku_ready, az_ready, el_ready = (sem("a_" + n) for n in ("va_ready", "ku_ready", "az_ready", "el_ready"))
    vv_ready, np1_ready, rr_ready, t2_ready, r3_ready, np_ready, uw_ready = (
        sem("a_" + n) for n in ("vv_ready", "np1", "rr", "t2", "r3", "np_ready", "uw_ready"))
    gs_ready, ss_ready, qe_ready, d_ready, c_ready, pv_done, o_taken = (
        sem("a_" + n) for n in ("gs_ready", "ss_ready", "qe_ready", "d_ready", "c_ready", "pv_done", "o_taken"))
    hc_ready, sq_ready, vr_ready, sv_ready = (sem("a_" + n) for n in ("hc", "sq", "vr", "sv"))
    passed = [sem(f"a_passed{i}") for i in range(4)]
    dve_own, act_own = sem("a_dve_own"), sem("a_act_own")
    NT = 20
    ctx = A["ctx_2048"].rearrange("b (c p) d -> b p c d", p=P)

    with nc.Block() as block:
        @block.sync
        def _(sp):
            sp.dma_start(WG[:, :, 0:NH], A["L0_xattn_Wi"].rearrange("(k p) h -> p k h", p=P)).then_inc(w_loaded, 16)
            sp.dma_start(WG[:, :, NH:2 * NH], A["L0_xattn_Wf"].rearrange("(k p) h -> p k h", p=P)).then_inc(w_loaded, 16)
            sp.dma_start(GLN[:, :], A["L0_xattn_ln_scale"].rearrange("(a d) -> a d", a=1).to_broadcast([P, D])).then_inc(w_loaded, 16)
            sp.wait_ge(pre_pool, 3)
            for r in range(3):
                for q, name in enumerate(("L0_xattn_bi", "L0_xattn_bf")):
                    sp.dma_start(BIAS[32 * r:32 * r + NH, q:q + 1], A[name].rearrange("(h a) -> h a", a=1)).then_inc(w_loaded, 16)
            sp.dma_start(CTX[:, :, :], ctx[0]).then_inc(ctx_loaded, 16)
            with sp.Fori(1, B) as b:
                sp.wait_ge(t_ready, b * NT + (8 - NT))
                sp.sem_inc(passed[3], 1)
                sp.wait_ge(va_ready, b * 2)
                sp.wait_ge(ku_ready, b)
                sp.dma_start(CTX[:, :, :], ctx[ds(b, 1)].rearrange("a p c d -> p (a c) d")).then_inc(ctx_loaded, 16)

        @block.gpsimd
        def _(pool):
            pool.memset(BIAS[:, :], 0.0).then_inc(pre_pool, 1)
            pool.memset(GS[:, :, :, :], 0.0).then_inc(pre_pool, 1)
            pool.memset(VA[:, :, :, DH:VW], 1.0).then_inc(pre_pool, 1)
            with pool.Fori(0, B) as b:
                pool.wait_ge(xn_ready, b * NC + 1)
                pool.sem_inc(passed[0], 1)
                pool.memset(OUT[:, 0, :, :], 0.0).then_inc(va_ready, 1)
                pool.wait_ge(ctx_loaded, b * 16 + 16)
                pool.sem_inc(passed[0], 1)
                pool.tensor_copy(VA[:, :, :, 0:DH],
                                 CTX[:, :, :].rearrange("p c (h d) -> p c h d", h=NH)).then_inc(va_ready, 1)

        @block.scalar
        def _(act):
            with act.Fori(0, B) as b:
                own = Tally(act, act_own, b, ACT_OWN_A)
                act.wait_ge(mv_ready, b + 1)
                act.wait_ge(pre_dve, PRE_DVE)
                nc.scalar.activation(SD[:, :], MV[:, :, 1], ACT.Sqrt, bias=EPS[:, 0:1]).then_inc(sd_ready, 1)
                for n in range(0, 8, 2):
                    act.wait_ge(t_ready, b * NT + n + 1)
                    dst = (QT if n < 4 else KT)[:, n % 4, :]
                    nc.scalar.copy(dst, T[0][:, :]).then_inc(t_taken[0], 1)
                act.wait_ge(az_ready, b + 1)
                own.inc(nc.scalar.activation(EL, AZ, ACT.Exp, scale=-1.0))
                own.wait()
                nc.scalar.activation(EL, EL, ACT.Ln, bias=EPS[0:96, 1:2]).then_inc(el_ready, 1)
                act.wait_ge(vv_ready, b * 3 + 3)
                nc.scalar.copy(NP[:, :, :], VV[:, :, :]).then_inc(np1_ready, 1)
                i = 0
                for c in range(1, NC):
                    nc.scalar.activation(UW[:, i:i + c, :], VV[0:NH, 0, 0:c * P], ACT.Exp,
                                         bias=VV[0:NH, 1, c * P - 1:c * P]).then_inc(uw_ready, 1)
                    i += c
                act.wait_ge(rr_ready, b + 1)
                nc.scalar.copy(T2[64:96, :, :], RR[64:96, :, :]).then_inc(t2_ready, 1)
                own.inc(nc.scalar.copy(NP[32:64, :, :], RR[32:64, :, :]))
                for c in range(1, NC):
                    nc.scalar.activation(UW[:, 5 + c, :], VV[0:NH, 1, c * P:(c + 1) * P], ACT.Exp,
                                         bias=FM[0:NH, c:c + 1]).then_inc(uw_ready, 1)
                nc.scalar.activation(UW[:, 9:13, :], EL[0:NH, :], ACT.Exp, scale=-1.0).then_inc(uw_ready, 1)
                act.wait_ge(r3_ready, b + 1)
                nc.scalar.copy(NP[64:96, :, :], RR[64:96, :, :]).then_inc(np_ready, 1)
                for h in range(NH):
                    act.wait_ge(qe_ready, b * NH + h + 1)
                    if h >= 2:
                        act.wait_ge(c_ready, b * NH + h - 1)
                    nc.scalar.activation(DD[:, h % 2, :], E[h % 2][:, :], ACT.Exp).then_inc(d_ready, 1)
                act.wait_ge(hc_ready, b + 1)
                nc.scalar.activation(SQ[:, :, :], HN[:, :, :], ACT.Square).then_inc(sq_ready, 1)
                act.wait_ge(vr_ready, b + 1)
                nc.scalar.activation(VR[:, :], VR[:, :], ACT.Sqrt, scale=1.0 / DH, bias=EPS[:, 2:3]).then_inc(sv_ready, 1)
                own.done()

        @block.tensor
        def _(pe):
            pe.wait_ge(pre_dve, PRE_DVE)
            pe.wait_ge(w_loaded, 9 * 16)
            with pe.Fori(0, B) as b:
                def bank(n):
                    if n >= 2:
                        pe.wait_ge(t_taken[n % 2], b * (NT // 2) + n // 2)
                    return T[n % 2]

                def taken(n):
                    pe.wait_ge(t_taken[n % 2], b * (NT // 2) + n // 2 + 1)

                for n in range(8):
                    if n == 4:
                        pe.wait_ge(ctx_loaded, b * 16 + 16)
                    src, k = (XN if n < 4 else CTX), n % 4
                    t = bank(n)
                    for c in range(NC):
                        if n == 0:
                            pe.wait_ge(xn_ready, b * NC + c + 1)
                        last = pe.transpose(t[:, c * P:(c + 1) * P], src[:, c, k * P:(k + 1) * P], idf)
                    last.then_inc(t_ready, 1)
                t = bank(8)
                taken(7)
                taken(6)
                for c in range(NC):
                    for k in range(2 * KD):
                        src = QT if k < KD else KT
                        last = pe.matmul(t[:, c * 32:(c + 1) * 32], src[:, k % KD, c * P:(c + 1) * P], WG[:, k, :],
                                         start=(k == 0), stop=(k == 2 * KD - 1))
                last.then_inc(t_ready, 1)
                for n in (9, 10):
                    t = bank(n)
                    taken(8)
                    for c in range(NC):
                        last = pe.transpose(t[0:96, c * P:(c + 1) * P], GS[:, c, n - 9, :], idf)
                    last.then_inc(t_ready, 1)
                t = bank(11)
                pe.wait_ge(uw_ready, b * 7 + 7)
                pe.sem_inc(passed[2], 1)
                for i in range(13):
                    last = pe.transpose(t[:, i * NH:(i + 1) * NH], UW[:, i, :], idf[0:NH, 0:NH])
                last.then_inc(t_ready, 1)
                pe.wait_ge(va_ready, b * 2 + 2)
                pe.wait_ge(ku_ready, b + 1)

                def scores(h):
                    g, j = divmod(h, HG)
                    r = slice(DH * j, DH * j + DH)
                    if h >= 2:
                        pe.wait_ge(c_ready, b * NH + h - 1)
                    for c in range(NC):
                        pe.matmul(QK[h % 2][:, c * P:(c + 1) * P], KT[r, g, c * P:(c + 1) * P],
                                  QT[r, g, c * P:(c + 1) * P], start=True, stop=True)
                    e = E[h % 2]
                    pick = PICK[0:96, h:h + 1]
                    pe.matmul(e[:, :], idb, FUT[:, :, :], start=True, stop=False)
                    pe.matmul(e[:, :], pick.to_broadcast([96, P]), NP[:, 1, :], start=False, stop=False)
                    for c in range(NC):
                        last = pe.matmul(e[:, c * P:(c + 1) * P], NP[:, 0, c * P:(c + 1) * P],
                                         pick.to_broadcast([96, P]), start=False, stop=(c == NC - 1))
                    last.then_inc(qe_ready, 1)

                def weigh(h):
                    pair, jj = divmod(h, 2)
                    if jj == 0 and pair >= 2:
                        pe.wait_ge(o_taken, b * (NH // 2) + pair - 1)
                    pe.wait_ge(c_ready, b * NH + h + 1)
                    o = O[pair % 2]
                    for c in range(NC):
                        at = (2 * c + jj) * VW
                        last = pe.matmul(o[:, at:at + VW], CC[:, h % 2, c * P:(c + 1) * P], VA[:, c, h, :],
                                         start=True, stop=True)
                    last.then_inc(pv_done, 1)

                def state(g):
                    t = bank(12 + 2 * g)
                    i = 0
                    for c in range(1, NC):
                        for u in range(c):
                            last = pe.matmul(t[:, (c - 1) * HG * VW:c * HG * VW], KU[:, i, g * P:(g + 1) * P],
                                             VA[:, u, g * HG:(g + 1) * HG, :], start=(u == 0), stop=(u == c - 1))
                            i += 1
                    last.then_inc(t_ready, 1)

                def read_state(g):
                    t = bank(13 + 2 * g)
                    taken(12 + 2 * g)
                    for c in range(1, NC):
                        last = pe.matmul(t[:, (c - 1) * HG * VW:c * HG * VW], QT[:, g, c * P:(c + 1) * P],
                                         SS[:, g % 2, c - 1, :], start=True, stop=True)
                    last.then_inc(t_ready, 1)

                state(0)
                pe.wait_ge(np_ready, b + 1)
                scores(0)
                for h in range(NH):
                    if h % HG == 0:
                        read_state(h // HG)
                    if h + 1 < NH:
                        scores(h + 1)
                    weigh(h)
                    if h % HG == 2 and h // HG + 1 < NH // HG:
                        state(h // HG + 1)

        @block.vector
        def _(v):
            v.wait_ge(w_loaded, 9 * 16)
            n_pre = [0]

            def pre(ins):
                n_pre[0] += 1
                ins.then_inc(pre_dve, 1)

            pre(v.memset(EPS[:, 0:1], 1e-5))
            pre(v.memset(EPS[:, 1:2], 1.0))
            pre(v.memset(EPS[:, 2:3], 1e-6))
            pre(v.memset(ONE[:, :], 1.0))
            for c in range(NC):
                pre(v.tensor_copy(FUT[:, c, :], CST[:, P:2 * P]))
            pre(v.tensor_copy(PICK[:, :], CST[:, 2 * P:2 * P + NH]))
            pre(v.tensor_tensor(WG[:, 4:8, :], WG[:, 4:8, :], WG[:, 8:12, :], ALU.add))
            pre(v.tensor_scalar(GLN[:, :], GLN[:, :], tg[:, 0:1], -1.0, ALU.mult, ALU.mult))
            assert n_pre[0] == PRE_DVE
            v.wait_ge(pre_dve, PRE_DVE)
            v.wait_ge(pre_pool, 3)
            own_mask = CST[:, 2 * P + NH:CST_W - 1]
            with v.Fori(0, B) as b:
                own = Tally(v, dve_own, b, DVE_OWN_A)
                for c in range(NC):
                    own.inc(v.bn_stats(ST[:, c, :], X[:, ds(b * NC + c, 1), :]))
                own.wait()
                v.sem_inc(passed[1], 1)
                for c in range(NC):
                    ins = v.bn_aggr(MV[:, c, :], ST[:, c, :])
                    if c < NC - 1:
                        own.inc(ins)
                ins.then_inc(mv_ready, 1)
                v.wait_ge(sd_ready, b + 1)
                own.inc(v.reciprocal(RS[:, :], SD[:, :]))
                own.wait()
                for c in range(NC):
                    v.tensor_scalar(XN[:, c, :], X[:, ds(b * NC + c, 1), :], MV[:, c, 0:1], RS[:, c:c + 1],
                                    ALU.subtract, ALU.mult).then_inc(xn_ready, 1)
                for n in range(1, 8, 2):
                    v.wait_ge(t_ready, b * NT + n + 1)
                    dst = (QT if n < 4 else KT)[:, n % 4, :]
                    v.tensor_copy(dst, T[1][:, :]).then_inc(t_taken[1], 1)
                v.wait_ge(t_ready, b * NT + 9)
                gates = T[0][:, 0:P].rearrange("p (c q h) -> p (c q) h", c=NC, q=2)
                gs = GS[:, :, :, :].rearrange("p c q r -> p (c q) r")
                for r in range(3):
                    ins = v.tensor_copy(gs[:, :, 32 * r:32 * r + NH], gates)
                    if r < 2:
                        own.inc(ins)
                ins.then_inc(t_taken[0], 1)
                v.wait_ge(t_ready, b * NT + 10)
                v.tensor_scalar(ZI, T[1][0:96, :], BIAS[:, 0:1], None, ALU.add).then_inc(t_taken[1], 1)
                v.wait_ge(t_ready, b * NT + 11)
                v.tensor_scalar(ZF, T[0][0:96, :], BIAS[:, 1:2], None, ALU.add).then_inc(t_taken[0], 1)
                v.wait_ge(t_taken[0], b * (NT // 2) + 6)
                v.scalar_tensor_tensor(out=AZ, in0=ZF, scalar=-1.0, in1=ZF, op0=ALU.mult, op1=ALU.max).then_inc(az_ready, 1)
                own.inc(v.tensor_scalar(MZ, ZF, 0.0, None, ALU.min))
                own.wait()
                v.wait_ge(el_ready, b + 1)
                own.inc(v.tensor_tensor(LF, MZ, EL, ALU.subtract))
                own.wait()
                own.inc(v.tensor_tensor_scan(FC, ONE[:, :], LF, 0.0, ALU.mult, ALU.add))
                own.wait()
                v.tensor_tensor(VV[:, 0, :], ZI, FC, ALU.subtract).then_inc(vv_ready, 1)
                v.wait_ge(vv_ready, b * 3 + 1)
                own.inc(v.tensor_tensor_scan(MZ, ONE[:, :], VV[:, 0, :], -3.0e38, ALU.mult, ALU.max))
                own.wait()
                own.inc(v.tensor_tensor(EL, FC, MZ, ALU.add))
                for c in range(1, NC):
                    own.inc(v.tensor_copy(FM[:, c:c + 1], MZ[:, c * P - 1:c * P]))
                own.wait()
                v.tensor_scalar(VV[:, 1, :], MZ, -1.0, None, ALU.mult).then_inc(vv_ready, 2)
                v.wait_ge(np1_ready, b + 1)
                v.tensor_tensor(RR[:, :, :], VV[:, :, :], NP[:, :, :], ALU.subtract).then_inc(rr_ready, 1)
                v.wait_ge(t2_ready, b + 1)
                v.tensor_tensor(RR[64:96, :, :], RR[64:96, :, :], T2[64:96, :, :], ALU.subtract).then_inc(r3_ready, 1)
                v.wait_ge(t_ready, b * NT + 12)
                v.tensor_copy(TM[:, :, :], T[1][:, 0:13 * NH].rearrange("p (i h) -> p i h", h=NH)).then_inc(t_taken[1], 1)
                v.wait_ge(t_taken[1], b * (NT // 2) + 6)
                v.wait_ge(ctx_loaded, b * 16 + 16)
                i = 0
                for c in range(1, NC):
                    for t in range(c):
                        ins = v.tensor_tensor(
                            KU[:, i, :].rearrange("p (h d) -> p h d", h=NH),
                            CTX[:, t, :].rearrange("p (h d) -> p h d", h=NH),
                            TM[:, i, :].unsqueeze(2).to_broadcast([P, NH, DH]), ALU.mult)
                        i += 1
                        if i < 6:
                            own.inc(ins)
                ins.then_inc(ku_ready, 1)

                def take_state(g):
                    v.wait_ge(t_ready, b * NT + 13 + 2 * g)
                    v.tensor_tensor(SS[:, g % 2, :, :], T[0][:, 0:(NC - 1) * HG * VW].rearrange("p (c f) -> p c f", c=NC - 1),
                                    own_mask.unsqueeze(1).to_broadcast([P, NC - 1, HG * VW]),
                                    ALU.mult).then_inc(t_taken[0], 1)

                def take_read(g):
                    v.wait_ge(t_ready, b * NT + 14 + 2 * g)
                    for c in range(1, NC):
                        ins = v.tensor_tensor(
                            OUT[:, c, g * HG:(g + 1) * HG, :],
                            T[1][:, (c - 1) * HG * VW:c * HG * VW].rearrange("p (h f) -> p h f", h=HG),
                            TM[:, 5 + c, g * HG:(g + 1) * HG].unsqueeze(2).to_broadcast([P, HG, VW]), ALU.mult)
                        if c < NC - 1:
                            own.inc(ins)
                    ins.then_inc(t_taken[1], 1)
                    v.wait_ge(t_taken[1], b * (NT // 2) + 7 + g)

                def take_pair(pair):
                    v.wait_ge(pv_done, b * NH + 2 * pair + 2)
                    o = OUT[:, :, 2 * pair:2 * pair + 2, :]
                    v.tensor_tensor(o, o, O[pair % 2][:, 0:2 * NC * VW].rearrange("p (c j f) -> p c j f", c=NC, j=2),
                                    ALU.add).then_inc(o_taken, 1)

                v.wait_ge(va_ready, b * 2 + 2)
                for h in range(NH):
                    if h % HG == 0:
                        take_state(h // HG)
                    v.wait_ge(d_ready, b * NH + h + 1)
                    if h >= 2:
                        v.wait_ge(pv_done, b * NH + h - 1)
                    v.scalar_tensor_tensor(out=CC[:, h % 2, :], in0=QK[h % 2][:, :], scalar=DH ** -0.5,
                                           in1=DD[:, h % 2, :], op0=ALU.mult, op1=ALU.mult).then_inc(c_ready, 1)
                    if h % HG == 0:
                        take_read(h // HG)
                    if h % 2 == 1 and h >= 3:
                        take_pair(h // 2 - 1)
                take_pair(NH // 2 - 1)
                v.wait_ge(o_taken, (b + 1) * (NH // 2))
                sums = OUT[:, :, :, DH].rearrange("p c h -> p (c h)")
                own.inc(v.scalar_tensor_tensor(out=DN[:, :], in0=sums, scalar=-1.0, in1=sums, op0=ALU.mult, op1=ALU.max))
                own.wait()
                own.inc(v.tensor_tensor(DN[:, :], DN[:, :], TM[:, 9:13, :].rearrange("p c h -> p (c h)"), ALU.max))
                own.wait()
                own.inc(v.tensor_scalar(DN[:, :], DN[:, :], 1e-6, None, ALU.add))
                own.wait()
                own.inc(v.reciprocal(DN[:, :], DN[:, :]))
                own.wait()
                bc = lambda x: x.unsqueeze(2).to_broadcast([P, NC * NH, DH])
                own.inc(v.tensor_tensor(HN[:, :, :], OUT[:, :, :, 0:DH].rearrange("p c h d -> p (c h) d"), bc(DN[:, :]), ALU.mult))
                own.wait()
                own.inc(v.tensor_reduce(MU[:, :], HN[:, :, :], AX.X, ALU.add))
                own.wait()
                v.scalar_tensor_tensor(out=HN[:, :, :], in0=bc(MU[:, :]), scalar=1.0 / DH, in1=HN[:, :, :],
                                       op0=ALU.mult, op1=ALU.subtract).then_inc(hc_ready, 1)
                v.wait_ge(sq_ready, b + 1)
                v.tensor_reduce(VR[:, :], SQ[:, :, :], AX.X, ALU.add).then_inc(vr_ready, 1)
                v.wait_ge(sv_ready, b + 1)
                own.inc(v.reciprocal(VR[:, :], VR[:, :]))
                own.wait()
                own.inc(v.tensor_tensor(HN[:, :, :], HN[:, :, :], bc(VR[:, :]), ALU.mult))
                own.wait()
                hn = HN[:, :, :].rearrange("p (c h) d -> p c (h d)", c=NC)
                own.inc(v.tensor_tensor(hn, hn, GLN[:, :].unsqueeze(1).to_broadcast([P, NC, D]), ALU.mult))
                own.wait()
                x = X[:, ds(b * NC, NC), :]
                own.inc(v.tensor_tensor(x, x, hn, ALU.add))
                own.wait()
                own.done()


N_FLAT = D * INTER
N_CTRL = int(D * INTER / 128.9)
RUNS = N_FLAT // P
RC = RUNS // P
QW = 2048
SUB = 512
PARTS = ((0, 0), (0, 1), (0, 2), (1, 0), (1, 1), (2, 0))


def run_orders():
    pos = np.arange(RUNS)
    gate = KD * (pos % INTER) + pos // INTER
    down = KI * (pos % D) + pos // D
    return gate, down


def spline_grid():
    t = np.linspace(0.0, N_CTRL - 1.0, N_FLAT, dtype=np.float64)
    i = np.clip(np.floor(t).astype(np.int64), 0, N_CTRL - 2)
    return t, i


def bf16_round(a):
    u = np.ascontiguousarray(a, dtype=np.float32).view(np.uint32).astype(np.uint64)
    u = (u + 0x7FFF + ((u >> 16) & 1)) & 0xFFFF0000
    return u.astype(np.uint32).view(np.float32)


def spline_constants():
    t, i = spline_grid()
    first = np.arange(RUNS) * P
    phase = t[first] - i[first]
    step = (N_CTRL - 1.0) / (N_FLAT - 1.0)
    basis = 0.5 * np.array([[0, 2, 0, 0], [-1, 0, 1, 0], [2, -5, 4, -1], [-1, 3, -3, 1]], np.float64)
    binom = [[1, 0, 0, 0], [1, 1, 0, 0], [1, 2, 1, 0], [1, 3, 3, 1]]
    coef = np.zeros((2, 4, 4, RUNS))
    for piece in range(2):
        u = phase - piece
        for m in range(4):
            for k in range(4):
                coef[piece, m, k] = sum(binom[l][m] * u ** (l - m) * basis[l, k] for l in range(m, 4))
    starts = (i.reshape(RUNS, P) == i[first][:, None]).sum(1).astype(np.float32)
    orders = run_orders()
    coefs = np.stack([coef[..., o] for o in orders]).reshape(2, 2, 4, 4, P, RC)
    coefs = np.ascontiguousarray(coefs.transpose(4, 0, 1, 2, 3, 5)).astype(np.float32).reshape(P, -1)
    starts = np.stack([starts[orders[0]], starts[orders[0]], starts[orders[1]]])
    power = np.stack([(np.arange(P) * step) ** m for m in range(4)])
    parts, rest = [], power
    for _ in range(3):
        parts.append(bf16_round(rest))
        rest = rest - parts[-1]
    powers = np.concatenate([parts[q] for _, q in PARTS]).astype(np.float32)
    return {"spline_coefs": coefs, "spline_starts": starts, "spline_powers": powers}


def windows(cp):
    _, i = spline_grid()
    base = i[np.arange(RUNS) * P]
    out = []
    for t, a in enumerate(cp):
        order = run_orders()[t // 2]
        at = np.clip(base[order][None, :] - 1 + np.arange(5)[:, None], 0, N_CTRL - 1)
        out.append(np.asarray(a)[at].reshape(5, P, RC).transpose(1, 0, 2))
    return np.ascontiguousarray(np.stack(out, axis=1))


def spline_phase(nc, A, at_row, WH, WL, SCL, stack):
    def sb(name, shape, dt=F32):
        return stack.enter_context(nc.sbuf_tensor(name, shape, dt))

    sem = nc.alloc_semaphore
    WIN = sb("WIN", [P, 3, 5, RC])
    COEF = sb("COEF", [P, 2, 2, 4, 4 * RC])
    TMP = sb("TMP", [P, 4, 4, RC])
    CF = sb("CF", [P, 6, 4, RC])
    PB = sb("PB", [P, 3, 6, 4, RC], BF16)
    PW = sb("PW", [24, P])
    PWB = sb("PWB", [24, P], BF16)
    MX = sb("MX", [P, 3])
    MXA = sb("MXA", [P, 3])
    SC = sb("SC", [P, 3])
    RH = sb("RH", [24, 2, 2, QW], BF16)
    START = COEF[:, :, :, :, :].rearrange("p o q m f -> p o (q m f)")
    MK = sb("MK", [P, 2, QW], U8)
    WF = sb("WF", [P, 4, SUB])
    PS = [stack.enter_context(nc.psum_tensor(f"SP{i}", [P, SUB], F32)) for i in range(8)]
    scratch = nc.dram_tensor("spline_scratch", [3, 6, 4, RUNS], BF16).ap()
    loaded, mx_ready, all_max, pw_ready, parts_ready, parts_stored, own_sem = (
        sem("b_" + n) for n in ("loaded", "mx", "all_max", "pw", "parts", "parts_stored", "own"))
    rh_loaded = [sem("b_rh0"), sem("b_rh1")]
    pp_ready, wf_copied, wf_selected, wh_ready, wl_ready = (
        sem("b_" + n) for n in ("pp", "wf_copied", "wf_selected", "wh", "wl"))
    passed, mk_ready = sem("b_passed"), sem("b_mk")
    NS = RUNS // SUB
    SEL0 = 8

    with nc.Block() as block:
        @block.sync
        def _(sp):
            sp.dma_start(WIN[:, :, :, :], A["spline_windows"]).then_inc(loaded, 16)
            sp.dma_start(COEF[:, :, :, :, :], A["spline_coefs"].rearrange("p (o q m f) -> p o q m f", o=2, q=2, m=4)).then_inc(loaded, 16)
            sp.dma_start(PW[:, :], A["spline_powers"]).then_inc(loaded, 16)
            sp.wait_ge(parts_ready, 3)
            for part in range(3):
                sp.dma_start(scratch[part].rearrange("a m (p c) -> p (a m) c", p=P),
                             PB[:, part, :, :, :].rearrange("p a m c -> p (a m) c")).then_inc(parts_stored, 16)
            sp.wait_ge(parts_stored, 48)
            with sp.Fori(0, 3) as t:
                for q in range(RUNS // QW):
                    cols = slice(q * QW, (q + 1) * QW)
                    sp.wait_ge(wf_selected, t * NS + 4 * q + SEL0 - 4)
                    for n, (part, _) in enumerate(PARTS):
                        sp.dma_start(RH[4 * n:4 * n + 4, q % 2, :, :],
                                     scratch[part, ds(2 * t, 2), :, cols].rearrange("a m c -> m a c")).then_inc(rh_loaded[q % 2], 16)
                    sp.dma_start(START[:, q % 2, :], A["spline_starts"][ds(t, 1), cols].to_broadcast([P, QW])).then_inc(rh_loaded[q % 2], 16)

        @block.gpsimd
        def _(pool):
            pool.wait_ge(mx_ready, 1)
            pool.partition_all_reduce(MXA[:, :], MX[:, :], P, RMAX).then_inc(all_max, 1)

        @block.scalar
        def _(act):
            with act.Fori(0, 3) as t:
                def high(n):
                    act.wait_ge(wf_selected, t * NS + n + 1 + SEL0)
                    nc.scalar.copy(WH[:, ds(t, 1), n * SUB:(n + 1) * SUB], WF[:, n % 4, :]).then_inc(wh_ready, 1)

                for n in range(NS):
                    act.wait_ge(pp_ready, t * NS + n + 1)
                    act.wait_ge(wl_ready, t * NS + n + 1)
                    nc.scalar.copy(WF[:, n % 4, :], PS[2 * (n % 4)][:, :]).then_inc(wf_copied, 1)
                    if n:
                        high(n - 1)
                high(NS - 1)

        @block.tensor
        def _(pe):
            pe.wait_ge(pw_ready, 1)
            with pe.Fori(0, 3) as t:
                for n in range(NS):
                    q = n // 4
                    if n % 4 == 0:
                        pe.wait_ge(rh_loaded[q % 2], t * (2 * 7 * 16) + (q // 2 + 1) * 7 * 16)
                    pe.wait_ge(wf_selected, t * NS + n - 3 + SEL0)
                    for piece in range(2):
                        last = pe.matmul(PS[2 * (n % 4) + piece][:, :], PWB[:, :],
                                         RH[:, q % 2, piece, (n % 4) * SUB:(n % 4 + 1) * SUB], start=True, stop=True)
                    last.then_inc(pp_ready, 1)

        @block.vector
        def _(v):
            own = Tally(v, own_sem, 0, 0)

            def step(ins):
                own.n += 1
                ins.then_inc(own_sem, 1)
                v.wait_ge(own_sem, own.n)

            v.wait_ge(loaded, 48)
            v.tensor_copy(PWB[:, :], PW[:, :]).then_inc(pw_ready, 1)
            v.tensor_reduce(MX[:, :], WIN[:, :, :, :].rearrange("p t k c -> p t (k c)"), AX.X, ALU.max,
                            apply_absolute_value=True).then_inc(mx_ready, 1)
            for tp in range(6):
                t, piece = divmod(tp, 2)
                step(v.tensor_tensor(TMP[:, :, :, :].rearrange("p m k c -> p m (k c)"),
                                     WIN[:, t, piece:piece + 4, :].rearrange("p k c -> p (k c)").unsqueeze(1).to_broadcast([P, 4, 4 * RC]),
                                     COEF[:, t // 2, piece, :, :], ALU.mult))
                step(v.tensor_reduce(CF[:, tp, :, :], TMP[:, :, :, :].rearrange("p m k c -> p m c k"), AX.X, ALU.add))
            v.wait_ge(all_max, 1)
            step(v.tensor_scalar(MXA[:, :], MXA[:, :], 1e-30, None, ALU.max))
            step(v.tensor_scalar(SCL[:, :].bitcast(U32), MXA[:, :].bitcast(U32), 0x7F800000, None, ALU.bitwise_and))
            step(v.reciprocal(SC[:, :], SCL[:, :]))
            step(v.tensor_scalar(SC[:, :], SC[:, :], 8192.0, None, ALU.mult))
            for t in range(3):
                c = CF[:, 2 * t:2 * t + 2, :, :]
                step(v.tensor_scalar(c, c, SC[:, t:t + 1], None, ALU.mult))
            v.tensor_copy(PB[:, 0, :, :, :], CF[:, :, :, :]).then_inc(parts_ready, 1)
            v.wait_ge(parts_ready, 1)
            step(v.tensor_tensor(CF[:, :, :, :], CF[:, :, :, :], PB[:, 0, :, :, :], ALU.subtract))
            v.tensor_copy(PB[:, 1, :, :, :], CF[:, :, :, :]).then_inc(parts_ready, 1)
            v.wait_ge(parts_ready, 2)
            step(v.tensor_tensor(CF[:, :, :, :], CF[:, :, :, :], PB[:, 1, :, :, :], ALU.subtract))
            v.tensor_copy(PB[:, 2, :, :, :], CF[:, :, :, :]).then_inc(parts_ready, 1)
            v.sem_inc(wf_selected, SEL0)
            v.sem_inc(wl_ready, 4)
            with v.Fori(0, 3) as t:
                def low(n):
                    v.wait_ge(wh_ready, t * NS + n + 1)
                    v.tensor_tensor(WL[:, ds(t, 1), n * SUB:(n + 1) * SUB], WF[:, n % 4, :],
                                    WH[:, ds(t, 1), n * SUB:(n + 1) * SUB], ALU.subtract).then_inc(wl_ready, 1)

                for n in range(NS):
                    q = n // 4
                    if n % 4 == 0:
                        v.wait_ge(rh_loaded[q % 2], t * (2 * 7 * 16) + (q // 2 + 1) * 7 * 16)
                        v.tensor_scalar(MK[:, q % 2, :], START[:, q % 2, :], at_row, None, ALU.is_le).then_inc(mk_ready, 1)
                        v.wait_ge(mk_ready, t * 4 + q + 1)
                        v.sem_inc(passed, 1)
                    v.wait_ge(wf_copied, t * NS + n + 1)
                    v.sem_inc(passed, 1)
                    v.copy_predicated(WF[:, n % 4, :], MK[:, q % 2, (n % 4) * SUB:(n % 4 + 1) * SUB],
                                      PS[2 * (n % 4) + 1][:, :]).then_inc(wf_selected, 1)
                    if n:
                        low(n - 1)
                low(NS - 1)


XS = 1024.0


def ffn0_phase(nc, A, X, tg, idf, WH, WL, SCL, stack):
    def sb(name, shape, dt=F32):
        return stack.enter_context(nc.sbuf_tensor(name, shape, dt))

    sem = nc.alloc_semaphore
    XN = sb("XN0", [P, NC, D])
    XH = sb("XH0", [P, KD, S], F16)
    XL = sb("XL0", [P, KD, S], F16)
    HH = sb("HH0", [P, KI, S], F16)
    HL = sb("HL0", [P, KI, S], F16)
    SG = sb("SG0", [P, 2, S])
    HM = sb("HM0", [P, 2, S])
    ST = sb("ST0", [P, NC, 6])
    MV = sb("MV0", [P, NC, 2])
    SD = sb("SD0", [P, NC])
    RS = sb("RS0", [P, NC])
    EPS = sb("EPS0", [P, 1])
    DS = sb("DS0", [P, 4])
    T, G, U, DN = ([stack.enter_context(nc.psum_tensor(f"F{n}{i}", [P, 512], F32)) for i in range(2)] for n in "TGUD")
    (mv_ready, sd_ready, xn_ready, t_ready, xh_ready, xl_ready, gu_ready, sg_ready, hm_ready, hh_ready, hl_ready,
     dn_ready, x_added, ds_ready, own_sem) = (sem("c_" + n) for n in (
         "mv", "sd", "xn", "t", "xh", "xl", "gu", "sg", "hm", "hh", "hl", "dn", "x_added", "ds", "own"))
    passed, pe_passed = sem("c_passed"), sem("c_pe_passed")

    with nc.Block() as block:
        @block.scalar
        def _(act):
            def norm(b):
                act.wait_ge(mv_ready, b + 1)
                nc.scalar.activation(SD[:, :], MV[:, :, 1], ACT.Sqrt, bias=EPS[:, 0:1]).then_inc(sd_ready, 1)

            def high(b):
                for k in range(KD):
                    act.wait_ge(t_ready, b * KD + k + 1)
                    nc.scalar.activation(XH[:, k, :], T[k % 2][:, :], ACT.Copy, scale=XS).then_inc(xh_ready, 1)

            def batch(b, more):
                with act.Fori(0, KI // 2) as u:
                    for w in range(2):
                        act.wait_ge(gu_ready, b * KI + 2 * u + w + 1)
                        act.wait_ge(hm_ready, b * KI + 2 * u + w + 1)
                        nc.scalar.activation(SG[:, w, :], G[w][:, :], ACT.Silu, scale=DS[:, 0:1]).then_inc(sg_ready, 1)
                    for w in range(2):
                        act.wait_ge(hm_ready, b * KI + 2 * u + w + 3)
                        nc.scalar.copy(HH[:, ds(2 * u + w, 1), :], HM[:, w, :]).then_inc(hh_ready, 1)
                if more:
                    norm(b + 1)
                    high(b + 1)

            act.wait_ge(ds_ready, 6)
            norm(0)
            high(0)
            with act.Fori(0, B - 1) as b:
                batch(b, True)
            batch(B - 1, False)

        @block.tensor
        def _(pe):
            def transposes(b):
                for k in range(KD):
                    pe.wait_ge(xl_ready, b * KD + k + 1)
                    if k == 0:
                        pe.wait_ge(xn_ready, b * NC + NC)
                    for c in range(NC):
                        last = pe.transpose(T[k % 2][:, c * P:(c + 1) * P], XN[:, c, k * P:(k + 1) * P], idf)
                    last.then_inc(t_ready, 1)

            def down(b, u):
                for w in range(2):
                    pe.wait_ge(x_added, b * NC + 2 * u + w + 1)
                    c = 2 * u + w
                    n = 0
                    for i in range(KI):
                        for lhs, rhs in ((HH, WH), (HH, WL), (HL, WH)):
                            n += 1
                            last = pe.matmul(DN[w][:, :], lhs[:, i, c * P:(c + 1) * P], rhs[:, 2, i * D:(i + 1) * D],
                                             start=(n == 1), stop=(n == 3 * KI))
                    last.then_inc(dn_ready, 1)

            def batch(b, more):
                pe.wait_ge(xl_ready, b * KD + KD + 2)
                pe.sem_inc(pe_passed, 1)
                with pe.Fori(0, KI // 2) as u:
                    for w in range(2):
                        pe.wait_ge(hm_ready, b * KI + 2 * u + w + 1)
                        for t, bank in ((0, G[w]), (1, U[w])):
                            n = 0
                            for k in range(KD):
                                cols = ds(u * (2 * P) + (k * INTER + w * P), P)
                                for lhs, rhs in ((WH, XH), (WH, XL), (WL, XH)):
                                    n += 1
                                    last = pe.matmul(bank[:, :], lhs[:, t, cols], rhs[:, k, :],
                                                     start=(n == 1), stop=(n == 3 * KD))
                        last.then_inc(gu_ready, 1)
                pe.wait_ge(hl_ready, b * KI + KI + 2)
                pe.sem_inc(pe_passed, 1)
                down(b, 0)
                if more:
                    transposes(b + 1)
                down(b, 1)

            transposes(0)
            with pe.Fori(0, B - 1) as b:
                batch(b, True)
            batch(B - 1, False)

        @block.vector
        def _(v):
            n_own = [0]

            def step(ins):
                n_own[0] += 1
                ins.then_inc(ds_ready, 1)
                v.wait_ge(ds_ready, n_own[0])

            step(v.memset(EPS[:, :], 1e-5))
            step(v.tensor_scalar(DS[:, 0:1], SCL[:, 0:1], 2.0 ** -23, None, ALU.mult))
            step(v.reciprocal(DS[:, 1:2], SCL[:, 0:1]))
            step(v.tensor_scalar(DS[:, 1:2], DS[:, 1:2], 2.0 ** -29, None, ALU.mult))
            step(v.tensor_scalar(DS[:, 2:3], SCL[:, 0:1], SCL[:, 1:2], SCL[:, 2:3], ALU.mult, ALU.mult))
            step(v.tensor_scalar(DS[:, 2:3], DS[:, 2:3], tg[:, 2:3], 2.0 ** -7, ALU.mult, ALU.mult))
            v.sem_inc(xl_ready, 2)
            v.sem_inc(hm_ready, 2)
            v.sem_inc(hl_ready, 2)
            v.sem_inc(x_added, 2)

            def norm(b):
                for c in range(NC):
                    v.bn_stats(ST[:, c, :], X[:, ds(b * NC + c, 1), :]).then_inc(own_sem, 1)
                v.wait_ge(own_sem, b * (2 * NC) + NC)
                v.sem_inc(passed, 1)
                for c in range(NC):
                    v.bn_aggr(MV[:, c, :], ST[:, c, :]).then_inc(*((own_sem, 1) if c < NC - 1 else (mv_ready, 1)))
                v.wait_ge(sd_ready, b + 1)
                v.reciprocal(RS[:, :], SD[:, :]).then_inc(own_sem, 1)
                v.wait_ge(own_sem, b * (2 * NC) + 2 * NC)
                for c in range(NC):
                    v.tensor_scalar(XN[:, c, :], X[:, ds(b * NC + c, 1), :], MV[:, c, 0:1], RS[:, c:c + 1],
                                    ALU.subtract, ALU.mult).then_inc(xn_ready, 1)

            def low(b):
                for k in range(KD):
                    v.wait_ge(xh_ready, b * KD + k + 1)
                    v.scalar_tensor_tensor(out=XL[:, k, :], in0=T[k % 2][:, :], scalar=XS, in1=XH[:, k, :],
                                           op0=ALU.mult, op1=ALU.subtract).then_inc(xl_ready, 1)

            def add(b, u):
                for w in range(2):
                    c = 2 * u + w
                    v.wait_ge(dn_ready, b * NC + c + 1)
                    x = X[:, ds(b * NC + c, 1), :]
                    v.scalar_tensor_tensor(out=x, in0=DN[w][:, :], scalar=DS[:, 2:3], in1=x,
                                           op0=ALU.mult, op1=ALU.add).then_inc(x_added, 1)

            def batch(b, more):
                with v.Fori(0, KI // 2) as u:
                    for w in range(2):
                        v.wait_ge(sg_ready, b * KI + 2 * u + w + 1)
                        v.wait_ge(hl_ready, b * KI + 2 * u + w + 1)
                        v.scalar_tensor_tensor(out=HM[:, w, :], in0=U[w][:, :], scalar=DS[:, 1:2], in1=SG[:, w, :],
                                               op0=ALU.mult, op1=ALU.mult).then_inc(hm_ready, 1)
                    for w in range(2):
                        v.wait_ge(hh_ready, b * KI + 2 * u + w + 1)
                        v.tensor_tensor(HL[:, ds(2 * u + w, 1), :], HM[:, w, :], HH[:, ds(2 * u + w, 1), :],
                                        ALU.subtract).then_inc(hl_ready, 1)
                if more:
                    norm(b + 1)
                add(b, 0)
                if more:
                    low(b + 1)
                add(b, 1)

            norm(0)
            low(0)
            with v.Fori(0, B - 1) as b:
                batch(b, True)
            batch(B - 1, False)


AH, AC = 8, 64
UNITS = AH * NC


def attention_phase(nc, A, X, tg, idf, stack):
    def sb(name, shape, dt=F32):
        return stack.enter_context(nc.sbuf_tensor(name, shape, dt))

    sem = nc.alloc_semaphore
    XN = sb("XN2", [P, NC, S])
    CTX = sb("CTX2", [P, NC, S])
    VT = sb("VT2", [P, NC, D])
    PR = sb("PR2", [P, 2, S])
    PT = sb("PT2", [P, 2, S])
    OT = sb("OT2", [P, NC, D])
    NM = sb("NM2", [P, UNITS])
    SM = sb("SM2", [P, UNITS])
    RC_ = sb("RC2", [P, UNITS])
    ST = sb("ST2", [P, NC, 6])
    MV = sb("MV2", [P, NC, 2])
    SD = sb("SD2", [P, NC])
    RS = sb("RS2", [P, NC])
    EPS = sb("EPS2", [P, 1])
    SB = [stack.enter_context(nc.psum_tensor(f"A_S{i}", [P, 512], F32)) for i in range(3)]
    PB = [stack.enter_context(nc.psum_tensor(f"A_P{i}", [P, 512], F32)) for i in range(2)]
    OB = [stack.enter_context(nc.psum_tensor(f"A_O{i}", [P, 512], F32)) for i in range(2)]
    TB = stack.enter_context(nc.psum_tensor("A_T", [P, 512], F32))
    (ctx_loaded, mv_ready, sd_ready, xn_ready, t_ready, t_taken, s_ready, max_ready, p_ready, pt_ready, o_ready,
     ot_ready, own_sem, passed, pe_passed, eps_ready) = (sem("d_" + n) for n in (
         "ctx", "mv", "sd", "xn", "t", "t_taken", "s", "max", "p", "pt", "o", "ot", "own", "passed", "pe_passed", "eps"))
    pt_taken = [sem("d_pt_taken0"), sem("d_pt_taken1")]
    NT = 2 * NC
    OWN = 2 * NC + 1 + UNITS
    ctx = A["ctx_2048"].rearrange("b (c p) d -> b p c d", p=P)

    with nc.Block() as block:
        @block.sync
        def _(sp):
            sp.dma_start(CTX[:, :, :], ctx[0]).then_inc(ctx_loaded, 16)
            with sp.Fori(1, B) as b:
                sp.wait_ge(s_ready, b * UNITS)
                sp.sem_inc(passed, 1)
                sp.dma_start(CTX[:, :, :], ctx[ds(b, 1)].rearrange("a p c d -> p (a c) d")).then_inc(ctx_loaded, 16)

        @block.scalar
        def _(act):
            act.wait_ge(eps_ready, 1)
            with act.Fori(0, B) as b:
                act.wait_ge(mv_ready, b + 1)
                nc.scalar.activation(SD[:, :], MV[:, :, 1], ACT.Sqrt, bias=EPS[:, 0:1]).then_inc(sd_ready, 1)

                def take(u):
                    act.wait_ge(pt_ready, b * UNITS + u + 1)
                    nc.scalar.copy(PT[:, 0, :], PB[0][:, :]).then_inc(pt_taken[0], 1)

                for u in range(UNITS):
                    act.wait_ge(max_ready, b * UNITS + u + 1)
                    if u >= 2:
                        act.wait_ge(pt_ready, b * UNITS + u - 1)
                    nc.scalar.activation(PR[:, u % 2, :], SB[u % 3][:, :], ACT.Exp, bias=NM[:, u:u + 1],
                                         accum_out=SM[:, u:u + 1]).then_inc(p_ready, 1)
                    if u >= 1 and (u - 1) % 2 == 0:
                        take(u - 1)

        @block.tensor
        def _(pe):
            with pe.Fori(0, B) as b:
                def scores(u):
                    h, q = divmod(u, NC)
                    c, r = h // 2, slice(AC * (h % 2), AC * (h % 2) + AC)
                    if u >= 3:
                        pe.wait_ge(p_ready, b * UNITS + u - 2)
                    pe.matmul(SB[u % 3][:, :], XN[r, c, q * P:(q + 1) * P], CTX[r, c, :],
                              start=True, stop=True).then_inc(s_ready, 1)

                def turn(u):
                    pe.wait_ge(p_ready, b * UNITS + u + 1)
                    if u >= 2:
                        pe.wait_ge(pt_taken[u % 2], b * (UNITS // 2) + u // 2)
                    for k in range(NC):
                        last = pe.transpose(PB[u % 2][:, k * P:(k + 1) * P], PR[:, u % 2, k * P:(k + 1) * P], idf)
                    last.then_inc(pt_ready, 1)

                def weigh(u):
                    h = u // NC
                    pe.wait_ge(pt_taken[u % 2], b * (UNITS // 2) + u // 2 + 1)
                    if u >= 2:
                        pe.wait_ge(ot_ready, b * UNITS + u - 1)
                    for k in range(NC):
                        last = pe.matmul(OB[u % 2][:, 0:AC], PT[:, u % 2, k * P:(k + 1) * P],
                                         VT[:, k, h * AC:(h + 1) * AC], start=(k == 0), stop=(k == NC - 1))
                    last.then_inc(o_ready, 1)

                def back(c):
                    pe.wait_ge(ot_ready, b * UNITS + (c + 1) * 2 * NC)
                    pe.wait_ge(t_taken, b * NT + NC + c + 1)
                    for k in range(NC):
                        last = pe.transpose(TB[:, k * P:(k + 1) * P], OT[:, k, c * P:(c + 1) * P], idf)
                    last.then_inc(t_ready, 1)

                pe.wait_ge(ctx_loaded, b * 16 + 16)
                for k in range(NC):
                    pe.wait_ge(t_taken, b * NT + k + 1)
                    for c in range(NC):
                        last = pe.transpose(TB[:, c * P:(c + 1) * P], CTX[:, c, k * P:(k + 1) * P], idf)
                    last.then_inc(t_ready, 1)
                pe.wait_ge(xn_ready, b * NC + NC)
                pe.sem_inc(pe_passed, 1)
                scores(0)
                scores(1)
                for u in range(UNITS + 4):
                    if u + 2 < UNITS:
                        scores(u + 2)
                    if u < UNITS:
                        turn(u)
                    if 1 <= u <= UNITS:
                        weigh(u - 1)
                    if u >= 2 * NC + 2 and (u - 2) % (2 * NC) == 0:
                        back((u - 2) // (2 * NC) - 1)

        @block.vector
        def _(v):
            v.memset(EPS[:, :], 1e-5).then_inc(eps_ready, 1)
            v.sem_inc(t_taken, 1)
            with v.Fori(0, B) as b:
                own = Tally(v, own_sem, b, OWN)
                for c in range(NC):
                    own.inc(v.bn_stats(ST[:, c, :], X[:, ds(b * NC + c, 1), :]))
                own.wait()
                v.sem_inc(passed, 1)
                for c in range(NC):
                    ins = v.bn_aggr(MV[:, c, :], ST[:, c, :])
                    if c < NC - 1:
                        own.inc(ins)
                ins.then_inc(mv_ready, 1)
                for k in range(NC):
                    v.wait_ge(t_ready, b * NT + k + 1)
                    v.tensor_copy(VT[:, k, :], TB[:, :]).then_inc(t_taken, 1)
                v.wait_ge(sd_ready, b + 1)
                own.inc(v.reciprocal(RS[:, :], SD[:, :]))
                own.wait()
                own.inc(v.tensor_scalar(RS[:, :], RS[:, :], 1.0 / AC, None, ALU.mult))
                own.wait()
                for c in range(NC):
                    v.tensor_scalar(XN[:, c, :], X[:, ds(b * NC + c, 1), :], MV[:, c, 0:1], RS[:, c:c + 1],
                                    ALU.subtract, ALU.mult).then_inc(xn_ready, 1)

                def top(u):
                    v.wait_ge(s_ready, b * UNITS + u + 1)
                    v.tensor_reduce(NM[:, u:u + 1], SB[u % 3][:, :], AX.X, ALU.max, negate=True).then_inc(max_ready, 1)

                def take(u):
                    v.wait_ge(pt_ready, b * UNITS + u + 1)
                    v.tensor_copy(PT[:, 1, :], PB[1][:, :]).then_inc(pt_taken[1], 1)

                def scale(u):
                    h, q = divmod(u, NC)
                    v.wait_ge(p_ready, b * UNITS + u + 1)
                    own.inc(v.reciprocal(RC_[:, u:u + 1], SM[:, u:u + 1]))
                    own.wait()
                    v.wait_ge(o_ready, b * UNITS + u + 1)
                    v.tensor_scalar(OT[:, q, h * AC:(h + 1) * AC], OB[u % 2][:, 0:AC], RC_[:, u:u + 1], None,
                                    ALU.mult).then_inc(ot_ready, 1)

                def add(c):
                    v.wait_ge(t_ready, b * NT + NC + c + 1)
                    x = X[:, ds(b * NC + c, 1), :]
                    v.scalar_tensor_tensor(out=x, in0=TB[:, :], scalar=tg[:, 1:2], in1=x,
                                           op0=ALU.mult, op1=ALU.add).then_inc(t_taken, 1)

                top(0)
                for u in range(UNITS + 5):
                    if u + 1 < UNITS:
                        top(u + 1)
                    if 1 <= u <= UNITS and (u - 1) % 2:
                        take(u - 1)
                    if 2 <= u < UNITS + 2:
                        scale(u - 2)
                    if u >= 2 * NC + 3 and (u - 3) % (2 * NC) == 0:
                        add((u - 3) // (2 * NC) - 1)
                v.wait_ge(t_taken, b * NT + NT + 1)
                v.sem_inc(passed, 1)
                own.done()


BLK = 32
GW = 4 * 512


def quantise(v, own, src, val, mag, inv, scale, nb):
    blocks = lambda a: a.rearrange("p (n k) -> p n k", k=BLK)
    wide = lambda a: a.unsqueeze(2).to_broadcast([P, nb, BLK])
    own.inc(v.tensor_tensor(blocks(val), blocks(src), wide(inv), ALU.mult))
    own.wait()
    yield
    own.inc(v.tensor_scalar(mag.bitcast(U32), val.bitcast(U32), 0x7F800000, None, ALU.bitwise_and))
    own.wait()
    own.inc(v.tensor_scalar(mag, mag, 2.0 ** -6, 1.5 * 2.0 ** 20, ALU.max, ALU.mult))
    own.wait()
    yield
    own.inc(v.tensor_tensor(val, val, mag, ALU.add))
    own.wait()
    own.inc(v.tensor_tensor(val, val, mag, ALU.subtract))
    own.wait()
    yield
    own.inc(v.tensor_tensor(blocks(val), blocks(val), wide(scale), ALU.mult))
    own.wait()


def weights_phase(nc, A, WH, WL, SCL, idh, stack):
    def sb(name, shape, dt=F32):
        return stack.enter_context(nc.sbuf_tensor(name, shape, dt))

    sem = nc.alloc_semaphore
    RAW = sb("RAW", [P, KI, D])
    VAL = sb("VALW", [P, 2, GW])
    MAG = sb("MAGW", [P, GW])
    QH = sb("QHW", [P, 2, GW], F16)
    QL = sb("QLW", [P, 2, GW], F16)
    AM = sb("AMW", [P, 4, GW // BLK])
    IV = sb("IVW", [P, 4, GW // BLK])
    MX = sb("MXW", [P, 1])
    MXA = sb("MXAW", [P, 1])
    SC = sb("SCW", [P, 1])
    TH, TL = ([stack.enter_context(nc.psum_tensor(f"W_{n}{i}", [P, 2, NC, P], F16)) for i in range(4)] for n in "HL")
    raw_loaded, mx_ready, all_max, val_ready, qh_ready, ql_ready, tw_ready, hi_taken, lo_taken, own_sem = (
        sem("e_" + n) for n in ("raw", "mx", "all_max", "val", "qh", "ql", "tw", "hi_taken", "lo_taken", "own"))
    names = ("L1_ffn_gate_w", "L1_ffn_up_w", "L1_ffn_down_w")
    PER_GROUP = 5

    def dest(W, t, g, j):
        if t < 2:
            return W[:, t, :].rearrange("p (k i) -> p k i", k=KD)[:, :, (4 * g + j) * P:(4 * g + j + 1) * P]
        return W[:, t, :].rearrange("p (i h) -> p i h", i=KI)[:, 4 * j:4 * j + 4, g * P:(g + 1) * P]

    with nc.Block() as block:
        @block.sync
        def _(sp):
            for t, name in enumerate(names):
                if t:
                    sp.wait_ge(own_sem, W_OWN * t)
                w = A[name].rearrange("(n p) h -> p n h", p=P) if t < 2 else A[name].rearrange("(n p) (q h) -> p n q h", p=P, h=D)
                dst = RAW[:, :, :] if t < 2 else RAW[:, :, :].rearrange("p (n q) h -> p n q h", q=4)
                sp.dma_start(dst, w).then_inc(raw_loaded, 16)

        @block.gpsimd
        def _(pool):
            for t in range(3):
                pool.wait_ge(mx_ready, t + 1)
                pool.partition_all_reduce(MXA[:, :], MX[:, :], P, RMAX).then_inc(all_max, 1)

        @block.scalar
        def _(act):
            for t in range(3):
                for g in range(4):
                    n = 4 * t + g
                    act.wait_ge(val_ready, n + 1)
                    if n >= 2:
                        act.wait_ge(tw_ready, 4 * (n - 1))
                    nc.scalar.copy(QH[:, n % 2, :], VAL[:, n % 2, :]).then_inc(qh_ready, 1)
                    for j in range(4):
                        act.wait_ge(tw_ready, 4 * n + j + 1)
                        nc.scalar.copy(dest(WH, t, g, j), TH[j][:, 0, :, :]).then_inc(hi_taken, 1)

        @block.tensor
        def _(pe):
            for n in range(12):
                pe.wait_ge(qh_ready, n + 1)
                pe.wait_ge(ql_ready, n + 1)
                for j in range(4):
                    if n:
                        pe.wait_ge(hi_taken, 4 * (n - 1) + j + 1)
                        pe.wait_ge(lo_taken, 4 * (n - 1) + j + 1)
                    for bank, q in ((TH[j], QH), (TL[j], QL)):
                        for k in range(NC):
                            last = pe.transpose(bank[:, 0, k, :], q[:, n % 2, j * D + k * P:j * D + (k + 1) * P], idh)
                    last.then_inc(tw_ready, 1)

        @block.vector
        def _(v):
            own = Tally(v, own_sem, 0, 3 * W_OWN)

            def step(ins):
                own.inc(ins)
                own.wait()

            def low(t, g):
                for j in range(4):
                    v.wait_ge(tw_ready, 4 * (4 * t + g) + j + 1)
                    v.tensor_copy(dest(WL, t, g, j), TL[j][:, 0, :, :]).then_inc(lo_taken, 1)

            for t in range(3):
                v.wait_ge(raw_loaded, 16 * (t + 1))
                for g in range(4):
                    step(v.tensor_reduce(AM[:, g, :], RAW[:, 4 * g:4 * g + 4, :].rearrange("p n (m k) -> p (n m) k", k=BLK),
                                         AX.X, ALU.max, apply_absolute_value=True))
                am = AM[:, :, :].rearrange("p g m -> p (g m)")
                iv = IV[:, :, :].rearrange("p g m -> p (g m)")
                v.tensor_reduce(MX[:, :], am, AX.X, ALU.max).then_inc(mx_ready, 1)
                step(v.tensor_scalar(am, am, 1.0 / 448.0, 1e-30, ALU.mult, ALU.max))
                step(v.reciprocal(iv, am))
                v.wait_ge(all_max, t + 1)
                step(v.tensor_scalar(MXA[:, :], MXA[:, :], 1e-30, None, ALU.max))
                step(v.tensor_scalar(SCL[:, t:t + 1].bitcast(U32), MXA[:, :].bitcast(U32), 0x7F800000, None, ALU.bitwise_and))
                step(v.reciprocal(SC[:, :], SCL[:, t:t + 1]))
                step(v.tensor_scalar(SC[:, :], SC[:, :], 8192.0, None, ALU.mult))
                step(v.tensor_scalar(am, am, SC[:, 0:1], None, ALU.mult))
                for g in range(4):
                    n = 4 * t + g
                    val = VAL[:, n % 2, :]
                    for _ in quantise(v, own, RAW[:, 4 * g:4 * g + 4, :].rearrange("p n h -> p (n h)"), val, MAG[:, :],
                                      IV[:, g, :], AM[:, g, :], GW // BLK):
                        pass
                    v.sem_inc(val_ready, 1)
                    v.wait_ge(qh_ready, n + 1)
                    v.tensor_tensor(QL[:, n % 2, :], val, QH[:, n % 2, :], ALU.subtract).then_inc(ql_ready, 1)
                    v.wait_ge(ql_ready, n + 1)
                    low(t, g)
                while own.n < W_OWN * (t + 1):
                    step(v.tensor_copy(MX[:, :], SC[:, :]))
            own.done()


W_OWN = 40


def ffn1_phase(nc, A, X, tg, idh, WH, WL, SCL, stack):
    def sb(name, shape, dt=F32):
        return stack.enter_context(nc.sbuf_tensor(name, shape, dt))

    sem = nc.alloc_semaphore
    XN = sb("XN3", [P, D])
    XV = sb("XV3", [P, D])
    XM = sb("XM3", [P, D])
    XQ = sb("XQ3", [P, 2, D], F16)
    XT = sb("XT3", [P, 2, KD, P], F16)
    H = sb("H3", [P, INTER])
    V = sb("V3", [P, INTER])
    M = sb("M3", [P, INTER])
    HQ = sb("HQ3", [P, 2, INTER], F16)
    HT = sb("HT3", [P, 4, 2, 4, P], F16)
    SG = sb("SG3", [P, 2, 512])
    XA = sb("XA3", [P, D // BLK])
    XI = sb("XI3", [P, D // BLK])
    HA = sb("HA3", [P, INTER // BLK])
    HI = sb("HI3", [P, INTER // BLK])
    HX = sb("HX3", [P, 4])
    RSC = sb("RSC3", [P, 1])
    ST = sb("ST3", [P, 6])
    MV = sb("MV3", [P, 2])
    SD = sb("SD3", [P, 1])
    EPS = sb("EPS3", [P, 1])
    DS = sb("DS3", [P, 4])
    G, U, DN = ([stack.enter_context(nc.psum_tensor(f"H{n}{i}", [P, 512], F32)) for i in range(2)] for n in "GUD")
    T = [stack.enter_context(nc.psum_tensor(f"HT{i}", [P, 2, 4, P], F16)) for i in range(2)]
    (mv_ready, sd_ready, xv_ready, xh_ready, xl_ready, xt_ready, xt_taken, gu_ready, sg_ready, h_ready, hv_ready,
     hh_ready, hl_ready, ht_ready, ht_taken, dn_ready, x_added, ds_ready, x_own, h_own) = (sem("f_" + n) for n in (
         "mv", "sd", "xv", "xh", "xl", "xt", "xt_taken", "gu", "sg", "h", "hv", "hh", "hl", "ht", "ht_taken", "dn",
         "x_added", "ds", "x_own", "h_own"))
    passed, pe_passed, act_passed = sem("f_passed"), sem("f_pe_passed"), sem("f_act_passed")
    IC = INTER // 512

    with nc.Block() as block:
        @block.scalar
        def _(act):
            def prepare(tt):
                act.wait_ge(mv_ready, tt + 1)
                nc.scalar.activation(SD[:, :], MV[:, 1:2], ACT.Sqrt, bias=EPS[:, 0:1]).then_inc(sd_ready, 1)
                act.wait_ge(xv_ready, tt + 1)
                nc.scalar.copy(XQ[:, 0, :], XV[:, :]).then_inc(xh_ready, 1)

            def stage(tt, first=False, last=False):
                if not last:
                    act.wait_ge(xt_ready, tt + 1)
                    nc.scalar.copy(XT[:, :, :, :], T[0][:, :, :, :]).then_inc(xt_taken, 1)
                    for i in range(IC):
                        act.wait_ge(gu_ready, tt * IC + i + 1)
                        act.wait_ge(h_ready, tt * IC + i + 1)
                        nc.scalar.activation(SG[:, i % 2, :], G[i % 2][:, :], ACT.Silu, scale=DS[:, 0:1]).then_inc(sg_ready, 1)
                if not first:
                    act.wait_ge(hv_ready, tt)
                    nc.scalar.copy(HQ[:, 0, :], V[:, :]).then_inc(hh_ready, 1)
                    for q in range(4):
                        act.wait_ge(ht_ready, (tt - 1) * 4 + q + 1)
                        nc.scalar.copy(HT[:, q, :, :, :], T[q % 2][:, :, :, :]).then_inc(ht_taken, 1)

            act.wait_ge(ds_ready, N_DS)
            prepare(0)
            stage(0, first=True)
            prepare(1)
            with act.Fori(1, TILES - 1) as tt:
                stage(tt)
                prepare(tt + 1)
            stage(TILES - 1)
            stage(TILES, last=True)

        @block.tensor
        def _(pe):
            def products(bank, terms, n, last=True):
                for i, (lhs, rhs) in enumerate(terms):
                    ins = pe.matmul(bank[:, :], lhs, rhs, start=(i == 0), stop=(i == len(terms) - 1))
                return ins

            def stage(tt, first=False, last=False):
                if not last:
                    pe.wait_ge(xl_ready, tt + 1)
                    pe.wait_ge(xh_ready, tt + 1)
                    if not first:
                        pe.wait_ge(ht_taken, (tt - 1) * 4)
                    for part in range(2):
                        for k in range(KD):
                            ins = pe.transpose(T[0][:, part, k, :], XQ[:, part, k * P:(k + 1) * P], idh)
                    ins.then_inc(xt_ready, 1)
                    pe.wait_ge(xt_taken, tt + 1)
                    for i in range(IC):
                        pe.wait_ge(h_ready, tt * IC + i + 1)
                        for t, bank in ((0, G[i % 2]), (1, U[i % 2])):
                            ins = products(bank, [(XT[:, lp, k, :], W[:, t, k * INTER + i * 512:k * INTER + (i + 1) * 512])
                                                  for k in range(KD) for lp, W in ((0, WH), (0, WL), (1, WH))], 0)
                        ins.then_inc(gu_ready, 1)
                if not first:
                    pe.wait_ge(hl_ready, tt)
                    for q in range(4):
                        if q >= 2:
                            pe.wait_ge(ht_taken, (tt - 1) * 4 + q - 1)
                        for part in range(2):
                            for k in range(4):
                                at = q * 512 + k * P
                                ins = pe.transpose(T[q % 2][:, part, k, :], HQ[:, part, at:at + P], idh)
                        ins.then_inc(ht_ready, 1)
                    pe.wait_ge(x_added, tt)
                    for q in range(4):
                        pe.wait_ge(ht_taken, (tt - 1) * 4 + q + 1)
                        for k in range(4):
                            for lp, W in ((0, WH), (0, WL), (1, WH)):
                                i = 4 * q + k
                                ins = pe.matmul(DN[0][:, :], HT[:, q, lp, k, :], W[:, 2, i * D:(i + 1) * D],
                                                start=(i == 0 and lp == 0 and W is WH), stop=(i == KI - 1 and lp == 1))
                    ins.then_inc(dn_ready, 1)

            stage(0, first=True)
            with pe.Fori(1, TILES) as tt:
                stage(tt)
            stage(TILES, last=True)

        @block.vector
        def _(v):
            n_ds = [0]

            def step(ins):
                n_ds[0] += 1
                ins.then_inc(ds_ready, 1)
                v.wait_ge(ds_ready, n_ds[0])

            step(v.memset(EPS[:, :], 1e-5))
            step(v.tensor_scalar(DS[:, 0:2], SCL[:, 0:2], 2.0 ** -23, None, ALU.mult))
            step(v.tensor_scalar(DS[:, 2:3], SCL[:, 2:3], tg[:, 3:4], 2.0 ** -26, ALU.mult, ALU.mult))
            assert n_ds[0] == N_DS
            v.sem_inc(h_ready, 2)
            v.sem_inc(x_added, 1)

            def prepare(tt):
                own = Tally(v, x_own, tt, X_OWN)
                x = X[:, ds(tt, 1), :]
                own.inc(v.bn_stats(ST[:, :], x))
                own.wait()
                v.sem_inc(passed, 1)
                v.bn_aggr(MV[:, :], ST[:, :]).then_inc(mv_ready, 1)
                v.wait_ge(sd_ready, tt + 1)
                own.inc(v.reciprocal(SD[:, :], SD[:, :]))
                own.wait()
                own.inc(v.tensor_scalar(XN[:, :], x, MV[:, 0:1], SD[:, 0:1], ALU.subtract, ALU.mult))
                own.wait()
                own.inc(v.tensor_reduce(XA[:, :], XN[:, :].rearrange("p (n k) -> p n k", k=BLK), AX.X, ALU.max,
                                        apply_absolute_value=True))
                own.wait()
                own.inc(v.tensor_scalar(XA[:, :], XA[:, :], 1.0 / 448.0, 1e-30, ALU.mult, ALU.max))
                own.wait()
                own.inc(v.reciprocal(XI[:, :], XA[:, :]))
                own.inc(v.tensor_scalar(XA[:, :], XA[:, :], XS, None, ALU.mult))
                own.wait()
                for _ in quantise(v, own, XN[:, :], XV[:, :], XM[:, :], XI[:, :], XA[:, :], D // BLK):
                    pass
                v.sem_inc(xv_ready, 1)
                v.wait_ge(xh_ready, tt + 1)
                v.tensor_tensor(XQ[:, 1, :], XV[:, :], XQ[:, 0, :], ALU.subtract).then_inc(xl_ready, 1)
                own.done()

            def gated(tt, i):
                v.wait_ge(sg_ready, tt * IC + i + 1)
                v.scalar_tensor_tensor(out=H[:, i * 512:(i + 1) * 512], in0=U[i % 2][:, :], scalar=DS[:, 1:2],
                                       in1=SG[:, i % 2, :], op0=ALU.mult, op1=ALU.mult).then_inc(h_ready, 1)

            def quant(tt):
                own = Tally(v, h_own, tt, H_OWN)
                v.wait_ge(h_ready, tt * IC + IC + 2)
                own.inc(v.tensor_reduce(HA[:, :], H[:, :].rearrange("p (n k) -> p n k", k=BLK), AX.X, ALU.max,
                                        apply_absolute_value=True))
                own.wait()
                own.inc(v.tensor_reduce(HX[:, 0:1], HA[:, :], AX.X, ALU.max))
                own.wait()
                own.inc(v.tensor_scalar(HX[:, 0:1], HX[:, 0:1], 1e-30, None, ALU.max))
                own.inc(v.tensor_scalar(HA[:, :], HA[:, :], 1.0 / 448.0, 1e-30, ALU.mult, ALU.max))
                own.wait()
                own.inc(v.reciprocal(HI[:, :], HA[:, :]))
                own.inc(v.tensor_scalar(HX[:, 1:2].bitcast(U32), HX[:, 0:1].bitcast(U32), 0x7F800000, None, ALU.bitwise_and))
                own.wait()
                own.inc(v.reciprocal(HX[:, 2:3], HX[:, 1:2]))
                own.inc(v.tensor_scalar(RSC[:, :], HX[:, 1:2], DS[:, 2:3], None, ALU.mult))
                own.wait()
                own.inc(v.tensor_scalar(HA[:, :], HA[:, :], HX[:, 2:3], 8192.0, ALU.mult, ALU.mult))
                own.wait()
                yield from quantise(v, own, H[:, :], V[:, :], M[:, :], HI[:, :], HA[:, :], INTER // BLK)
                v.sem_inc(hv_ready, 1)
                v.wait_ge(hh_ready, tt + 1)
                v.tensor_tensor(HQ[:, 1, :], V[:, :], HQ[:, 0, :], ALU.subtract).then_inc(hl_ready, 1)
                v.wait_ge(hl_ready, tt + 1)
                own.done()

            def add(tt):
                v.wait_ge(dn_ready, tt + 1)
                x = X[:, ds(tt, 1), :]
                v.scalar_tensor_tensor(out=x, in0=DN[0][:, :], scalar=RSC[:, 0:1], in1=x,
                                       op0=ALU.mult, op1=ALU.add).then_inc(x_added, 1)

            def stage(tt, first=False, last=False):
                parts = iter(()) if first else quant(tt - 1)
                for i in range(IC):
                    next(parts, None)
                    if not last:
                        gated(tt, i)
                next(parts, None)

            prepare(0)
            stage(0, first=True)
            prepare(1)
            with v.Fori(1, TILES - 1) as tt:
                stage(tt)
                prepare(tt + 1)
                add(tt - 1)
                v.wait_ge(x_added, tt + 1)
                v.sem_inc(passed, 1)
            stage(TILES - 1)
            add(TILES - 2)
            v.wait_ge(x_added, TILES)
            stage(TILES, last=True)
            add(TILES - 1)


N_DS = 3
X_OWN = 13
H_OWN = 15


def extra_inputs(z):
    out = {"shape_constants": shape_constants(), **spline_constants()}
    out["spline_windows"] = windows([z[f"L0_ffn_{n}_cp"] for n in ("gate", "up", "down")])
    return out


PRE_DVE = 11
DVE_OWN_A = 41
ACT_OWN_A = 2


def build_program(nc, A, out, upto=9):
    with ExitStack() as top:
        X = top.enter_context(nc.sbuf_tensor("X", [P, TILES, D], F32))
        CST = top.enter_context(nc.sbuf_tensor("CST", [P, CST_W], F32))
        IDB = top.enter_context(nc.sbuf_tensor("IDB", [P, P], BF16))
        IDH = top.enter_context(nc.sbuf_tensor("IDH", [P, P], F16))
        TG = top.enter_context(nc.sbuf_tensor("TG", [P, 4], F32))
        loaded, ready, stored = nc.alloc_semaphore("loaded"), nc.alloc_semaphore("consts_ready"), nc.alloc_semaphore("stored")
        xr = A["x"].rearrange("b (c p) d -> p (b c) d", p=P)
        with nc.Block() as block:
            @block.sync
            def _(sp):
                sp.dma_start(CST[:, :], A["shape_constants"]).then_inc(loaded, 16)
                for q, name in enumerate(("g_xattn", "g_ffn")):
                    sp.dma_start(TG[:, 2 * q:2 * q + 2], A[name].rearrange("(a n) -> a n", a=1).to_broadcast([P, 2])).then_inc(loaded, 16)
                for b in range(B):
                    sp.dma_start(X[:, b * NC:(b + 1) * NC, :], xr[:, b * NC:(b + 1) * NC, :]).then_inc(loaded, 16)

            @block.vector
            def _(v):
                v.wait_ge(loaded, 7 * 16)
                v.tensor_copy(IDB[:, :], CST[:, 0:P]).then_inc(ready, 1)
                v.tensor_copy(IDH[:, :], CST[:, 0:P]).then_inc(ready, 1)

            @block.scalar
            def _(act):
                act.wait_ge(loaded, 7 * 16)
                nc.scalar.activation(TG[:, :], TG[:, :], ACT.Tanh).then_inc(ready, 1)
                act.wait_ge(ready, 3)

        with ExitStack() as stack:
            mlstm_phase(nc, A, X, TG, CST, CST[:, 0:P], IDB[:, :], stack)
        if upto >= 2:
            SCL = top.enter_context(nc.sbuf_tensor("SCL", [P, 3], F32))
            with ExitStack() as weights:
                WH = weights.enter_context(nc.sbuf_tensor("W0H", [P, 3, RUNS], F16))
                WL = weights.enter_context(nc.sbuf_tensor("W0L", [P, 3, RUNS], F16))
                with ExitStack() as stack:
                    spline_phase(nc, A, CST[:, CST_W - 1:CST_W], WH, WL, SCL, stack)
                with ExitStack() as stack:
                    ffn0_phase(nc, A, X, TG, CST[:, 0:P], WH, WL, SCL, stack)
        if upto >= 3:
            with ExitStack() as stack:
                attention_phase(nc, A, X, TG, CST[:, 0:P], stack)
        if upto >= 4:
            with ExitStack() as weights:
                WH = weights.enter_context(nc.sbuf_tensor("W1H", [P, 3, RUNS], F16))
                WL = weights.enter_context(nc.sbuf_tensor("W1L", [P, 3, RUNS], F16))
                with ExitStack() as stack:
                    weights_phase(nc, A, WH, WL, SCL, IDH[:, :], stack)
                with ExitStack() as stack:
                    ffn1_phase(nc, A, X, TG, IDH[:, :], WH, WL, SCL, stack)
        orr = out.rearrange("b (c p) d -> p (b c) d", p=P)
        with nc.Block() as block:
            @block.sync
            def _(sp):
                for b in range(B):
                    sp.dma_start(orr[:, b * NC:(b + 1) * NC, :], X[:, b * NC:(b + 1) * NC, :]).then_inc(stored, 16)
                sp.wait_ge(stored, 16 * B)


_INS = ["x", "ctx_2048", "g_xattn", "g_ffn", "L0_xattn_Wi", "L0_xattn_bi", "L0_xattn_Wf", "L0_xattn_bf",
        "L0_xattn_ln_scale", "L1_ffn_gate_w", "L1_ffn_up_w", "L1_ffn_down_w"]


def kernel(**inputs):
    import numpy as _np
    import concourse.bacc as _bacc
    from concourse import mybir as _mybir
    from concourse.bass_utils import run_bass_kernel_spmd as _run

    nc = _bacc.Bacc("TRN2", target_bir_lowering=False, num_devices=1)
    given = {name: _np.asarray(a) for name, a in inputs.items()}
    arrays = {name: _np.ascontiguousarray(given[name]) for name in _INS}
    arrays.update(extra_inputs(given))
    arrays = {f"in_{name}_dram": a for name, a in arrays.items()}
    args = {}
    for name, a in arrays.items():
        args[name[3:-5]] = nc.dram_tensor(name, a.shape, _mybir.dt.from_np(a.dtype), kind="ExternalInput").ap()
    out = nc.dram_tensor("out_0_dram", (B, S, D), _mybir.dt.float32, kind="ExternalOutput").ap()
    build_program(nc, args, out)
    r = _run(nc, [arrays], core_ids=[0])
    return r.results[0]["out_0_dram"]
```

```python
from contextlib import ExitStack

import concourse.bass as bass
from concourse import mybir
import numpy as np

F32 = mybir.dt.float32
F16 = mybir.dt.float16
BF16 = mybir.dt.bfloat16
U32 = mybir.dt.uint32
U8 = mybir.dt.uint8
ALU = mybir.AluOpType
ACT = mybir.ActivationFunctionType
AX = mybir.AxisListType
RMAX = bass.bass_isa.ReduceOp.max
ds = bass.ds

P = 128
B, S, D = 4, 512, 512
NC = S // P
KD = D // P
TILES = B * NC
NH, DH = 16, 32
HG = P // DH
VW = DH + 1
INTER = 2048
KI = INTER // P


class Tally:

    def __init__(self, eng, sem, it, per):
        self.eng, self.sem, self.it, self.per, self.n = eng, sem, it, per, 0

    def inc(self, ins):
        self.n += 1
        ins.then_inc(self.sem, 1)

    def wait(self):
        self.eng.wait_ge(self.sem, self.it * self.per + self.n)

    def done(self):
        assert self.n == self.per, self.n


def shape_constants():
    ident = np.eye(P, dtype=np.float32)
    t, s = np.mgrid[0:P, 0:P]
    future = np.where(t > s, np.float32(-1e30), np.float32(0))
    k, h = np.mgrid[0:P, 0:NH]
    pick = ((k % 32 == h) & (k < 96)).astype(np.float32)
    p, c = np.mgrid[0:P, 0:HG * VW]
    own = np.where(p // DH == c // VW, np.float32(DH ** -0.5), np.float32(0))
    return np.concatenate([ident, future, pick, own, np.arange(P)[:, None]], axis=1).astype(np.float32)


CST_W = P + P + NH + HG * VW + 1


def mlstm_phase(nc, A, X, tg, CST, idf, idb, spline, stack):
    def sb(name, shape, dt=F32):
        return stack.enter_context(nc.sbuf_tensor(name, shape, dt))

    def ps(name):
        return stack.enter_context(nc.psum_tensor(name, [P, 512], F32))

    sem = nc.alloc_semaphore
    XN = sb("XN", [P, NC, D])
    CTX = sb("CTX", [P, NC, D])
    QT = sb("QT", [P, KD, S])
    KT = sb("KT", [P, KD, S])
    VA = sb("VA", [P, NC, NH, VW])
    OUT = sb("OUT", [P, NC, NH, VW])
    HN = sb("HN", [P, NC * NH, DH])
    SQ = sb("SQ", [P, NC * NH, DH])
    KU = sb("KU", [P, 6, D])
    SS = sb("SS", [P, 2, NC - 1, HG * VW])
    DD = sb("DD", [P, 2, S])
    CC = sb("CC", [P, 2, S])
    WG = sb("WG", [P, 12, 32])
    GS = sb("GS", [P, NC, 2, 96])
    TM = sb("TM", [P, 13, NH])
    ROW = sb("ROW", [96, 8, S])
    ZF, ZI, AZ, MZ, LF, FC, FM, EL = (ROW[:, i, :] for i in range(8))
    VV = sb("VV", [96, 2, S])
    RR = sb("RR", [96, 2, S])
    NP = sb("NP", [96, 2, S], BF16)
    T2 = sb("T2", [96, 2, S], BF16)
    UW = sb("UW", [NH, 13, P])
    ONE = sb("ONE", [96, S])
    BIAS = sb("BIAS", [96, 2])
    GLN = sb("GLN", [P, D])
    ST = sb("ST", [P, NC, 6])
    MV = sb("MV", [P, NC, 2])
    SD = sb("SD", [P, NC])
    RS = sb("RS", [P, NC])
    MU = sb("MU", [P, NC * NH])
    VR = sb("VR", [P, NC * NH])
    DN = sb("DN", [P, NC * NH])
    FUT = sb("FUT", [P, NC, P], BF16)
    PICK = sb("PICK", [P, NH], BF16)
    EPS = sb("EPS", [P, 3])
    T = [ps("T0"), ps("T1")]
    QK = [ps("QK0"), ps("QK1")]
    E = [ps("E0"), ps("E1")]
    O = [ps("O0"), ps("O1")]

    ctx_loaded, w_loaded, pre_dve, pre_act = (sem("a_" + n) for n in ("ctx_loaded", "w_loaded", "pre_dve", "pre_act"))
    pre_pool = sem("a_pre_pool")
    mv_ready, sd_ready, xn_ready, t_ready = (sem("a_" + n) for n in ("mv_ready", "sd_ready", "xn_ready", "t_ready"))
    t_taken = [sem("a_t_taken0"), sem("a_t_taken1")]
    va_ready, ku_ready, az_ready, el_ready = (sem("a_" + n) for n in ("va_ready", "ku_ready", "az_ready", "el_ready"))
    vv_ready, np1_ready, rr_ready, t2_ready, r3_ready, np_ready, uw_ready = (
        sem("a_" + n) for n in ("vv_ready", "np1", "rr", "t2", "r3", "np_ready", "uw_ready"))
    gs_ready, ss_ready, qe_ready, d_ready, c_ready, pv_done, o_taken = (
        sem("a_" + n) for n in ("gs_ready", "ss_ready", "qe_ready", "d_ready", "c_ready", "pv_done", "o_taken"))
    hc_ready, sq_ready, vr_ready, sv_ready = (sem("a_" + n) for n in ("hc", "sq", "vr", "sv"))
    passed = [sem(f"a_passed{i}") for i in range(4)]
    dve_own, fin_own, act_own = sem("a_dve_own"), sem("a_fin_own"), sem("a_act_own")
    NT = 20
    ctx = A["ctx_2048"].rearrange("b (c p) d -> b p c d", p=P)

    with nc.Block() as block:
        @block.sync
        def _(sp):
            sp.dma_start(WG[:, :, 0:NH], A["L0_xattn_Wi"].rearrange("(k p) h -> p k h", p=P)).then_inc(w_loaded, 16)
            sp.dma_start(WG[:, :, NH:2 * NH], A["L0_xattn_Wf"].rearrange("(k p) h -> p k h", p=P)).then_inc(w_loaded, 16)
            sp.dma_start(GLN[:, :], A["L0_xattn_ln_scale"].rearrange("(a d) -> a d", a=1).to_broadcast([P, D])).then_inc(w_loaded, 16)
            sp.wait_ge(pre_pool, 3)
            for r in range(3):
                for q, name in enumerate(("L0_xattn_bi", "L0_xattn_bf")):
                    sp.dma_start(BIAS[32 * r:32 * r + NH, q:q + 1], A[name].rearrange("(h a) -> h a", a=1)).then_inc(w_loaded, 16)
            sp.dma_start(CTX[:, :, :], ctx[0]).then_inc(ctx_loaded, 16)
            spline.load(sp)
            with sp.Fori(1, B) as b:
                sp.wait_ge(t_ready, b * NT + (8 - NT))
                sp.sem_inc(passed[3], 1)
                sp.wait_ge(va_ready, b * 2)
                sp.wait_ge(ku_ready, b)
                sp.dma_start(CTX[:, :, :], ctx[ds(b, 1)].rearrange("a p c d -> p (a c) d")).then_inc(ctx_loaded, 16)
            spline.store(sp)

        @block.gpsimd
        def _(pool):
            pool.memset(BIAS[:, :], 0.0).then_inc(pre_pool, 1)
            pool.memset(GS[:, :, :, :], 0.0).then_inc(pre_pool, 1)
            pool.memset(VA[:, :, :, DH:VW], 1.0).then_inc(pre_pool, 1)

            def batch(b, first=False):
                pool.wait_ge(xn_ready, b * NC + 1)
                pool.sem_inc(passed[0], 1)
                pool.wait_ge(ctx_loaded, b * 16 + 16)
                pool.sem_inc(passed[0], 1)
                pool.tensor_copy(VA[:, :, :, 0:DH],
                                 CTX[:, :, :].rearrange("p c (h d) -> p c h d", h=NH)).then_inc(va_ready, 1)
                if not first:
                    pool.wait_ge(hc_ready, b)
                    pool.sem_inc(passed[0], 1)
                pool.memset(OUT[:, 0, :, :], 0.0).then_inc(va_ready, 1)

            batch(0, first=True)
            spline.largest(pool)
            with pool.Fori(1, B) as b:
                batch(b)

        @block.scalar
        def _(act):
            def norms(b):
                act.wait_ge(hc_ready, b + 1)
                nc.scalar.activation(SQ[:, :, :], HN[:, :, :], ACT.Square).then_inc(sq_ready, 1)
                act.wait_ge(vr_ready, b + 1)
                nc.scalar.activation(VR[:, :], VR[:, :], ACT.Sqrt, scale=1.0 / DH, bias=EPS[:, 2:3]).then_inc(sv_ready, 1)

            def batch(b, first=False):
                own = Tally(act, act_own, b, ACT_OWN_A)
                act.wait_ge(mv_ready, b + 1)
                act.wait_ge(pre_dve, PRE_DVE)
                nc.scalar.activation(SD[:, :], MV[:, :, 1], ACT.Sqrt, bias=EPS[:, 0:1]).then_inc(sd_ready, 1)
                for n in range(8):
                    act.wait_ge(t_ready, b * NT + n + 1)
                    dst = (QT if n < 4 else KT)[:, n % 4, :]
                    nc.scalar.copy(dst, T[n % 2][:, :]).then_inc(t_taken[n % 2], 1)
                if not first:
                    norms(b - 1)
                act.wait_ge(az_ready, b + 1)
                own.inc(nc.scalar.activation(EL, AZ, ACT.Exp, scale=-1.0))
                own.wait()
                nc.scalar.activation(EL, EL, ACT.Ln, bias=EPS[0:96, 1:2]).then_inc(el_ready, 1)
                act.wait_ge(vv_ready, b * 3 + 3)
                nc.scalar.copy(NP[:, :, :], VV[:, :, :]).then_inc(np1_ready, 1)
                i = 0
                for c in range(1, NC):
                    nc.scalar.activation(UW[:, i:i + c, :], VV[0:NH, 0, 0:c * P], ACT.Exp,
                                         bias=VV[0:NH, 1, c * P - 1:c * P]).then_inc(uw_ready, 1)
                    i += c
                act.wait_ge(rr_ready, b + 1)
                nc.scalar.copy(T2[64:96, :, :], RR[64:96, :, :]).then_inc(t2_ready, 1)
                own.inc(nc.scalar.copy(NP[32:64, :, :], RR[32:64, :, :]))
                for c in range(1, NC):
                    nc.scalar.activation(UW[:, 5 + c, :], VV[0:NH, 1, c * P:(c + 1) * P], ACT.Exp,
                                         bias=FM[0:NH, c:c + 1]).then_inc(uw_ready, 1)
                nc.scalar.activation(UW[:, 9:13, :], EL[0:NH, :], ACT.Exp, scale=-1.0).then_inc(uw_ready, 1)
                act.wait_ge(r3_ready, b + 1)
                nc.scalar.copy(NP[64:96, :, :], RR[64:96, :, :]).then_inc(np_ready, 1)
                for h in range(NH):
                    act.wait_ge(qe_ready, b * NH + h + 1)
                    if h >= 2:
                        act.wait_ge(c_ready, b * NH + h - 1)
                    nc.scalar.activation(DD[:, h % 2, :], E[h % 2][:, :], ACT.Exp).then_inc(d_ready, 1)
                own.done()

            batch(0, first=True)
            with act.Fori(1, B) as b:
                batch(b)
            norms(B - 1)

        @block.tensor
        def _(pe):
            pe.wait_ge(pre_dve, PRE_DVE)
            pe.wait_ge(w_loaded, 9 * 16)
            with pe.Fori(0, B) as b:
                def keep_warm(n, bank=E[0]):
                    for _ in range(n):
                        pe.matmul(bank[:, :], idb, FUT[:, :, :], start=True, stop=True)

                def bank(n):
                    if n >= 2:
                        pe.wait_ge(t_taken[n % 2], b * (NT // 2) + n // 2)
                    return T[n % 2]

                def taken(n):
                    pe.wait_ge(t_taken[n % 2], b * (NT // 2) + n // 2 + 1)

                for n in range(8):
                    if n == 4:
                        pe.wait_ge(ctx_loaded, b * 16 + 16)
                    src, k = (XN if n < 4 else CTX), n % 4
                    t = bank(n)
                    for c in range(NC):
                        if n == 0:
                            pe.wait_ge(xn_ready, b * NC + c + 1)
                        last = pe.transpose(t[:, c * P:(c + 1) * P], src[:, c, k * P:(k + 1) * P], idf)
                    last.then_inc(t_ready, 1)
                t = bank(8)
                taken(7)
                taken(6)
                for c in range(NC):
                    for k in range(2 * KD):
                        src = QT if k < KD else KT
                        last = pe.matmul(t[:, c * 32:(c + 1) * 32], src[:, k % KD, c * P:(c + 1) * P], WG[:, k, :],
                                         start=(k == 0), stop=(k == 2 * KD - 1))
                last.then_inc(t_ready, 1)
                for n in (9, 10):
                    t = bank(n)
                    taken(8)
                    for c in range(NC):
                        last = pe.transpose(t[0:96, c * P:(c + 1) * P], GS[:, c, n - 9, :], idf)
                    last.then_inc(t_ready, 1)
                t = bank(11)
                pe.wait_ge(uw_ready, b * 7 + 7)
                pe.sem_inc(passed[2], 1)
                for i in range(13):
                    last = pe.transpose(t[:, i * NH:(i + 1) * NH], UW[:, i, :], idf[0:NH, 0:NH])
                last.then_inc(t_ready, 1)
                keep_warm(WARM_START)
                pe.wait_ge(va_ready, b * 2 + 2)
                pe.wait_ge(ku_ready, b + 1)

                def scores(h):
                    g, j = divmod(h, HG)
                    r = slice(DH * j, DH * j + DH)
                    if h >= 2:
                        pe.wait_ge(c_ready, b * NH + h - 1)
                    for c in range(NC):
                        pe.matmul(QK[h % 2][:, c * P:(c + 1) * P], KT[r, g, c * P:(c + 1) * P],
                                  QT[r, g, c * P:(c + 1) * P], start=True, stop=True)
                    e = E[h % 2]
                    pick = PICK[0:96, h:h + 1]
                    pe.matmul(e[:, :], idb, FUT[:, :, :], start=True, stop=False)
                    pe.matmul(e[:, :], pick.to_broadcast([96, P]), NP[:, 1, :], start=False, stop=False)
                    for c in range(NC):
                        last = pe.matmul(e[:, c * P:(c + 1) * P], NP[:, 0, c * P:(c + 1) * P],
                                         pick.to_broadcast([96, P]), start=False, stop=(c == NC - 1))
                    last.then_inc(qe_ready, 1)

                def weigh(h):
                    pair, jj = divmod(h, 2)
                    if jj == 0 and pair >= 2:
                        pe.wait_ge(o_taken, b * (NH // 2) + pair - 1)
                    pe.wait_ge(c_ready, b * NH + h + 1)
                    o = O[pair % 2]
                    for c in range(NC):
                        at = (2 * c + jj) * VW
                        last = pe.matmul(o[:, at:at + VW], CC[:, h % 2, c * P:(c + 1) * P], VA[:, c, h, :],
                                         start=True, stop=True)
                    last.then_inc(pv_done, 1)

                def state(g):
                    t = bank(12 + 2 * g)
                    i = 0
                    for c in range(1, NC):
                        for u in range(c):
                            last = pe.matmul(t[:, (c - 1) * HG * VW:c * HG * VW], KU[:, i, g * P:(g + 1) * P],
                                             VA[:, u, g * HG:(g + 1) * HG, :], start=(u == 0), stop=(u == c - 1))
                            i += 1
                    last.then_inc(t_ready, 1)

                def read_state(g):
                    t = bank(13 + 2 * g)
                    taken(12 + 2 * g)
                    for c in range(1, NC):
                        last = pe.matmul(t[:, (c - 1) * HG * VW:c * HG * VW], QT[:, g, c * P:(c + 1) * P],
                                         SS[:, g % 2, c - 1, :], start=True, stop=True)
                    last.then_inc(t_ready, 1)

                state(0)
                pe.wait_ge(np_ready, b + 1)
                scores(0)
                for h in range(NH):
                    if h % HG == 0:
                        read_state(h // HG)
                    if h + 1 < NH:
                        scores(h + 1)
                    weigh(h)
                    keep_warm(WARM_HEAD, E[h % 2])
                    if h % HG == 2 and h // HG + 1 < NH // HG:
                        state(h // HG + 1)

        @block.vector
        def _(v):
            v.wait_ge(w_loaded, 9 * 16)
            n_pre = [0]

            def pre(ins):
                n_pre[0] += 1
                ins.then_inc(pre_dve, 1)

            pre(v.memset(EPS[:, 0:1], 1e-5))
            pre(v.memset(EPS[:, 1:2], 1.0))
            pre(v.memset(EPS[:, 2:3], 1e-6))
            pre(v.memset(ONE[:, :], 1.0))
            for c in range(NC):
                pre(v.tensor_copy(FUT[:, c, :], CST[:, P:2 * P]))
            pre(v.tensor_copy(PICK[:, :], CST[:, 2 * P:2 * P + NH]))
            pre(v.tensor_tensor(WG[:, 4:8, :], WG[:, 4:8, :], WG[:, 8:12, :], ALU.add))
            pre(v.tensor_scalar(GLN[:, :], GLN[:, :], tg[:, 0:1], -1.0, ALU.mult, ALU.mult))
            assert n_pre[0] == PRE_DVE
            v.wait_ge(pre_dve, PRE_DVE)
            v.wait_ge(pre_pool, 3)
            own_mask = CST[:, 2 * P + NH:CST_W - 1]
            def finish(b):
                own = Tally(v, fin_own, b, FIN_OWN_A)
                sums = OUT[:, :, :, DH].rearrange("p c h -> p (c h)")
                own.inc(v.scalar_tensor_tensor(out=DN[:, :], in0=sums, scalar=-1.0, in1=sums, op0=ALU.mult, op1=ALU.max))
                own.wait()
                own.inc(v.tensor_tensor(DN[:, :], DN[:, :], TM[:, 9:13, :].rearrange("p c h -> p (c h)"), ALU.max))
                own.wait()
                own.inc(v.tensor_scalar(DN[:, :], DN[:, :], 1e-6, None, ALU.add))
                own.wait()
                own.inc(v.reciprocal(DN[:, :], DN[:, :]))
                own.wait()
                bc = lambda x: x.unsqueeze(2).to_broadcast([P, NC * NH, DH])
                own.inc(v.tensor_tensor(HN[:, :, :], OUT[:, :, :, 0:DH].rearrange("p c h d -> p (c h) d"), bc(DN[:, :]), ALU.mult))
                own.wait()
                own.inc(v.tensor_reduce(MU[:, :], HN[:, :, :], AX.X, ALU.add))
                own.wait()
                v.scalar_tensor_tensor(out=HN[:, :, :], in0=bc(MU[:, :]), scalar=1.0 / DH, in1=HN[:, :, :],
                                       op0=ALU.mult, op1=ALU.subtract).then_inc(hc_ready, 1)
                v.wait_ge(sq_ready, b + 1)
                v.tensor_reduce(VR[:, :], SQ[:, :, :], AX.X, ALU.add).then_inc(vr_ready, 1)
                v.wait_ge(sv_ready, b + 1)
                own.inc(v.reciprocal(VR[:, :], VR[:, :]))
                own.wait()
                yield
                own.inc(v.tensor_tensor(HN[:, :, :], HN[:, :, :], bc(VR[:, :]), ALU.mult))
                own.wait()
                yield
                hn = HN[:, :, :].rearrange("p (c h) d -> p c (h d)", c=NC)
                own.inc(v.tensor_tensor(hn, hn, GLN[:, :].unsqueeze(1).to_broadcast([P, NC, D]), ALU.mult))
                own.wait()
                yield
                x = X[:, ds(b * NC, NC), :]
                own.inc(v.tensor_tensor(x, x, hn, ALU.add))
                own.wait()
                own.done()

            def batch(b, first=False):
                own = Tally(v, dve_own, b, DVE_OWN_A)
                for c in range(NC):
                    own.inc(v.bn_stats(ST[:, c, :], X[:, ds(b * NC + c, 1), :]))
                own.wait()
                v.sem_inc(passed[1], 1)
                for c in range(NC):
                    ins = v.bn_aggr(MV[:, c, :], ST[:, c, :])
                    if c < NC - 1:
                        own.inc(ins)
                ins.then_inc(mv_ready, 1)
                v.wait_ge(sd_ready, b + 1)
                own.inc(v.reciprocal(RS[:, :], SD[:, :]))
                own.wait()
                for c in range(NC):
                    v.tensor_scalar(XN[:, c, :], X[:, ds(b * NC + c, 1), :], MV[:, c, 0:1], RS[:, c:c + 1],
                                    ALU.subtract, ALU.mult).then_inc(xn_ready, 1)
                before = iter(()) if first else finish(b - 1)
                next(before, None)
                v.wait_ge(t_ready, b * NT + 9)
                gates = T[0][:, 0:P].rearrange("p (c q h) -> p (c q) h", c=NC, q=2)
                gs = GS[:, :, :, :].rearrange("p c q r -> p (c q) r")
                for r in range(3):
                    ins = v.tensor_copy(gs[:, :, 32 * r:32 * r + NH], gates)
                    if r < 2:
                        own.inc(ins)
                ins.then_inc(t_taken[0], 1)
                v.wait_ge(t_ready, b * NT + 10)
                v.tensor_scalar(ZI, T[1][0:96, :], BIAS[:, 0:1], None, ALU.add).then_inc(t_taken[1], 1)
                v.wait_ge(t_ready, b * NT + 11)
                v.tensor_scalar(ZF, T[0][0:96, :], BIAS[:, 1:2], None, ALU.add).then_inc(t_taken[0], 1)
                v.wait_ge(t_taken[0], b * (NT // 2) + 6)
                v.scalar_tensor_tensor(out=AZ, in0=ZF, scalar=-1.0, in1=ZF, op0=ALU.mult, op1=ALU.max).then_inc(az_ready, 1)
                own.inc(v.tensor_scalar(MZ, ZF, 0.0, None, ALU.min))
                own.wait()
                next(before, None)
                v.wait_ge(el_ready, b + 1)
                own.inc(v.tensor_tensor(LF, MZ, EL, ALU.subtract))
                own.wait()
                own.inc(v.tensor_tensor_scan(FC, ONE[:, :], LF, 0.0, ALU.mult, ALU.add))
                own.wait()
                v.tensor_tensor(VV[:, 0, :], ZI, FC, ALU.subtract).then_inc(vv_ready, 1)
                v.wait_ge(vv_ready, b * 3 + 1)
                own.inc(v.tensor_tensor_scan(MZ, ONE[:, :], VV[:, 0, :], -3.0e38, ALU.mult, ALU.max))
                own.wait()
                own.inc(v.tensor_tensor(EL, FC, MZ, ALU.add))
                for c in range(1, NC):
                    own.inc(v.tensor_copy(FM[:, c:c + 1], MZ[:, c * P - 1:c * P]))
                own.wait()
                v.tensor_scalar(VV[:, 1, :], MZ, -1.0, None, ALU.mult).then_inc(vv_ready, 2)
                next(before, None)
                v.wait_ge(np1_ready, b + 1)
                v.tensor_tensor(RR[:, :, :], VV[:, :, :], NP[:, :, :], ALU.subtract).then_inc(rr_ready, 1)
                v.wait_ge(t2_ready, b + 1)
                v.tensor_tensor(RR[64:96, :, :], RR[64:96, :, :], T2[64:96, :, :], ALU.subtract).then_inc(r3_ready, 1)
                next(before, None)
                v.wait_ge(t_ready, b * NT + 12)
                v.tensor_copy(TM[:, :, :], T[1][:, 0:13 * NH].rearrange("p (i h) -> p i h", h=NH)).then_inc(t_taken[1], 1)
                v.wait_ge(t_taken[1], b * (NT // 2) + 6)
                v.wait_ge(ctx_loaded, b * 16 + 16)
                i = 0
                for c in range(1, NC):
                    for t in range(c):
                        ins = v.tensor_tensor(
                            KU[:, i, :].rearrange("p (h d) -> p h d", h=NH),
                            CTX[:, t, :].rearrange("p (h d) -> p h d", h=NH),
                            TM[:, i, :].unsqueeze(2).to_broadcast([P, NH, DH]), ALU.mult)
                        i += 1
                        if i < 6:
                            own.inc(ins)
                ins.then_inc(ku_ready, 1)

                def take_state(g):
                    v.wait_ge(t_ready, b * NT + 13 + 2 * g)
                    v.tensor_tensor(SS[:, g % 2, :, :], T[0][:, 0:(NC - 1) * HG * VW].rearrange("p (c f) -> p c f", c=NC - 1),
                                    own_mask.unsqueeze(1).to_broadcast([P, NC - 1, HG * VW]),
                                    ALU.mult).then_inc(t_taken[0], 1)

                def take_read(g):
                    v.wait_ge(t_ready, b * NT + 14 + 2 * g)
                    for c in range(1, NC):
                        ins = v.tensor_tensor(
                            OUT[:, c, g * HG:(g + 1) * HG, :],
                            T[1][:, (c - 1) * HG * VW:c * HG * VW].rearrange("p (h f) -> p h f", h=HG),
                            TM[:, 5 + c, g * HG:(g + 1) * HG].unsqueeze(2).to_broadcast([P, HG, VW]), ALU.mult)
                        if c < NC - 1:
                            own.inc(ins)
                    ins.then_inc(t_taken[1], 1)
                    v.wait_ge(t_taken[1], b * (NT // 2) + 7 + g)

                def take_pair(pair):
                    v.wait_ge(pv_done, b * NH + 2 * pair + 2)
                    o = OUT[:, :, 2 * pair:2 * pair + 2, :]
                    v.tensor_tensor(o, o, O[pair % 2][:, 0:2 * NC * VW].rearrange("p (c j f) -> p c j f", c=NC, j=2),
                                    ALU.add).then_inc(o_taken, 1)

                v.wait_ge(va_ready, b * 2 + 2)
                for h in range(NH):
                    if h % HG == 0:
                        take_state(h // HG)
                    v.wait_ge(d_ready, b * NH + h + 1)
                    if h >= 2:
                        v.wait_ge(pv_done, b * NH + h - 1)
                    v.scalar_tensor_tensor(out=CC[:, h % 2, :], in0=QK[h % 2][:, :], scalar=DH ** -0.5,
                                           in1=DD[:, h % 2, :], op0=ALU.mult, op1=ALU.mult).then_inc(c_ready, 1)
                    if h % HG == 0:
                        take_read(h // HG)
                    if h % 2 == 1 and h >= 3:
                        take_pair(h // 2 - 1)
                    if first:
                        next(coefficients, None)
                take_pair(NH // 2 - 1)
                v.wait_ge(o_taken, (b + 1) * (NH // 2))
                own.done()

            coefficients = spline.vector_steps(v)
            batch(0, first=True)
            for _ in coefficients:
                pass
            with v.Fori(1, B) as b:
                batch(b)
            for _ in finish(B - 1):
                pass


N_FLAT = D * INTER
N_CTRL = int(D * INTER / 128.9)
RUNS = N_FLAT // P
RC = RUNS // P
QW = 2048
SUB = 512
PARTS = ((0, 0), (0, 1), (0, 2), (1, 0), (1, 1), (2, 0))


def run_orders():
    pos = np.arange(RUNS)
    gate = KD * (pos % INTER) + pos // INTER
    down = KI * (pos % D) + pos // D
    return gate, down


def spline_grid():
    t = np.linspace(0.0, N_CTRL - 1.0, N_FLAT, dtype=np.float64)
    i = np.clip(np.floor(t).astype(np.int64), 0, N_CTRL - 2)
    return t, i


def bf16_round(a):
    u = np.ascontiguousarray(a, dtype=np.float32).view(np.uint32).astype(np.uint64)
    u = (u + 0x7FFF + ((u >> 16) & 1)) & 0xFFFF0000
    return u.astype(np.uint32).view(np.float32)


def spline_constants():
    t, i = spline_grid()
    first = np.arange(RUNS) * P
    phase = t[first] - i[first]
    step = (N_CTRL - 1.0) / (N_FLAT - 1.0)
    basis = 0.5 * np.array([[0, 2, 0, 0], [-1, 0, 1, 0], [2, -5, 4, -1], [-1, 3, -3, 1]], np.float64)
    binom = [[1, 0, 0, 0], [1, 1, 0, 0], [1, 2, 1, 0], [1, 3, 3, 1]]
    coef = np.zeros((2, 4, 4, RUNS))
    for piece in range(2):
        u = phase - piece
        for m in range(4):
            for k in range(4):
                coef[piece, m, k] = sum(binom[l][m] * u ** (l - m) * basis[l, k] for l in range(m, 4))
    starts = (i.reshape(RUNS, P) == i[first][:, None]).sum(1).astype(np.float32)
    orders = run_orders()
    coefs = np.stack([coef[..., o] for o in orders]).reshape(2, 2, 4, 4, P, RC)
    coefs = np.ascontiguousarray(coefs.transpose(4, 0, 1, 2, 3, 5)).astype(np.float32).reshape(P, -1)
    starts = np.stack([starts[orders[0]], starts[orders[0]], starts[orders[1]]])
    power = np.stack([(np.arange(P) * step) ** m for m in range(4)])
    parts, rest = [], power
    for _ in range(3):
        parts.append(bf16_round(rest))
        rest = rest - parts[-1]
    powers = np.concatenate([parts[q] for _, q in PARTS]).astype(np.float32)
    return {"spline_coefs": coefs, "spline_starts": starts, "spline_powers": powers}


def windows(cp):
    _, i = spline_grid()
    base = i[np.arange(RUNS) * P]
    out = []
    for t, a in enumerate(cp):
        order = run_orders()[t // 2]
        at = np.clip(base[order][None, :] - 1 + np.arange(5)[:, None], 0, N_CTRL - 1)
        out.append(np.asarray(a)[at].reshape(5, P, RC).transpose(1, 0, 2))
    return np.ascontiguousarray(np.stack(out, axis=1))


class SplineCoefficients:

    def __init__(self, nc, A, SCL, scratch, stack):
        def sb(name, shape, dt=F32):
            return stack.enter_context(nc.sbuf_tensor(name, shape, dt))

        self.A, self.SCL, self.scratch = A, SCL, scratch
        self.WIN = sb("WIN", [P, 3, 5, RC])
        self.COEF = sb("COEF", [P, 2, 2, 4, 4 * RC])
        self.TMP = sb("TMP", [P, 4, 4, RC])
        self.CF = sb("CF", [P, 6, 4, RC])
        self.PB = sb("PB", [P, 3, 6, 4, RC], BF16)
        self.MX = sb("MX", [P, 3])
        self.MXA = sb("MXA", [P, 3])
        self.SC = sb("SC", [P, 3])
        self.loaded, self.mx_ready, self.all_max, self.parts_ready, self.parts_stored, self.own = (
            nc.alloc_semaphore("k_" + n) for n in ("loaded", "mx", "all_max", "parts", "parts_stored", "own"))

    def load(self, sp):
        sp.dma_start(self.WIN[:, :, :, :], self.A["spline_windows"]).then_inc(self.loaded, 16)
        sp.dma_start(self.COEF[:, :, :, :, :],
                     self.A["spline_coefs"].rearrange("p (o q m f) -> p o q m f", o=2, q=2, m=4)).then_inc(self.loaded, 16)

    def store(self, sp):
        sp.wait_ge(self.parts_ready, 3)
        for part in range(3):
            sp.dma_start(self.scratch[part].rearrange("a m (p c) -> p (a m) c", p=P),
                         self.PB[:, part, :, :, :].rearrange("p a m c -> p (a m) c")).then_inc(self.parts_stored, 16)
        sp.wait_ge(self.parts_stored, 48)

    def largest(self, pool):
        pool.wait_ge(self.mx_ready, 1)
        pool.partition_all_reduce(self.MXA[:, :], self.MX[:, :], P, RMAX).then_inc(self.all_max, 1)

    def vector_steps(self, v):
        WIN, COEF, TMP, CF, PB, MX, MXA, SC, SCL = (
            self.WIN, self.COEF, self.TMP, self.CF, self.PB, self.MX, self.MXA, self.SC, self.SCL)
        own, parts_ready = Tally(v, self.own, 0, 0), self.parts_ready

        def step(ins):
            own.inc(ins)
            own.wait()

        v.wait_ge(self.loaded, 32)
        v.tensor_reduce(MX[:, :], WIN[:, :, :, :].rearrange("p t k c -> p t (k c)"), AX.X, ALU.max,
                        apply_absolute_value=True).then_inc(self.mx_ready, 1)
        for tp in range(6):
            t, piece = divmod(tp, 2)
            step(v.tensor_tensor(TMP[:, :, :, :].rearrange("p m k c -> p m (k c)"),
                                 WIN[:, t, piece:piece + 4, :].rearrange("p k c -> p (k c)").unsqueeze(1).to_broadcast([P, 4, 4 * RC]),
                                 COEF[:, t // 2, piece, :, :], ALU.mult))
            yield
            step(v.tensor_reduce(CF[:, tp, :, :], TMP[:, :, :, :].rearrange("p m k c -> p m c k"), AX.X, ALU.add))
            yield
        yield
        v.wait_ge(self.all_max, 1)
        step(v.tensor_scalar(MXA[:, :], MXA[:, :], 1e-30, None, ALU.max))
        step(v.tensor_scalar(SCL[:, :].bitcast(U32), MXA[:, :].bitcast(U32), 0x7F800000, None, ALU.bitwise_and))
        step(v.reciprocal(SC[:, :], SCL[:, :]))
        step(v.tensor_scalar(SC[:, :], SC[:, :], 8192.0, None, ALU.mult))
        for t in range(3):
            c = CF[:, 2 * t:2 * t + 2, :, :]
            step(v.tensor_scalar(c, c, SC[:, t:t + 1], None, ALU.mult))
        v.tensor_copy(PB[:, 0, :, :, :], CF[:, :, :, :]).then_inc(parts_ready, 1)
        v.wait_ge(parts_ready, 1)
        yield
        step(v.tensor_tensor(CF[:, :, :, :], CF[:, :, :, :], PB[:, 0, :, :, :], ALU.subtract))
        v.tensor_copy(PB[:, 1, :, :, :], CF[:, :, :, :]).then_inc(parts_ready, 1)
        v.wait_ge(parts_ready, 2)
        yield
        step(v.tensor_tensor(CF[:, :, :, :], CF[:, :, :, :], PB[:, 1, :, :, :], ALU.subtract))
        v.tensor_copy(PB[:, 2, :, :, :], CF[:, :, :, :]).then_inc(parts_ready, 1)

def spline_phase(nc, A, at_row, WH, WL, scratch, stack):
    def sb(name, shape, dt=F32):
        return stack.enter_context(nc.sbuf_tensor(name, shape, dt))

    sem = nc.alloc_semaphore
    PW = sb("PW", [24, P])
    PWB = sb("PWB", [24, P], BF16)
    RH = sb("RH", [24, 2, 2, QW], BF16)
    START = sb("START", [P, 2, QW])
    MK = sb("MK", [P, 2, QW], U8)
    WF = sb("WF", [P, 4, SUB])
    PS = [stack.enter_context(nc.psum_tensor(f"SP{i}", [P, SUB], F32)) for i in range(8)]
    loaded, pw_ready = sem("b_loaded"), sem("b_pw")
    rh_loaded = [sem("b_rh0"), sem("b_rh1")]
    pp_ready, wf_copied, wf_selected, wh_ready, wl_ready = (
        sem("b_" + n) for n in ("pp", "wf_copied", "wf_selected", "wh", "wl"))
    passed, mk_ready = sem("b_passed"), sem("b_mk")
    NS = RUNS // SUB
    SEL0 = 8

    with nc.Block() as block:
        @block.sync
        def _(sp):
            sp.dma_start(PW[:, :], A["spline_powers"]).then_inc(loaded, 16)
            with sp.Fori(0, 3) as t:
                for q in range(RUNS // QW):
                    cols = slice(q * QW, (q + 1) * QW)
                    sp.wait_ge(wf_selected, t * NS + 4 * q + SEL0 - 4)
                    for n, (part, _) in enumerate(PARTS):
                        sp.dma_start(RH[4 * n:4 * n + 4, q % 2, :, :],
                                     scratch[part, ds(2 * t, 2), :, cols].rearrange("a m c -> m a c")).then_inc(rh_loaded[q % 2], 16)
                    sp.dma_start(START[:, q % 2, :], A["spline_starts"][ds(t, 1), cols].to_broadcast([P, QW])).then_inc(rh_loaded[q % 2], 16)

        @block.scalar
        def _(act):
            with act.Fori(0, 3) as t:
                def high(n):
                    act.wait_ge(wf_selected, t * NS + n + 1 + SEL0)
                    nc.scalar.copy(WH[:, ds(t, 1), n * SUB:(n + 1) * SUB], WF[:, n % 4, :]).then_inc(wh_ready, 1)

                for n in range(NS):
                    act.wait_ge(pp_ready, t * NS + n + 1)
                    act.wait_ge(wl_ready, t * NS + n + 1)
                    nc.scalar.copy(WF[:, n % 4, :], PS[2 * (n % 4)][:, :]).then_inc(wf_copied, 1)
                    if n:
                        high(n - 1)
                high(NS - 1)

        @block.tensor
        def _(pe):
            pe.wait_ge(pw_ready, 1)
            with pe.Fori(0, 3) as t:
                for n in range(NS):
                    q = n // 4
                    if n % 4 == 0:
                        pe.wait_ge(rh_loaded[q % 2], t * (2 * 7 * 16) + (q // 2 + 1) * 7 * 16)
                    pe.wait_ge(wf_selected, t * NS + n - 3 + SEL0)
                    for piece in range(2):
                        last = pe.matmul(PS[2 * (n % 4) + piece][:, :], PWB[:, :],
                                         RH[:, q % 2, piece, (n % 4) * SUB:(n % 4 + 1) * SUB], start=True, stop=True)
                    last.then_inc(pp_ready, 1)

        @block.vector
        def _(v):
            v.wait_ge(loaded, 16)
            v.tensor_copy(PWB[:, :], PW[:, :]).then_inc(pw_ready, 1)
            v.sem_inc(wf_selected, SEL0)
            v.sem_inc(wl_ready, 4)
            with v.Fori(0, 3) as t:
                def low(n):
                    v.wait_ge(wh_ready, t * NS + n + 1)
                    v.tensor_tensor(WL[:, ds(t, 1), n * SUB:(n + 1) * SUB], WF[:, n % 4, :],
                                    WH[:, ds(t, 1), n * SUB:(n + 1) * SUB], ALU.subtract).then_inc(wl_ready, 1)

                for n in range(NS):
                    q = n // 4
                    if n % 4 == 0:
                        v.wait_ge(rh_loaded[q % 2], t * (2 * 7 * 16) + (q // 2 + 1) * 7 * 16)
                        v.tensor_scalar(MK[:, q % 2, :], START[:, q % 2, :], at_row, None, ALU.is_le).then_inc(mk_ready, 1)
                        v.wait_ge(mk_ready, t * 4 + q + 1)
                        v.sem_inc(passed, 1)
                    v.wait_ge(wf_copied, t * NS + n + 1)
                    v.sem_inc(passed, 1)
                    v.copy_predicated(WF[:, n % 4, :], MK[:, q % 2, (n % 4) * SUB:(n % 4 + 1) * SUB],
                                      PS[2 * (n % 4) + 1][:, :]).then_inc(wf_selected, 1)
                    if n:
                        low(n - 1)
                low(NS - 1)


XS = 1024.0


def ffn0_phase(nc, A, X, tg, idf, WH, WL, SCL, stack):
    def sb(name, shape, dt=F32):
        return stack.enter_context(nc.sbuf_tensor(name, shape, dt))

    sem = nc.alloc_semaphore
    XN = sb("XN0", [P, NC, D])
    XH = sb("XH0", [P, KD, S], F16)
    XL = sb("XL0", [P, KD, S], F16)
    HH = sb("HH0", [P, KI, S], F16)
    HL = sb("HL0", [P, KI, S], F16)
    SG = sb("SG0", [P, 2, S])
    HM = sb("HM0", [P, 2, S])
    ST = sb("ST0", [P, NC, 6])
    MV = sb("MV0", [P, NC, 2])
    SD = sb("SD0", [P, NC])
    RS = sb("RS0", [P, NC])
    EPS = sb("EPS0", [P, 1])
    DS = sb("DS0", [P, 4])
    T, G, U, DN = ([stack.enter_context(nc.psum_tensor(f"F{n}{i}", [P, 512], F32)) for i in range(2)] for n in "TGUD")
    (mv_ready, sd_ready, xn_ready, t_ready, xh_ready, xl_ready, gu_ready, sg_ready, hm_ready, hh_ready, hl_ready,
     dn_ready, x_added, ds_ready, own_sem) = (sem("c_" + n) for n in (
         "mv", "sd", "xn", "t", "xh", "xl", "gu", "sg", "hm", "hh", "hl", "dn", "x_added", "ds", "own"))
    passed, pe_passed = sem("c_passed"), sem("c_pe_passed")

    with nc.Block() as block:
        @block.scalar
        def _(act):
            def norm(b):
                act.wait_ge(mv_ready, b + 1)
                nc.scalar.activation(SD[:, :], MV[:, :, 1], ACT.Sqrt, bias=EPS[:, 0:1]).then_inc(sd_ready, 1)

            def high(b):
                for k in range(KD):
                    act.wait_ge(t_ready, b * KD + k + 1)
                    nc.scalar.activation(XH[:, k, :], T[k % 2][:, :], ACT.Copy, scale=XS).then_inc(xh_ready, 1)

            def batch(b, more):
                with act.Fori(0, KI // 2) as u:
                    for w in range(2):
                        act.wait_ge(gu_ready, b * KI + 2 * u + w + 1)
                        act.wait_ge(hm_ready, b * KI + 2 * u + w + 1)
                        nc.scalar.activation(SG[:, w, :], G[w][:, :], ACT.Silu, scale=DS[:, 0:1]).then_inc(sg_ready, 1)
                    for w in range(2):
                        act.wait_ge(hm_ready, b * KI + 2 * u + w + 3)
                        nc.scalar.copy(HH[:, ds(2 * u + w, 1), :], HM[:, w, :]).then_inc(hh_ready, 1)
                if more:
                    norm(b + 1)
                    high(b + 1)

            act.wait_ge(ds_ready, 6)
            norm(0)
            high(0)
            with act.Fori(0, B - 1) as b:
                batch(b, True)
            batch(B - 1, False)

        @block.tensor
        def _(pe):
            def transposes(b):
                for k in range(KD):
                    pe.wait_ge(xl_ready, b * KD + k + 1)
                    if k == 0:
                        pe.wait_ge(xn_ready, b * NC + NC)
                    for c in range(NC):
                        last = pe.transpose(T[k % 2][:, c * P:(c + 1) * P], XN[:, c, k * P:(k + 1) * P], idf)
                    last.then_inc(t_ready, 1)

            def down(b, u):
                for w in range(2):
                    pe.wait_ge(x_added, b * NC + 2 * u + w + 1)
                    c = 2 * u + w
                    n = 0
                    for i in range(KI):
                        for lhs, rhs in ((HH, WH), (HH, WL), (HL, WH)):
                            n += 1
                            last = pe.matmul(DN[w][:, :], lhs[:, i, c * P:(c + 1) * P], rhs[:, 2, i * D:(i + 1) * D],
                                             start=(n == 1), stop=(n == 3 * KI))
                    last.then_inc(dn_ready, 1)

            def batch(b, more):
                pe.wait_ge(xl_ready, b * KD + KD + 2)
                pe.sem_inc(pe_passed, 1)
                with pe.Fori(0, KI // 2) as u:
                    for w in range(2):
                        pe.wait_ge(hm_ready, b * KI + 2 * u + w + 1)
                        for t, bank in ((0, G[w]), (1, U[w])):
                            n = 0
                            for k in range(KD):
                                cols = ds(u * (2 * P) + (k * INTER + w * P), P)
                                for lhs, rhs in ((WH, XH), (WH, XL), (WL, XH)):
                                    n += 1
                                    last = pe.matmul(bank[:, :], lhs[:, t, cols], rhs[:, k, :],
                                                     start=(n == 1), stop=(n == 3 * KD))
                        last.then_inc(gu_ready, 1)
                pe.wait_ge(hl_ready, b * KI + KI + 2)
                pe.sem_inc(pe_passed, 1)
                down(b, 0)
                if more:
                    transposes(b + 1)
                down(b, 1)

            transposes(0)
            with pe.Fori(0, B - 1) as b:
                batch(b, True)
            batch(B - 1, False)

        @block.vector
        def _(v):
            n_own = [0]

            def step(ins):
                n_own[0] += 1
                ins.then_inc(ds_ready, 1)
                v.wait_ge(ds_ready, n_own[0])

            step(v.memset(EPS[:, :], 1e-5))
            step(v.tensor_scalar(DS[:, 0:1], SCL[:, 0:1], 2.0 ** -23, None, ALU.mult))
            step(v.reciprocal(DS[:, 1:2], SCL[:, 0:1]))
            step(v.tensor_scalar(DS[:, 1:2], DS[:, 1:2], 2.0 ** -29, None, ALU.mult))
            step(v.tensor_scalar(DS[:, 2:3], SCL[:, 0:1], SCL[:, 1:2], SCL[:, 2:3], ALU.mult, ALU.mult))
            step(v.tensor_scalar(DS[:, 2:3], DS[:, 2:3], tg[:, 2:3], 2.0 ** -7, ALU.mult, ALU.mult))
            v.sem_inc(xl_ready, 2)
            v.sem_inc(hm_ready, 2)
            v.sem_inc(hl_ready, 2)
            v.sem_inc(x_added, 2)

            def norm(b):
                for c in range(NC):
                    v.bn_stats(ST[:, c, :], X[:, ds(b * NC + c, 1), :]).then_inc(own_sem, 1)
                v.wait_ge(own_sem, b * (2 * NC) + NC)
                v.sem_inc(passed, 1)
                for c in range(NC):
                    v.bn_aggr(MV[:, c, :], ST[:, c, :]).then_inc(*((own_sem, 1) if c < NC - 1 else (mv_ready, 1)))
                v.wait_ge(sd_ready, b + 1)
                v.reciprocal(RS[:, :], SD[:, :]).then_inc(own_sem, 1)
                v.wait_ge(own_sem, b * (2 * NC) + 2 * NC)
                for c in range(NC):
                    v.tensor_scalar(XN[:, c, :], X[:, ds(b * NC + c, 1), :], MV[:, c, 0:1], RS[:, c:c + 1],
                                    ALU.subtract, ALU.mult).then_inc(xn_ready, 1)

            def low(b):
                for k in range(KD):
                    v.wait_ge(xh_ready, b * KD + k + 1)
                    v.scalar_tensor_tensor(out=XL[:, k, :], in0=T[k % 2][:, :], scalar=XS, in1=XH[:, k, :],
                                           op0=ALU.mult, op1=ALU.subtract).then_inc(xl_ready, 1)

            def add(b, u):
                for w in range(2):
                    c = 2 * u + w
                    v.wait_ge(dn_ready, b * NC + c + 1)
                    x = X[:, ds(b * NC + c, 1), :]
                    v.scalar_tensor_tensor(out=x, in0=DN[w][:, :], scalar=DS[:, 2:3], in1=x,
                                           op0=ALU.mult, op1=ALU.add).then_inc(x_added, 1)

            def batch(b, more):
                with v.Fori(0, KI // 2) as u:
                    for w in range(2):
                        v.wait_ge(sg_ready, b * KI + 2 * u + w + 1)
                        v.wait_ge(hl_ready, b * KI + 2 * u + w + 1)
                        v.scalar_tensor_tensor(out=HM[:, w, :], in0=U[w][:, :], scalar=DS[:, 1:2], in1=SG[:, w, :],
                                               op0=ALU.mult, op1=ALU.mult).then_inc(hm_ready, 1)
                    for w in range(2):
                        v.wait_ge(hh_ready, b * KI + 2 * u + w + 1)
                        v.tensor_tensor(HL[:, ds(2 * u + w, 1), :], HM[:, w, :], HH[:, ds(2 * u + w, 1), :],
                                        ALU.subtract).then_inc(hl_ready, 1)
                if more:
                    norm(b + 1)
                add(b, 0)
                if more:
                    low(b + 1)
                add(b, 1)

            norm(0)
            low(0)
            with v.Fori(0, B - 1) as b:
                batch(b, True)
            batch(B - 1, False)


AH, AC = 8, 64
UNITS = AH * NC


def attention_phase(nc, A, X, tg, idf, stack):
    def sb(name, shape, dt=F32):
        return stack.enter_context(nc.sbuf_tensor(name, shape, dt))

    sem = nc.alloc_semaphore
    XN = sb("XN2", [P, NC, S])
    CTX = sb("CTX2", [P, NC, S])
    QH = sb("QH2", [P, NC, S], F16)
    QL = sb("QL2", [P, NC, S], F16)
    KH = sb("KH2", [P, NC, 2, S], F16)
    KL = sb("KL2", [P, NC, 2, S], F16)
    VH = sb("VH2", [P, NC, D], F16)
    VL = sb("VL2", [P, NC, D], F16)
    PR = sb("PR2", [P, 2, S])
    PH = sb("PH2", [P, 3, S], F16)
    PL = sb("PL2", [P, 3, S], F16)
    OT = sb("OT2", [P, NC, D])
    NM = sb("NM2", [P, 2, UNITS])
    SM = sb("SM2", [P, UNITS])
    RC_ = sb("RC2", [P, UNITS])
    ST = sb("ST2", [P, NC, 6])
    MV = sb("MV2", [P, NC, 2])
    SD = sb("SD2", [P, NC])
    RS = sb("RS2", [P, NC])
    EPS = sb("EPS2", [P, 1])
    CM = sb("CM2", [P, 8])
    SB = [stack.enter_context(nc.psum_tensor(f"A_S{i}", [P, 512], F32)) for i in range(3)]
    PB = [stack.enter_context(nc.psum_tensor(f"A_P{i}", [P, 512], F32)) for i in range(2)]
    OB = [stack.enter_context(nc.psum_tensor(f"A_O{i}", [P, 512], F32)) for i in range(2)]
    TB = stack.enter_context(nc.psum_tensor("A_T", [P, 512], F32))
    (ctx_loaded, mv_ready, sd_ready, xn_ready, t_ready, t_taken, s_ready, max_ready, p_ready, pt_ready, ph_ready,
     pl_ready, o_ready, ot_ready, own_sem, passed, pre_ready, cm_ready, cm_all, cs_ready, vh_ready,
     vl_ready, kh_ready, kl_ready, qh_ready, ql_ready, rc_ready) = (sem("d_" + n) for n in (
         "ctx", "mv", "sd", "xn", "t", "t_taken", "s", "max", "p", "pt", "ph", "pl", "o", "ot", "own", "passed", "pre", "cm", "cm_all", "cs", "vh", "vl", "kh", "kl", "qh", "ql", "rc"))
    NT = 2 * NC
    TT = 1 + NC
    OWN = 2 * NC + 6 + UNITS
    ctx = A["ctx_2048"].rearrange("b (c p) d -> b p c d", p=P)
    half = [slice(0, AC), slice(AC, P)]

    with nc.Block() as block:
        @block.sync
        def _(sp):
            sp.dma_start(CTX[:, :, :], ctx[0]).then_inc(ctx_loaded, 16)
            with sp.Fori(1, B) as b:
                sp.wait_ge(t_ready, b * NT + (NC - NT))
                sp.sem_inc(passed, 1)
                sp.wait_ge(kl_ready, b * 2)
                sp.sem_inc(passed, 1)
                sp.wait_ge(kh_ready, b * 2)
                sp.sem_inc(passed, 1)
                sp.dma_start(CTX[:, :, :], ctx[ds(b, 1)].rearrange("a p c d -> p (a c) d")).then_inc(ctx_loaded, 16)

        @block.gpsimd
        def _(pool):
            pool.memset(KH[:, :, :, :], 0.0).then_inc(pre_ready, 1)
            pool.memset(KL[:, :, :, :], 0.0).then_inc(pre_ready, 1)
            with pool.Fori(0, B) as b:
                pool.wait_ge(cm_ready, b + 1)
                pool.sem_inc(passed, 1)
                pool.partition_all_reduce(CM[:, 1:2], CM[:, 0:1], P, RMAX).then_inc(cm_all, 1)

        @block.scalar
        def _(act):
            act.wait_ge(pre_ready, 3)
            with act.Fori(0, B) as b:
                act.wait_ge(mv_ready, b + 1)
                nc.scalar.activation(SD[:, :], MV[:, :, 1], ACT.Sqrt, bias=EPS[:, 0:1]).then_inc(sd_ready, 1)
                act.wait_ge(cs_ready, b + 1)
                for par in range(2):
                    nc.scalar.activation(KH[half[par], :, par, :], CTX[half[par], :, :], ACT.Copy,
                                         scale=CM[half[par], 4:5]).then_inc(kh_ready, 1)
                act.wait_ge(xn_ready, b * NC + NC)
                nc.scalar.copy(QH[:, :, :], XN[:, :, :]).then_inc(qh_ready, 1)
                for k in range(NC):
                    act.wait_ge(t_ready, b * NT + k + 1)
                    nc.scalar.activation(VH[:, k, :], (SB + [TB])[k][:, :], ACT.Copy, scale=CM[:, 4:5]).then_inc(vh_ready, 1)

                def high(u):
                    act.wait_ge(pt_ready, b * UNITS + u + 1)
                    nc.scalar.activation(PH[:, u % 3, :], PB[u % 2][:, :], ACT.Copy, scale=XS).then_inc(ph_ready, 1)

                def scale(u):
                    h, q = divmod(u, NC)
                    act.wait_ge(o_ready, b * UNITS + u + 1)
                    act.wait_ge(rc_ready, b * UNITS + u + 1)
                    nc.scalar.activation(OT[:, q, h * AC:(h + 1) * AC], OB[u % 2][:, 0:AC], ACT.Copy,
                                         scale=RC_[:, u:u + 1]).then_inc(ot_ready, 1)

                for u in range(UNITS):
                    act.wait_ge(max_ready, b * UNITS + u + 1)
                    if u >= 2:
                        act.wait_ge(pt_ready, b * UNITS + u - 1)
                    nc.scalar.activation(PR[:, u % 2, :], SB[u % 3][:, :], ACT.Exp, bias=NM[:, 1, u:u + 1],
                                         scale=CM[:, 5:6], accum_out=SM[:, u:u + 1]).then_inc(p_ready, 1)
                    if u >= 1:
                        high(u - 1)
                    if u >= 3:
                        scale(u - 3)
                high(UNITS - 1)
                for u in range(UNITS - 3, UNITS):
                    scale(u)

        @block.tensor
        def _(pe):
            with pe.Fori(0, B) as b:
                def scores(u):
                    h, q = divmod(u, NC)
                    c, par = divmod(h, 2)
                    if u >= 3:
                        pe.wait_ge(p_ready, b * UNITS + u - 2)
                    cols = slice(q * P, (q + 1) * P)
                    for i, (lhs, rhs) in enumerate(((QH, KH), (QH, KL), (QL, KH))):
                        last = pe.matmul(SB[u % 3][:, :], lhs[:, c, cols], rhs[:, c, par, :], start=(i == 0), stop=(i == 2))
                    last.then_inc(s_ready, 1)

                def turn(u):
                    pe.wait_ge(p_ready, b * UNITS + u + 1)
                    if u >= 2:
                        pe.wait_ge(pl_ready, b * UNITS + u - 1)
                    for k in range(NC):
                        last = pe.transpose(PB[u % 2][:, k * P:(k + 1) * P], PR[:, u % 2, k * P:(k + 1) * P], idf)
                    last.then_inc(pt_ready, 1)

                def weigh(u):
                    h = u // NC
                    pe.wait_ge(pl_ready, b * UNITS + u + 1)
                    if u >= 2:
                        pe.wait_ge(ot_ready, b * UNITS + u - 1)
                    n = 0
                    for k in range(NC):
                        for lhs, rhs in ((PH, VH), (PH, VL), (PL, VH)):
                            n += 1
                            last = pe.matmul(OB[u % 2][:, 0:AC], lhs[:, u % 3, k * P:(k + 1) * P],
                                             rhs[:, k, h * AC:(h + 1) * AC], start=(n == 1), stop=(n == 3 * NC))
                    last.then_inc(o_ready, 1)

                def back(c):
                    pe.wait_ge(ot_ready, b * UNITS + (c + 1) * 2 * NC)
                    pe.wait_ge(t_taken, b * TT + c + 2)
                    for k in range(NC):
                        last = pe.transpose(TB[:, k * P:(k + 1) * P], OT[:, k, c * P:(c + 1) * P], idf)
                    last.then_inc(t_ready, 1)

                pe.wait_ge(ctx_loaded, b * 16 + 16)
                for k in range(NC):
                    if k == NC - 1:
                        pe.wait_ge(t_taken, b * TT + 1)
                    for c in range(NC):
                        last = pe.transpose((SB + [TB])[k][:, c * P:(c + 1) * P], CTX[:, c, k * P:(k + 1) * P], idf)
                    last.then_inc(t_ready, 1)
                pe.wait_ge(kh_ready, b * 2 + 2)
                pe.wait_ge(kl_ready, b * 2 + 2)
                pe.wait_ge(ql_ready, b + 1)
                pe.wait_ge(vl_ready, b * (NC - 1) + NC - 1)
                pe.wait_ge(t_taken, b * TT + 2)
                scores(0)
                scores(1)
                for u in range(UNITS + 5):
                    if u + 2 < UNITS:
                        scores(u + 2)
                    if u < UNITS:
                        turn(u)
                    if 2 <= u < UNITS + 2:
                        weigh(u - 2)
                    if u >= 2 * NC + 4 and (u - 4) % (2 * NC) == 0:
                        back((u - 4) // (2 * NC) - 1)

        @block.vector
        def _(v):
            v.memset(EPS[:, :], 1e-5).then_inc(pre_ready, 1)
            v.sem_inc(t_taken, 1)
            v.wait_ge(pre_ready, 3)
            with v.Fori(0, B) as b:
                own = Tally(v, own_sem, b, OWN)
                v.wait_ge(ctx_loaded, b * 16 + 16)
                v.tensor_reduce(CM[:, 0:1], CTX[:, :, :].rearrange("p c d -> p (c d)"), AX.X, ALU.max,
                                apply_absolute_value=True).then_inc(cm_ready, 1)
                for c in range(NC):
                    own.inc(v.bn_stats(ST[:, c, :], X[:, ds(b * NC + c, 1), :]))
                own.wait()
                v.sem_inc(passed, 1)
                for c in range(NC):
                    ins = v.bn_aggr(MV[:, c, :], ST[:, c, :])
                    if c < NC - 1:
                        own.inc(ins)
                ins.then_inc(mv_ready, 1)
                v.wait_ge(cm_all, b + 1)
                own.inc(v.tensor_scalar(CM[:, 1:2], CM[:, 1:2], 1e-30, None, ALU.max))
                own.wait()
                own.inc(v.tensor_scalar(CM[:, 2:3].bitcast(U32), CM[:, 1:2].bitcast(U32), 0x7F800000, None, ALU.bitwise_and))
                own.wait()
                own.inc(v.reciprocal(CM[:, 3:4], CM[:, 2:3]))
                own.wait()
                own.inc(v.tensor_scalar(CM[:, 5:6], CM[:, 2:3], 2.0 ** -23 / AC, None, ALU.mult))
                own.inc(v.tensor_scalar(CM[:, 6:7], CM[:, 2:3], tg[:, 1:2], 2.0 ** -23, ALU.mult, ALU.mult))
                v.tensor_scalar(CM[:, 4:5], CM[:, 3:4], 8192.0, None, ALU.mult).then_inc(cs_ready, 1)
                v.wait_ge(sd_ready, b + 1)
                own.inc(v.reciprocal(RS[:, :], SD[:, :]))
                own.wait()
                own.inc(v.tensor_scalar(RS[:, :], RS[:, :], XS, None, ALU.mult))
                own.wait()
                for c in range(NC):
                    v.tensor_scalar(XN[:, c, :], X[:, ds(b * NC + c, 1), :], MV[:, c, 0:1], RS[:, c:c + 1],
                                    ALU.subtract, ALU.mult).then_inc(xn_ready, 1)
                v.wait_ge(cs_ready, b + 1)
                for par in range(2):
                    v.wait_ge(kh_ready, b * 2 + par + 1)
                    v.scalar_tensor_tensor(out=KL[half[par], :, par, :], in0=CTX[half[par], :, :], scalar=CM[half[par], 4:5],
                                           in1=KH[half[par], :, par, :], op0=ALU.mult, op1=ALU.subtract).then_inc(kl_ready, 1)
                v.wait_ge(qh_ready, b + 1)
                v.wait_ge(xn_ready, b * NC + NC)
                v.tensor_tensor(QL[:, :, :], XN[:, :, :], QH[:, :, :], ALU.subtract).then_inc(ql_ready, 1)
                for k in range(NC):
                    v.wait_ge(vh_ready, b * NC + k + 1)
                    v.scalar_tensor_tensor(out=VL[:, k, :], in0=(SB + [TB])[k][:, :], scalar=CM[:, 4:5], in1=VH[:, k, :],
                                           op0=ALU.mult, op1=ALU.subtract).then_inc(vl_ready if k < NC - 1 else t_taken, 1)

                def top(u):
                    v.wait_ge(s_ready, b * UNITS + u + 1)
                    own.inc(v.tensor_reduce(NM[:, 0, u:u + 1], SB[u % 3][:, :], AX.X, ALU.max, negate=True))
                    own.wait()
                    v.tensor_scalar(NM[:, 1, u:u + 1], NM[:, 0, u:u + 1], CM[:, 5:6], None, ALU.mult).then_inc(max_ready, 1)

                def low(u):
                    v.wait_ge(ph_ready, b * UNITS + u + 1)
                    v.scalar_tensor_tensor(out=PL[:, u % 3, :], in0=PB[u % 2][:, :], scalar=XS, in1=PH[:, u % 3, :],
                                           op0=ALU.mult, op1=ALU.subtract).then_inc(pl_ready, 1)

                def over_sum(u):
                    v.wait_ge(p_ready, b * UNITS + u + 1)
                    v.reciprocal(RC_[:, u:u + 1], SM[:, u:u + 1]).then_inc(rc_ready, 1)

                def add(c):
                    v.wait_ge(t_ready, b * NT + NC + c + 1)
                    x = X[:, ds(b * NC + c, 1), :]
                    v.scalar_tensor_tensor(out=x, in0=TB[:, :], scalar=CM[:, 6:7], in1=x,
                                           op0=ALU.mult, op1=ALU.add).then_inc(t_taken, 1)

                top(0)
                for u in range(UNITS + 6):
                    if u + 1 < UNITS:
                        top(u + 1)
                    if 1 <= u <= UNITS:
                        low(u - 1)
                    if u < UNITS:
                        over_sum(u)
                    if u >= 2 * NC + 5 and (u - 5) % (2 * NC) == 0:
                        add((u - 5) // (2 * NC) - 1)
                v.wait_ge(t_taken, b * TT + TT + 1)
                v.sem_inc(passed, 1)
                own.done()


BLK = 32
GW = 4 * 512


def rounded(v, own, src, val, mag, inv, nb):
    blocks = lambda a: a.rearrange("p (n k) -> p n k", k=BLK)
    wide = lambda a: a.unsqueeze(2).to_broadcast([P, nb, BLK])
    own.inc(v.tensor_tensor(blocks(val), blocks(src), wide(inv), ALU.mult))
    own.wait()
    yield
    own.inc(v.tensor_scalar(mag.bitcast(U32), val.bitcast(U32), 0x7F800000, None, ALU.bitwise_and))
    own.wait()
    own.inc(v.tensor_scalar(mag, mag, 2.0 ** -6, 1.5 * 2.0 ** 20, ALU.max, ALU.mult))
    own.wait()
    yield
    own.inc(v.tensor_tensor(val, val, mag, ALU.add))
    own.wait()
    own.inc(v.tensor_tensor(val, val, mag, ALU.subtract))
    own.wait()


def quantise(v, own, src, val, mag, inv, scale, nb):
    yield from rounded(v, own, src, val, mag, inv, nb)
    yield
    blocks = val.rearrange("p (n k) -> p n k", k=BLK)
    own.inc(v.tensor_tensor(blocks, blocks, scale.unsqueeze(2).to_broadcast([P, nb, BLK]), ALU.mult))
    own.wait()


def weights_phase(nc, A, WH, WL, SCL, idh, stack):
    def sb(name, shape, dt=F32):
        return stack.enter_context(nc.sbuf_tensor(name, shape, dt))

    sem = nc.alloc_semaphore
    RAW = sb("RAW", [P, KI, D])
    VAL = sb("VALW", [P, 2, GW])
    MAG = sb("MAGW", [P, GW])
    QH = sb("QHW", [P, 2, GW], F16)
    QL = sb("QLW", [P, 2, GW], F16)
    AM = sb("AMW", [P, 2, 4, GW // BLK])
    IV = sb("IVW", [P, 4, GW // BLK])
    MX = sb("MXW", [P, 1])
    MXA = sb("MXAW", [P, 1])
    SC = sb("SCW", [P, 1])
    TH, TL = ([stack.enter_context(nc.psum_tensor(f"W_{n}{i}", [P, 2, NC, P], F16)) for i in range(4)] for n in "HL")
    raw_loaded = [sem(f"e_raw{g}") for g in range(4)]
    raw_used, mx_ready, all_max, rounded_ready, scale_ready, val_ready, qh_ready, ql_ready, tw_ready, tw_taken, own_sem = (
        sem("e_" + n) for n in ("raw_used", "mx", "all_max", "rounded", "scale", "val", "qh", "ql", "tw", "tw_taken", "own"))
    names = ("L1_ffn_gate_w", "L1_ffn_up_w", "L1_ffn_down_w")

    def dest(W, t, g, j):
        if t < 2:
            return W[:, t, :].rearrange("p (k i) -> p k i", k=KD)[:, :, (4 * g + j) * P:(4 * g + j + 1) * P]
        return W[:, t, :].rearrange("p (i h) -> p i h", i=KI)[:, 4 * j:4 * j + 4, g * P:(g + 1) * P]

    with nc.Block() as block:
        @block.sync
        def _(sp):
            for t, name in enumerate(names):
                w = (A[name].rearrange("(g n p) h -> p g n h", p=P, g=4) if t < 2
                     else A[name].rearrange("(g p) (n h) -> p g n h", p=P, h=D))
                for g in range(4):
                    if t:
                        sp.wait_ge(raw_used, 4 * (t - 1) + g + 1)
                    sp.dma_start(RAW[:, 4 * g:4 * g + 4, :], w[:, g, :, :]).then_inc(raw_loaded[g], 16)

        @block.gpsimd
        def _(pool):
            for t in range(3):
                pool.wait_ge(mx_ready, t + 1)
                pool.partition_all_reduce(MXA[:, :], MX[:, :], P, RMAX).then_inc(all_max, 1)
                pool.wait_ge(scale_ready, t + 1)
                for g in range(4):
                    n = 4 * t + g
                    val = VAL[:, n % 2, :]
                    blocks = val.rearrange("p (n k) -> p n k", k=BLK)
                    pool.wait_ge(rounded_ready, n + 1)
                    pool.tensor_tensor(blocks, blocks, AM[:, t % 2, g, :].unsqueeze(2).to_broadcast([P, GW // BLK, BLK]),
                                       ALU.mult).then_inc(val_ready, 1)
                    pool.wait_ge(qh_ready, n + 1)
                    pool.tensor_tensor(QL[:, n % 2, :], val, QH[:, n % 2, :], ALU.subtract).then_inc(ql_ready, 1)

        @block.scalar
        def _(act):
            def take(n):
                for j in range(4):
                    act.wait_ge(tw_ready, 4 * n + j + 1)
                    nc.scalar.copy(dest(WH, n // 4, n % 4, j), TH[j][:, 0, :, :])
                    nc.scalar.copy(dest(WL, n // 4, n % 4, j), TL[j][:, 0, :, :]).then_inc(tw_taken, 1)

            for n in range(12):
                act.wait_ge(val_ready, n + 1)
                if n >= 2:
                    act.wait_ge(tw_ready, 4 * (n - 1))
                nc.scalar.copy(QH[:, n % 2, :], VAL[:, n % 2, :]).then_inc(qh_ready, 1)
                if n:
                    take(n - 1)
            take(11)

        @block.tensor
        def _(pe):
            for n in range(12):
                pe.wait_ge(qh_ready, n + 1)
                pe.wait_ge(ql_ready, n + 1)
                for j in range(4):
                    if n:
                        pe.wait_ge(tw_taken, 4 * (n - 1) + j + 1)
                    for bank, q in ((TH[j], QH), (TL[j], QL)):
                        for k in range(NC):
                            last = pe.transpose(bank[:, 0, k, :], q[:, n % 2, j * D + k * P:j * D + (k + 1) * P], idh)
                    last.then_inc(tw_ready, 1)

        @block.vector
        def _(v):
            own = Tally(v, own_sem, 0, W_OWN)

            def step(ins):
                own.inc(ins)
                own.wait()

            for t in range(3):
                for g in range(4):
                    v.wait_ge(raw_loaded[g], 16 * (t + 1))
                    step(v.tensor_reduce(AM[:, t % 2, g, :], RAW[:, 4 * g:4 * g + 4, :].rearrange("p n (m k) -> p (n m) k", k=BLK),
                                         AX.X, ALU.max, apply_absolute_value=True))
                am = AM[:, t % 2, :, :].rearrange("p g m -> p (g m)")
                iv = IV[:, :, :].rearrange("p g m -> p (g m)")
                v.tensor_reduce(MX[:, :], am, AX.X, ALU.max).then_inc(mx_ready, 1)
                step(v.tensor_scalar(am, am, 1.0 / 448.0, 1e-30, ALU.mult, ALU.max))
                step(v.reciprocal(iv, am))
                for g in range(4):
                    n = 4 * t + g
                    if n >= 2:
                        v.wait_ge(ql_ready, n - 1)
                    for i, _ in enumerate(rounded(v, own, RAW[:, 4 * g:4 * g + 4, :].rearrange("p n h -> p (n h)"),
                                                  VAL[:, n % 2, :], MAG[:, :], IV[:, g, :], GW // BLK)):
                        if i == 0:
                            v.sem_inc(raw_used, 1)
                    v.sem_inc(rounded_ready, 1)
                    if g == 0:
                        v.wait_ge(all_max, t + 1)
                        step(v.tensor_scalar(MXA[:, :], MXA[:, :], 1e-30, None, ALU.max))
                        step(v.tensor_scalar(SCL[:, t:t + 1].bitcast(U32), MXA[:, :].bitcast(U32), 0x7F800000, None, ALU.bitwise_and))
                        step(v.reciprocal(SC[:, :], SCL[:, t:t + 1]))
                        step(v.tensor_scalar(SC[:, :], SC[:, :], 8192.0, None, ALU.mult))
                        step(v.tensor_scalar(am, am, SC[:, 0:1], None, ALU.mult))
                        v.sem_inc(scale_ready, 1)
            own.done()


W_OWN = 93


def ffn1_phase(nc, A, X, tg, idh, WH, WL, SCL, orr, stored, stack):
    def sb(name, shape, dt=F32):
        return stack.enter_context(nc.sbuf_tensor(name, shape, dt))

    sem = nc.alloc_semaphore
    XN = sb("XN3", [P, D])
    XV = sb("XV3", [P, D])
    XM = sb("XM3", [P, D])
    XQ = sb("XQ3", [P, 2, D], F16)
    XT = sb("XT3", [P, 2, KD, P], F16)
    H = sb("H3", [P, INTER])
    V = sb("V3", [P, INTER])
    M = sb("M3", [P, INTER])
    HQ = sb("HQ3", [P, 2, INTER], F16)
    HT = sb("HT3", [P, 4, 2, 4, P], F16)
    SG = sb("SG3", [P, 2, 512])
    XA = sb("XA3", [P, D // BLK])
    XI = sb("XI3", [P, D // BLK])
    HA = sb("HA3", [P, INTER // BLK])
    HI = sb("HI3", [P, INTER // BLK])
    HX = sb("HX3", [P, 4])
    RSC = sb("RSC3", [P, 1])
    ST = sb("ST3", [P, 6])
    MV = sb("MV3", [P, 2])
    SD = sb("SD3", [P, 1])
    EPS = sb("EPS3", [P, 1])
    DS = sb("DS3", [P, 4])
    G, U, DN = ([stack.enter_context(nc.psum_tensor(f"H{n}{i}", [P, 512], F32)) for i in range(2)] for n in "GUD")
    T = [stack.enter_context(nc.psum_tensor(f"HT{i}", [P, 2, 4, P], F16)) for i in range(2)]
    (mv_ready, sd_ready, xv_ready, xh_ready, xl_ready, xt_ready, xt_taken, gu_ready, sg_ready, h_ready, hv_ready,
     hh_ready, hl_ready, ht_ready, ht_taken, dn_ready, x_added, ds_ready, x_own, s_own, h_own) = (sem("f_" + n) for n in (
         "mv", "sd", "xv", "xh", "xl", "xt", "xt_taken", "gu", "sg", "h", "hv", "hh", "hl", "ht", "ht_taken", "dn",
         "x_added", "ds", "x_own", "s_own", "h_own"))
    passed, passed_sp = sem("f_passed"), sem("f_passed_sp")
    IC = INTER // 512

    with nc.Block() as block:
        @block.sync
        def _(sp):
            with sp.Fori(0, TILES) as tt:
                sp.wait_ge(x_added, tt + 2)
                sp.sem_inc(passed_sp, 1)
                sp.dma_start(orr[:, ds(tt, 1), :], X[:, ds(tt, 1), :]).then_inc(stored, 16)
            sp.wait_ge(stored, 16 * TILES)

        @block.scalar
        def _(act):
            def deviation(tt):
                act.wait_ge(mv_ready, tt + 1)
                nc.scalar.activation(SD[:, :], MV[:, 1:2], ACT.Sqrt, bias=EPS[:, 0:1]).then_inc(sd_ready, 1)

            def prepare(tt):
                act.wait_ge(xv_ready, tt + 1)
                nc.scalar.copy(XQ[:, 0, :], XV[:, :]).then_inc(xh_ready, 1)

            def stage(tt, gate_up=True, quant=True, down=True, more=True):
                if gate_up:
                    act.wait_ge(xt_ready, tt + 1)
                    nc.scalar.copy(XT[:, :, :, :], T[0][:, :, :, :]).then_inc(xt_taken, 1)
                    if more:
                        deviation(tt + 1)

                def silu(i):
                    if gate_up:
                        act.wait_ge(gu_ready, tt * IC + i + 1)
                        act.wait_ge(h_ready, tt * IC + i + 1)
                        nc.scalar.activation(SG[:, i % 2, :], G[i % 2][:, :], ACT.Silu, scale=DS[:, 0:1]).then_inc(sg_ready, 1)

                silu(0)
                if down:
                    for q in range(4):
                        act.wait_ge(ht_ready, (tt - 2) * 4 + q + 1)
                        nc.scalar.copy(HT[:, q, :, :, :], T[q % 2][:, :, :, :]).then_inc(ht_taken, 1)
                if quant:
                    act.wait_ge(hv_ready, tt)
                    nc.scalar.copy(HQ[:, 0, :], V[:, :]).then_inc(hh_ready, 1)
                silu(1)
                if gate_up and more:
                    prepare(tt + 1)
                silu(2)
                silu(3)

            act.wait_ge(ds_ready, N_DS)
            deviation(0)
            prepare(0)
            stage(0, quant=False, down=False)
            stage(1, down=False)
            with act.Fori(2, TILES - 1) as tt:
                stage(tt)
            stage(TILES - 1, more=False)
            stage(TILES, gate_up=False)
            stage(TILES + 1, gate_up=False, quant=False)

        @block.tensor
        def _(pe):
            def products(bank, terms):
                for i, (lhs, rhs) in enumerate(terms):
                    ins = pe.matmul(bank[:, :], lhs, rhs, start=(i == 0), stop=(i == len(terms) - 1))
                return ins

            def gate_up_products(tt, i):
                pe.wait_ge(h_ready, tt * IC + i + 1)
                for t, bank in ((0, G[i % 2]), (1, U[i % 2])):
                    ins = products(bank, [(XT[:, lp, k, :], W[:, t, k * INTER + i * 512:k * INTER + (i + 1) * 512])
                                          for k in range(KD) for lp, W in ((0, WH), (0, WL), (1, WH))])
                ins.then_inc(gu_ready, 1)

            def down_products(n):
                pe.wait_ge(hl_ready, n + 1)
                for q in range(4):
                    if q >= 2:
                        pe.wait_ge(ht_taken, n * 4 + q - 1)
                    for part in range(2):
                        for k in range(4):
                            at = q * 512 + k * P
                            ins = pe.transpose(T[q % 2][:, part, k, :], HQ[:, part, at:at + P], idh)
                    ins.then_inc(ht_ready, 1)
                pe.wait_ge(x_added, n + 1)
                for q in range(4):
                    pe.wait_ge(ht_taken, n * 4 + q + 1)
                    for k in range(4):
                        for lp, W in ((0, WH), (0, WL), (1, WH)):
                            i = 4 * q + k
                            ins = pe.matmul(DN[0][:, :], HT[:, q, lp, k, :], W[:, 2, i * D:(i + 1) * D],
                                            start=(i == 0 and lp == 0 and W is WH), stop=(i == KI - 1 and lp == 1))
                ins.then_inc(dn_ready, 1)

            def stage(tt, gate_up=True, down=True):
                if gate_up:
                    pe.wait_ge(xl_ready, tt + 1)
                    pe.wait_ge(xh_ready, tt + 1)
                    for part in range(2):
                        for k in range(KD):
                            ins = pe.transpose(T[0][:, part, k, :], XQ[:, part, k * P:(k + 1) * P], idh)
                    ins.then_inc(xt_ready, 1)
                    pe.wait_ge(xt_taken, tt + 1)
                    gate_up_products(tt, 0)
                if down:
                    down_products(tt - 2)
                if gate_up:
                    for i in range(1, IC):
                        gate_up_products(tt, i)

            stage(0, down=False)
            stage(1, down=False)
            with pe.Fori(2, TILES) as tt:
                stage(tt)
            stage(TILES, gate_up=False)
            stage(TILES + 1, gate_up=False)

        @block.vector
        def _(v):
            n_ds = [0]

            def step(ins):
                n_ds[0] += 1
                ins.then_inc(ds_ready, 1)
                v.wait_ge(ds_ready, n_ds[0])

            step(v.memset(EPS[:, :], 1e-5))
            step(v.tensor_scalar(DS[:, 0:2], SCL[:, 0:2], 2.0 ** -23, None, ALU.mult))
            step(v.tensor_scalar(DS[:, 2:3], SCL[:, 2:3], tg[:, 3:4], 2.0 ** -26, ALU.mult, ALU.mult))
            assert n_ds[0] == N_DS
            v.sem_inc(h_ready, 2)
            v.sem_inc(x_added, 1)

            def moments(tt):
                own = Tally(v, s_own, tt, S_OWN)
                own.inc(v.bn_stats(ST[:, :], X[:, ds(tt, 1), :]))
                own.wait()
                v.sem_inc(passed, 1)
                v.bn_aggr(MV[:, :], ST[:, :]).then_inc(mv_ready, 1)
                own.done()

            def prepare(tt):
                own = Tally(v, x_own, tt, X_OWN)
                x = X[:, ds(tt, 1), :]
                v.wait_ge(sd_ready, tt + 1)
                own.inc(v.reciprocal(SD[:, :], SD[:, :]))
                own.wait()
                own.inc(v.tensor_scalar(XN[:, :], x, MV[:, 0:1], SD[:, 0:1], ALU.subtract, ALU.mult))
                own.wait()
                own.inc(v.tensor_reduce(XA[:, :], XN[:, :].rearrange("p (n k) -> p n k", k=BLK), AX.X, ALU.max,
                                        apply_absolute_value=True))
                own.wait()
                own.inc(v.tensor_scalar(XA[:, :], XA[:, :], 1.0 / 448.0, 1e-30, ALU.mult, ALU.max))
                own.wait()
                own.inc(v.reciprocal(XI[:, :], XA[:, :]))
                own.inc(v.tensor_scalar(XA[:, :], XA[:, :], XS, None, ALU.mult))
                own.wait()
                for _ in quantise(v, own, XN[:, :], XV[:, :], XM[:, :], XI[:, :], XA[:, :], D // BLK):
                    pass
                v.sem_inc(xv_ready, 1)
                v.wait_ge(xh_ready, tt + 1)
                v.tensor_tensor(XQ[:, 1, :], XV[:, :], XQ[:, 0, :], ALU.subtract).then_inc(xl_ready, 1)
                own.done()

            def gated(tt, i):
                v.wait_ge(sg_ready, tt * IC + i + 1)
                v.scalar_tensor_tensor(out=H[:, i * 512:(i + 1) * 512], in0=U[i % 2][:, :], scalar=DS[:, 1:2],
                                       in1=SG[:, i % 2, :], op0=ALU.mult, op1=ALU.mult).then_inc(h_ready, 1)

            def quant(tt):
                own = Tally(v, h_own, tt, H_OWN)
                v.wait_ge(h_ready, tt * IC + IC + 2)
                own.inc(v.tensor_reduce(HA[:, :], H[:, :].rearrange("p (n k) -> p n k", k=BLK), AX.X, ALU.max,
                                        apply_absolute_value=True))
                own.wait()
                own.inc(v.tensor_reduce(HX[:, 0:1], HA[:, :], AX.X, ALU.max))
                own.wait()
                own.inc(v.tensor_scalar(HX[:, 0:1], HX[:, 0:1], 1e-30, None, ALU.max))
                own.inc(v.tensor_scalar(HA[:, :], HA[:, :], 1.0 / 448.0, 1e-30, ALU.mult, ALU.max))
                own.wait()
                own.inc(v.reciprocal(HI[:, :], HA[:, :]))
                own.inc(v.tensor_scalar(HX[:, 1:2].bitcast(U32), HX[:, 0:1].bitcast(U32), 0x7F800000, None, ALU.bitwise_and))
                own.wait()
                own.inc(v.reciprocal(HX[:, 2:3], HX[:, 1:2]))
                own.wait()
                own.inc(v.tensor_scalar(HA[:, :], HA[:, :], HX[:, 2:3], 8192.0, ALU.mult, ALU.mult))
                own.wait()
                yield from quantise(v, own, H[:, :], V[:, :], M[:, :], HI[:, :], HA[:, :], INTER // BLK)
                v.sem_inc(hv_ready, 1)
                yield
                v.wait_ge(x_added, tt + 1)
                own.inc(v.tensor_scalar(RSC[:, :], HX[:, 1:2], DS[:, 2:3], None, ALU.mult))
                v.wait_ge(hh_ready, tt + 1)
                v.tensor_tensor(HQ[:, 1, :], V[:, :], HQ[:, 0, :], ALU.subtract).then_inc(hl_ready, 1)
                v.wait_ge(hl_ready, tt + 1)
                own.wait()
                own.done()

            def add(tt):
                v.wait_ge(dn_ready, tt + 1)
                x = X[:, ds(tt, 1), :]
                v.scalar_tensor_tensor(out=x, in0=DN[0][:, :], scalar=RSC[:, 0:1], in1=x,
                                       op0=ALU.mult, op1=ALU.add).then_inc(x_added, 1)

            def stage(tt, gate_up=True, quantised=True, down=True, more=True):
                if gate_up and more:
                    moments(tt + 1)
                parts = quant(tt - 1) if quantised else iter(())
                next(parts, None)
                if gate_up:
                    gated(tt, 0)
                for _ in range(3):
                    next(parts, None)
                if down:
                    add(tt - 2)
                next(parts, None)
                if gate_up:
                    gated(tt, 1)
                    if more:
                        prepare(tt + 1)
                    gated(tt, 2)
                    gated(tt, 3)

            moments(0)
            prepare(0)
            stage(0, quantised=False, down=False)
            stage(1, down=False)
            with v.Fori(2, TILES - 1) as tt:
                stage(tt)
            stage(TILES - 1, more=False)
            stage(TILES, gate_up=False)
            stage(TILES + 1, gate_up=False, quantised=False)
            v.wait_ge(x_added, TILES + 1)


N_DS = 3
S_OWN = 1
X_OWN = 12
H_OWN = 15


def extra_inputs(z):
    out = {"shape_constants": shape_constants(), **spline_constants()}
    out["spline_windows"] = windows([z[f"L0_ffn_{n}_cp"] for n in ("gate", "up", "down")])
    return out


PRE_DVE = 11
DVE_OWN_A = 31
WARM_START = 16
WARM_HEAD = 1
FIN_OWN_A = 10
ACT_OWN_A = 2


def build_program(nc, A, out):
    with ExitStack() as top:
        X = top.enter_context(nc.sbuf_tensor("X", [P, TILES, D], F32))
        CST = top.enter_context(nc.sbuf_tensor("CST", [P, CST_W], F32))
        IDB = top.enter_context(nc.sbuf_tensor("IDB", [P, P], BF16))
        IDH = top.enter_context(nc.sbuf_tensor("IDH", [P, P], F16))
        SCL = top.enter_context(nc.sbuf_tensor("SCL", [P, 3], F32))
        scratch = nc.dram_tensor("spline_scratch", [3, 6, 4, RUNS], BF16).ap()
        TG = top.enter_context(nc.sbuf_tensor("TG", [P, 4], F32))
        loaded, ready, stored = nc.alloc_semaphore("loaded"), nc.alloc_semaphore("consts_ready"), nc.alloc_semaphore("stored")
        orr = out.rearrange("b (c p) d -> p (b c) d", p=P)
        xr = A["x"].rearrange("b (c p) d -> p (b c) d", p=P)
        with nc.Block() as block:
            @block.sync
            def _(sp):
                sp.dma_start(CST[:, :], A["shape_constants"]).then_inc(loaded, 16)
                for q, name in enumerate(("g_xattn", "g_ffn")):
                    sp.dma_start(TG[:, 2 * q:2 * q + 2], A[name].rearrange("(a n) -> a n", a=1).to_broadcast([P, 2])).then_inc(loaded, 16)
                for b in range(B):
                    sp.dma_start(X[:, b * NC:(b + 1) * NC, :], xr[:, b * NC:(b + 1) * NC, :]).then_inc(loaded, 16)

            @block.vector
            def _(v):
                v.wait_ge(loaded, 7 * 16)
                v.tensor_copy(IDB[:, :], CST[:, 0:P]).then_inc(ready, 1)
                v.tensor_copy(IDH[:, :], CST[:, 0:P]).then_inc(ready, 1)

            @block.scalar
            def _(act):
                act.wait_ge(loaded, 7 * 16)
                nc.scalar.activation(TG[:, :], TG[:, :], ACT.Tanh).then_inc(ready, 1)
                act.wait_ge(ready, 3)

        with ExitStack() as stack:
            spline = SplineCoefficients(nc, A, SCL, scratch, stack)
            mlstm_phase(nc, A, X, TG, CST, CST[:, 0:P], IDB[:, :], spline, stack)
        with ExitStack() as weights:
            WH = weights.enter_context(nc.sbuf_tensor("W0H", [P, 3, RUNS], F16))
            WL = weights.enter_context(nc.sbuf_tensor("W0L", [P, 3, RUNS], F16))
            with ExitStack() as stack:
                spline_phase(nc, A, CST[:, CST_W - 1:CST_W], WH, WL, scratch, stack)
            with ExitStack() as stack:
                ffn0_phase(nc, A, X, TG, CST[:, 0:P], WH, WL, SCL, stack)
        with ExitStack() as stack:
            attention_phase(nc, A, X, TG, CST[:, 0:P], stack)
        with ExitStack() as weights:
            WH = weights.enter_context(nc.sbuf_tensor("W1H", [P, 3, RUNS], F16))
            WL = weights.enter_context(nc.sbuf_tensor("W1L", [P, 3, RUNS], F16))
            with ExitStack() as stack:
                weights_phase(nc, A, WH, WL, SCL, IDH[:, :], stack)
            with ExitStack() as stack:
                ffn1_phase(nc, A, X, TG, IDH[:, :], WH, WL, SCL, orr, stored, stack)


_INS = ["x", "ctx_2048", "g_xattn", "g_ffn", "L0_xattn_Wi", "L0_xattn_bi", "L0_xattn_Wf", "L0_xattn_bf",
        "L0_xattn_ln_scale", "L1_ffn_gate_w", "L1_ffn_up_w", "L1_ffn_down_w"]


def kernel(**inputs):
    import numpy as _np
    import concourse.bacc as _bacc
    from concourse import mybir as _mybir
    from concourse.bass_utils import run_bass_kernel_spmd as _run

    nc = _bacc.Bacc("TRN2", target_bir_lowering=False, num_devices=1)
    given = {name: _np.asarray(a) for name, a in inputs.items()}
    arrays = {name: _np.ascontiguousarray(given[name]) for name in _INS}
    arrays.update(extra_inputs(given))
    arrays = {f"in_{name}_dram": a for name, a in arrays.items()}
    args = {}
    for name, a in arrays.items():
        args[name[3:-5]] = nc.dram_tensor(name, a.shape, _mybir.dt.from_np(a.dtype), kind="ExternalInput").ap()
    out = nc.dram_tensor("out_0_dram", (B, S, D), _mybir.dt.float32, kind="ExternalOutput").ap()
    build_program(nc, args, out)
    r = _run(nc, [arrays], core_ids=[0])
    return r.results[0]["out_0_dram"]
```

```python
from contextlib import ExitStack

import concourse.bass as bass
from concourse import mybir
import numpy as np

F32 = mybir.dt.float32
F16 = mybir.dt.float16
BF16 = mybir.dt.bfloat16
U32 = mybir.dt.uint32
U8 = mybir.dt.uint8
I32 = mybir.dt.int32
ALU = mybir.AluOpType
ACT = mybir.ActivationFunctionType
AX = mybir.AxisListType
RMAX = bass.bass_isa.ReduceOp.max
ds = bass.ds

P = 128
B, S, D = 4, 512, 512
NC = S // P
KD = D // P
TILES = B * NC
NH, DH = 16, 32
HG = P // DH
VW = DH + 1
INTER = 2048
KI = INTER // P


class Tally:

    def __init__(self, eng, sem, it, per):
        self.eng, self.sem, self.it, self.per, self.n = eng, sem, it, per, 0

    def inc(self, ins):
        self.n += 1
        ins.then_inc(self.sem, 1)

    def wait(self):
        self.eng.wait_ge(self.sem, self.it * self.per + self.n)

    def done(self):
        assert self.n == self.per, self.n


def shape_constants():
    ident = np.eye(P, dtype=np.float32)
    t, s = np.mgrid[0:P, 0:P]
    future = np.where(t > s, np.float32(-1e30), np.float32(0))
    k, h = np.mgrid[0:P, 0:NH]
    pick = ((k % 32 == h) & (k < 96)).astype(np.float32)
    p, c = np.mgrid[0:P, 0:HG * VW]
    own = np.where(p // DH == c // VW, np.float32(DH ** -0.5), np.float32(0))
    return np.concatenate([ident, future, pick, own, np.arange(P)[:, None]], axis=1).astype(np.float32)


CST_W = P + P + NH + HG * VW + 1


def mlstm_phase(nc, A, X, tg, CST, idf, idb, spline, x_loaded, stack):
    def sb(name, shape, dt=F32):
        return stack.enter_context(nc.sbuf_tensor(name, shape, dt))

    def ps(name):
        return stack.enter_context(nc.psum_tensor(name, [P, 512], F32))

    sem = nc.alloc_semaphore
    XN = sb("XN", [P, NC, D])
    CTX = sb("CTX", [P, NC, D])
    QT = sb("QT", [P, KD, S])
    KT = sb("KT", [P, KD, S])
    VA = sb("VA", [P, NC, NH, VW])
    OUT = sb("OUT", [P, NC, NH, VW])
    HN = sb("HN", [P, NC * NH, DH])
    SQ = sb("SQ", [P, NC * NH, DH])
    KU = sb("KU", [P, 6, D])
    SS = sb("SS", [P, 2, NC - 1, HG * VW])
    DD = sb("DD", [P, 2, S])
    CC = sb("CC", [P, 2, S])
    WG = sb("WG", [P, 12, 32])
    GS = sb("GS", [P, NC, 2, 96])
    TM = sb("TM", [P, 13, NH])
    ROW = sb("ROW", [96, 8, S])
    ZF, ZI, AZ, MZ, LF, FC, FM, EL = (ROW[:, i, :] for i in range(8))
    VV = sb("VV", [96, 2, S])
    RR = sb("RR", [96, 2, S])
    NP = sb("NP", [96, 2, S], BF16)
    T2 = sb("T2", [96, 2, S], BF16)
    UW = sb("UW", [NH, 13, P])
    ONE = sb("ONE", [96, S])
    BIAS = sb("BIAS", [96, 2])
    GLN = sb("GLN", [P, D])
    ST = sb("ST", [P, NC, 6])
    MV = sb("MV", [P, NC, 2])
    SD = sb("SD", [P, NC])
    RS = sb("RS", [P, NC])
    MU = sb("MU", [P, NC * NH])
    VR = sb("VR", [P, NC * NH])
    DN = sb("DN", [P, NC * NH])
    FUT = sb("FUT", [P, NC, P], BF16)
    PICK = sb("PICK", [P, NH], BF16)
    EPS = sb("EPS", [P, 3])
    T = [ps("T0"), ps("T1")]
    QK = [ps("QK0"), ps("QK1")]
    E = [ps("E0"), ps("E1")]
    O = [ps("O0"), ps("O1")]

    ctx_loaded, w_loaded, pre_dve, pre_act = (sem("a_" + n) for n in ("ctx_loaded", "w_loaded", "pre_dve", "pre_act"))
    pre_pool = sem("a_pre_pool")
    mv_ready, sd_ready, xn_ready, t_ready = (sem("a_" + n) for n in ("mv_ready", "sd_ready", "xn_ready", "t_ready"))
    t_taken = [sem("a_t_taken0"), sem("a_t_taken1")]
    va_ready, ku_ready, az_ready, el_ready = (sem("a_" + n) for n in ("va_ready", "ku_ready", "az_ready", "el_ready"))
    vv_ready, np1_ready, rr_ready, t2_ready, r3_ready, np_ready, uw_ready = (
        sem("a_" + n) for n in ("vv_ready", "np1", "rr", "t2", "r3", "np_ready", "uw_ready"))
    gs_ready, ss_ready, qe_ready, d_ready, c_ready, pv_done, o_taken = (
        sem("a_" + n) for n in ("gs_ready", "ss_ready", "qe_ready", "d_ready", "c_ready", "pv_done", "o_taken"))
    hc_ready, sq_ready, vr_ready, sv_ready = (sem("a_" + n) for n in ("hc", "sq", "vr", "sv"))
    passed = [sem(f"a_passed{i}") for i in range(4)]
    dve_own, fin_own, act_own = sem("a_dve_own"), sem("a_fin_own"), sem("a_act_own")
    NT = 20
    ctx = A["ctx_2048"].rearrange("b (c p) d -> b p c d", p=P)

    with nc.Block() as block:
        @block.sync
        def _(sp):
            sp.dma_start(WG[:, :, 0:NH], A["L0_xattn_Wi"].rearrange("(k p) h -> p k h", p=P)).then_inc(w_loaded, 16)
            sp.dma_start(WG[:, :, NH:2 * NH], A["L0_xattn_Wf"].rearrange("(k p) h -> p k h", p=P)).then_inc(w_loaded, 16)
            sp.dma_start(GLN[:, :], A["L0_xattn_ln_scale"].rearrange("(a d) -> a d", a=1).to_broadcast([P, D])).then_inc(w_loaded, 16)
            sp.wait_ge(pre_pool, 3)
            for r in range(3):
                for q, name in enumerate(("L0_xattn_bi", "L0_xattn_bf")):
                    sp.dma_start(BIAS[32 * r:32 * r + NH, q:q + 1], A[name].rearrange("(h a) -> h a", a=1)).then_inc(w_loaded, 16)
            sp.dma_start(CTX[:, :, :], ctx[0]).then_inc(ctx_loaded, 16)
            spline.load(sp)
            with sp.Fori(1, B) as b:
                sp.wait_ge(t_ready, b * NT + (8 - NT))
                sp.sem_inc(passed[3], 1)
                sp.wait_ge(va_ready, b * 2)
                sp.wait_ge(ku_ready, b)
                sp.dma_start(CTX[:, :, :], ctx[ds(b, 1)].rearrange("a p c d -> p (a c) d")).then_inc(ctx_loaded, 16)
            spline.store(sp)

        @block.gpsimd
        def _(pool):
            pool.memset(BIAS[:, :], 0.0).then_inc(pre_pool, 1)
            pool.memset(GS[:, :, :, :], 0.0).then_inc(pre_pool, 1)
            pool.memset(VA[:, :, :, DH:VW], 1.0).then_inc(pre_pool, 1)

            def batch(b, first=False):
                pool.wait_ge(xn_ready, b * NC + 1)
                pool.sem_inc(passed[0], 1)
                pool.wait_ge(ctx_loaded, b * 16 + 16)
                pool.sem_inc(passed[0], 1)
                pool.tensor_copy(VA[:, :, :, 0:DH],
                                 CTX[:, :, :].rearrange("p c (h d) -> p c h d", h=NH)).then_inc(va_ready, 1)
                if not first:
                    pool.wait_ge(hc_ready, b)
                    pool.sem_inc(passed[0], 1)
                pool.memset(OUT[:, 0, :, :], 0.0).then_inc(va_ready, 1)

            batch(0, first=True)
            spline.largest(pool)
            with pool.Fori(1, B) as b:
                batch(b)

        @block.scalar
        def _(act):
            def norms(b):
                act.wait_ge(hc_ready, b + 1)
                nc.scalar.activation(SQ[:, :, :], HN[:, :, :], ACT.Square).then_inc(sq_ready, 1)
                act.wait_ge(vr_ready, b + 1)
                nc.scalar.activation(VR[:, :], VR[:, :], ACT.Sqrt, scale=1.0 / DH, bias=EPS[:, 2:3]).then_inc(sv_ready, 1)

            def batch(b, first=False):
                own = Tally(act, act_own, b, ACT_OWN_A)
                act.wait_ge(mv_ready, b + 1)
                act.wait_ge(pre_dve, PRE_DVE)
                nc.scalar.activation(SD[:, :], MV[:, :, 1], ACT.Sqrt, bias=EPS[:, 0:1]).then_inc(sd_ready, 1)
                for n in range(8):
                    act.wait_ge(t_ready, b * NT + n + 1)
                    dst = (QT if n < 4 else KT)[:, n % 4, :]
                    nc.scalar.copy(dst, T[n % 2][:, :]).then_inc(t_taken[n % 2], 1)
                if not first:
                    norms(b - 1)
                act.wait_ge(az_ready, b + 1)
                own.inc(nc.scalar.activation(EL, AZ, ACT.Exp, scale=-1.0))
                own.wait()
                nc.scalar.activation(EL, EL, ACT.Ln, bias=EPS[0:96, 1:2]).then_inc(el_ready, 1)
                act.wait_ge(vv_ready, b * 3 + 3)
                nc.scalar.copy(NP[:, :, :], VV[:, :, :]).then_inc(np1_ready, 1)
                i = 0
                for c in range(1, NC):
                    nc.scalar.activation(UW[:, i:i + c, :], VV[0:NH, 0, 0:c * P], ACT.Exp,
                                         bias=VV[0:NH, 1, c * P - 1:c * P]).then_inc(uw_ready, 1)
                    i += c
                act.wait_ge(rr_ready, b + 1)
                nc.scalar.copy(T2[64:96, :, :], RR[64:96, :, :]).then_inc(t2_ready, 1)
                own.inc(nc.scalar.copy(NP[32:64, :, :], RR[32:64, :, :]))
                for c in range(1, NC):
                    nc.scalar.activation(UW[:, 5 + c, :], VV[0:NH, 1, c * P:(c + 1) * P], ACT.Exp,
                                         bias=FM[0:NH, c:c + 1]).then_inc(uw_ready, 1)
                nc.scalar.activation(UW[:, 9:13, :], EL[0:NH, :], ACT.Exp, scale=-1.0).then_inc(uw_ready, 1)
                act.wait_ge(r3_ready, b + 1)
                nc.scalar.copy(NP[64:96, :, :], RR[64:96, :, :]).then_inc(np_ready, 1)
                for h in range(NH):
                    act.wait_ge(qe_ready, b * NH + h + 1)
                    if h >= 2:
                        act.wait_ge(c_ready, b * NH + h - 1)
                    nc.scalar.activation(DD[:, h % 2, :], E[h % 2][:, :], ACT.Exp).then_inc(d_ready, 1)
                own.done()

            batch(0, first=True)
            with act.Fori(1, B) as b:
                batch(b)
            norms(B - 1)

        @block.tensor
        def _(pe):
            pe.wait_ge(pre_dve, PRE_DVE)
            pe.wait_ge(w_loaded, 9 * 16)
            with pe.Fori(0, B) as b:
                def keep_warm(n, bank=E[0]):
                    for _ in range(n):
                        pe.matmul(bank[:, :], idb, FUT[:, :, :], start=True, stop=True)

                def bank(n):
                    if n >= 2:
                        pe.wait_ge(t_taken[n % 2], b * (NT // 2) + n // 2)
                    return T[n % 2]

                def taken(n):
                    pe.wait_ge(t_taken[n % 2], b * (NT // 2) + n // 2 + 1)

                for n in range(8):
                    if n == 4:
                        pe.wait_ge(ctx_loaded, b * 16 + 16)
                    src, k = (XN if n < 4 else CTX), n % 4
                    t = bank(n)
                    for c in range(NC):
                        if n == 0:
                            pe.wait_ge(xn_ready, b * NC + c + 1)
                        last = pe.transpose(t[:, c * P:(c + 1) * P], src[:, c, k * P:(k + 1) * P], idf)
                    last.then_inc(t_ready, 1)
                t = bank(8)
                taken(7)
                taken(6)
                for c in range(NC):
                    for k in range(2 * KD):
                        src = QT if k < KD else KT
                        last = pe.matmul(t[:, c * 32:(c + 1) * 32], src[:, k % KD, c * P:(c + 1) * P], WG[:, k, :],
                                         start=(k == 0), stop=(k == 2 * KD - 1))
                last.then_inc(t_ready, 1)
                for n in (9, 10):
                    t = bank(n)
                    taken(8)
                    for c in range(NC):
                        last = pe.transpose(t[0:96, c * P:(c + 1) * P], GS[:, c, n - 9, :], idf)
                    last.then_inc(t_ready, 1)
                t = bank(11)
                pe.wait_ge(uw_ready, b * 7 + 7)
                pe.sem_inc(passed[2], 1)
                for i in range(13):
                    last = pe.transpose(t[:, i * NH:(i + 1) * NH], UW[:, i, :], idf[0:NH, 0:NH])
                last.then_inc(t_ready, 1)
                keep_warm(WARM_START)
                pe.wait_ge(va_ready, b * 2 + 2)
                pe.wait_ge(ku_ready, b + 1)

                def scores(h):
                    g, j = divmod(h, HG)
                    r = slice(DH * j, DH * j + DH)
                    if h >= 2:
                        pe.wait_ge(c_ready, b * NH + h - 1)
                    for c in range(NC):
                        pe.matmul(QK[h % 2][:, c * P:(c + 1) * P], KT[r, g, c * P:(c + 1) * P],
                                  QT[r, g, c * P:(c + 1) * P], start=True, stop=True)
                    e = E[h % 2]
                    pick = PICK[0:96, h:h + 1]
                    pe.matmul(e[:, :], idb, FUT[:, :, :], start=True, stop=False)
                    pe.matmul(e[:, :], pick.to_broadcast([96, P]), NP[:, 1, :], start=False, stop=False)
                    for c in range(NC):
                        last = pe.matmul(e[:, c * P:(c + 1) * P], NP[:, 0, c * P:(c + 1) * P],
                                         pick.to_broadcast([96, P]), start=False, stop=(c == NC - 1))
                    last.then_inc(qe_ready, 1)

                def weigh(h):
                    pair, jj = divmod(h, 2)
                    if jj == 0 and pair >= 2:
                        pe.wait_ge(o_taken, b * (NH // 2) + pair - 1)
                    pe.wait_ge(c_ready, b * NH + h + 1)
                    o = O[pair % 2]
                    for c in range(NC):
                        at = (2 * c + jj) * VW
                        last = pe.matmul(o[:, at:at + VW], CC[:, h % 2, c * P:(c + 1) * P], VA[:, c, h, :],
                                         start=True, stop=True)
                    last.then_inc(pv_done, 1)

                def state(g):
                    t = bank(12 + 2 * g)
                    i = 0
                    for c in range(1, NC):
                        for u in range(c):
                            last = pe.matmul(t[:, (c - 1) * HG * VW:c * HG * VW], KU[:, i, g * P:(g + 1) * P],
                                             VA[:, u, g * HG:(g + 1) * HG, :], start=(u == 0), stop=(u == c - 1))
                            i += 1
                    last.then_inc(t_ready, 1)

                def read_state(g):
                    t = bank(13 + 2 * g)
                    taken(12 + 2 * g)
                    for c in range(1, NC):
                        last = pe.matmul(t[:, (c - 1) * HG * VW:c * HG * VW], QT[:, g, c * P:(c + 1) * P],
                                         SS[:, g % 2, c - 1, :], start=True, stop=True)
                    last.then_inc(t_ready, 1)

                state(0)
                pe.wait_ge(np_ready, b + 1)
                scores(0)
                for h in range(NH):
                    if h % HG == 0:
                        read_state(h // HG)
                    if h + 1 < NH:
                        scores(h + 1)
                    weigh(h)
                    keep_warm(WARM_HEAD, E[h % 2])
                    if h % HG == 2 and h // HG + 1 < NH // HG:
                        state(h // HG + 1)

        @block.vector
        def _(v):
            v.wait_ge(w_loaded, 9 * 16)
            n_pre = [0]

            def pre(ins):
                n_pre[0] += 1
                ins.then_inc(pre_dve, 1)

            pre(v.memset(EPS[:, 0:1], 1e-5))
            pre(v.memset(EPS[:, 1:2], 1.0))
            pre(v.memset(EPS[:, 2:3], 1e-6))
            pre(v.memset(ONE[:, :], 1.0))
            for c in range(NC):
                pre(v.tensor_copy(FUT[:, c, :], CST[:, P:2 * P]))
            pre(v.tensor_copy(PICK[:, :], CST[:, 2 * P:2 * P + NH]))
            pre(v.tensor_tensor(WG[:, 4:8, :], WG[:, 4:8, :], WG[:, 8:12, :], ALU.add))
            pre(v.tensor_scalar(GLN[:, :], GLN[:, :], tg[:, 0:1], -1.0, ALU.mult, ALU.mult))
            assert n_pre[0] == PRE_DVE
            v.wait_ge(pre_dve, PRE_DVE)
            v.wait_ge(pre_pool, 3)
            own_mask = CST[:, 2 * P + NH:CST_W - 1]
            def finish(b):
                own = Tally(v, fin_own, b, FIN_OWN_A)
                sums = OUT[:, :, :, DH].rearrange("p c h -> p (c h)")
                own.inc(v.scalar_tensor_tensor(out=DN[:, :], in0=sums, scalar=-1.0, in1=sums, op0=ALU.mult, op1=ALU.max))
                own.wait()
                own.inc(v.tensor_tensor(DN[:, :], DN[:, :], TM[:, 9:13, :].rearrange("p c h -> p (c h)"), ALU.max))
                own.wait()
                own.inc(v.tensor_scalar(DN[:, :], DN[:, :], 1e-6, None, ALU.add))
                own.wait()
                own.inc(v.reciprocal(DN[:, :], DN[:, :]))
                own.wait()
                bc = lambda x: x.unsqueeze(2).to_broadcast([P, NC * NH, DH])
                own.inc(v.tensor_tensor(HN[:, :, :], OUT[:, :, :, 0:DH].rearrange("p c h d -> p (c h) d"), bc(DN[:, :]), ALU.mult))
                own.wait()
                own.inc(v.tensor_reduce(MU[:, :], HN[:, :, :], AX.X, ALU.add))
                own.wait()
                v.scalar_tensor_tensor(out=HN[:, :, :], in0=bc(MU[:, :]), scalar=1.0 / DH, in1=HN[:, :, :],
                                       op0=ALU.mult, op1=ALU.subtract).then_inc(hc_ready, 1)
                v.wait_ge(sq_ready, b + 1)
                v.tensor_reduce(VR[:, :], SQ[:, :, :], AX.X, ALU.add).then_inc(vr_ready, 1)
                v.wait_ge(sv_ready, b + 1)
                own.inc(v.reciprocal(VR[:, :], VR[:, :]))
                own.wait()
                yield
                own.inc(v.tensor_tensor(HN[:, :, :], HN[:, :, :], bc(VR[:, :]), ALU.mult))
                own.wait()
                yield
                hn = HN[:, :, :].rearrange("p (c h) d -> p c (h d)", c=NC)
                own.inc(v.tensor_tensor(hn, hn, GLN[:, :].unsqueeze(1).to_broadcast([P, NC, D]), ALU.mult))
                own.wait()
                yield
                x = X[:, ds(b * NC, NC), :]
                own.inc(v.tensor_tensor(x, x, hn, ALU.add))
                own.wait()
                own.done()

            def batch(b, first=False):
                own = Tally(v, dve_own, b, DVE_OWN_A)
                for c in range(NC):
                    own.inc(v.bn_stats(ST[:, c, :], X[:, ds(b * NC + c, 1), :]))
                own.wait()
                v.sem_inc(passed[1], 1)
                for c in range(NC):
                    ins = v.bn_aggr(MV[:, c, :], ST[:, c, :])
                    if c < NC - 1:
                        own.inc(ins)
                ins.then_inc(mv_ready, 1)
                v.wait_ge(sd_ready, b + 1)
                own.inc(v.reciprocal(RS[:, :], SD[:, :]))
                own.wait()
                for c in range(NC):
                    v.tensor_scalar(XN[:, c, :], X[:, ds(b * NC + c, 1), :], MV[:, c, 0:1], RS[:, c:c + 1],
                                    ALU.subtract, ALU.mult).then_inc(xn_ready, 1)
                before = iter(()) if first else finish(b - 1)
                next(before, None)
                v.wait_ge(t_ready, b * NT + 9)
                gates = T[0][:, 0:P].rearrange("p (c q h) -> p (c q) h", c=NC, q=2)
                gs = GS[:, :, :, :].rearrange("p c q r -> p (c q) r")
                for r in range(3):
                    ins = v.tensor_copy(gs[:, :, 32 * r:32 * r + NH], gates)
                    if r < 2:
                        own.inc(ins)
                ins.then_inc(t_taken[0], 1)
                v.wait_ge(t_ready, b * NT + 10)
                v.tensor_scalar(ZI, T[1][0:96, :], BIAS[:, 0:1], None, ALU.add).then_inc(t_taken[1], 1)
                v.wait_ge(t_ready, b * NT + 11)
                v.tensor_scalar(ZF, T[0][0:96, :], BIAS[:, 1:2], None, ALU.add).then_inc(t_taken[0], 1)
                v.wait_ge(t_taken[0], b * (NT // 2) + 6)
                v.scalar_tensor_tensor(out=AZ, in0=ZF, scalar=-1.0, in1=ZF, op0=ALU.mult, op1=ALU.max).then_inc(az_ready, 1)
                own.inc(v.tensor_scalar(MZ, ZF, 0.0, None, ALU.min))
                own.wait()
                next(before, None)
                v.wait_ge(el_ready, b + 1)
                own.inc(v.tensor_tensor(LF, MZ, EL, ALU.subtract))
                own.wait()
                own.inc(v.tensor_tensor_scan(FC, ONE[:, :], LF, 0.0, ALU.mult, ALU.add))
                own.wait()
                v.tensor_tensor(VV[:, 0, :], ZI, FC, ALU.subtract).then_inc(vv_ready, 1)
                v.wait_ge(vv_ready, b * 3 + 1)
                own.inc(v.tensor_tensor_scan(MZ, ONE[:, :], VV[:, 0, :], -3.0e38, ALU.mult, ALU.max))
                own.wait()
                own.inc(v.tensor_tensor(EL, FC, MZ, ALU.add))
                for c in range(1, NC):
                    own.inc(v.tensor_copy(FM[:, c:c + 1], MZ[:, c * P - 1:c * P]))
                own.wait()
                v.tensor_scalar(VV[:, 1, :], MZ, -1.0, None, ALU.mult).then_inc(vv_ready, 2)
                next(before, None)
                v.wait_ge(np1_ready, b + 1)
                v.tensor_tensor(RR[:, :, :], VV[:, :, :], NP[:, :, :], ALU.subtract).then_inc(rr_ready, 1)
                v.wait_ge(t2_ready, b + 1)
                v.tensor_tensor(RR[64:96, :, :], RR[64:96, :, :], T2[64:96, :, :], ALU.subtract).then_inc(r3_ready, 1)
                next(before, None)
                v.wait_ge(t_ready, b * NT + 12)
                v.tensor_copy(TM[:, :, :], T[1][:, 0:13 * NH].rearrange("p (i h) -> p i h", h=NH)).then_inc(t_taken[1], 1)
                v.wait_ge(t_taken[1], b * (NT // 2) + 6)
                v.wait_ge(ctx_loaded, b * 16 + 16)
                i = 0
                for c in range(1, NC):
                    for t in range(c):
                        ins = v.tensor_tensor(
                            KU[:, i, :].rearrange("p (h d) -> p h d", h=NH),
                            CTX[:, t, :].rearrange("p (h d) -> p h d", h=NH),
                            TM[:, i, :].unsqueeze(2).to_broadcast([P, NH, DH]), ALU.mult)
                        i += 1
                        if i < 6:
                            own.inc(ins)
                ins.then_inc(ku_ready, 1)

                def take_state(g):
                    v.wait_ge(t_ready, b * NT + 13 + 2 * g)
                    v.tensor_tensor(SS[:, g % 2, :, :], T[0][:, 0:(NC - 1) * HG * VW].rearrange("p (c f) -> p c f", c=NC - 1),
                                    own_mask.unsqueeze(1).to_broadcast([P, NC - 1, HG * VW]),
                                    ALU.mult).then_inc(t_taken[0], 1)

                def take_read(g):
                    v.wait_ge(t_ready, b * NT + 14 + 2 * g)
                    for c in range(1, NC):
                        ins = v.tensor_tensor(
                            OUT[:, c, g * HG:(g + 1) * HG, :],
                            T[1][:, (c - 1) * HG * VW:c * HG * VW].rearrange("p (h f) -> p h f", h=HG),
                            TM[:, 5 + c, g * HG:(g + 1) * HG].unsqueeze(2).to_broadcast([P, HG, VW]), ALU.mult)
                        if c < NC - 1:
                            own.inc(ins)
                    ins.then_inc(t_taken[1], 1)
                    v.wait_ge(t_taken[1], b * (NT // 2) + 7 + g)

                def take_pair(pair):
                    v.wait_ge(pv_done, b * NH + 2 * pair + 2)
                    o = OUT[:, :, 2 * pair:2 * pair + 2, :]
                    v.tensor_tensor(o, o, O[pair % 2][:, 0:2 * NC * VW].rearrange("p (c j f) -> p c j f", c=NC, j=2),
                                    ALU.add).then_inc(o_taken, 1)

                v.wait_ge(va_ready, b * 2 + 2)
                for h in range(NH):
                    if h % HG == 0:
                        take_state(h // HG)
                    v.wait_ge(d_ready, b * NH + h + 1)
                    if h >= 2:
                        v.wait_ge(pv_done, b * NH + h - 1)
                    v.scalar_tensor_tensor(out=CC[:, h % 2, :], in0=QK[h % 2][:, :], scalar=DH ** -0.5,
                                           in1=DD[:, h % 2, :], op0=ALU.mult, op1=ALU.mult).then_inc(c_ready, 1)
                    if h % HG == 0:
                        take_read(h // HG)
                    if h % 2 == 1 and h >= 3:
                        take_pair(h // 2 - 1)
                    if first:
                        next(coefficients, None)
                take_pair(NH // 2 - 1)
                v.wait_ge(o_taken, (b + 1) * (NH // 2))
                own.done()

            coefficients = spline.vector_steps(v)
            batch(0, first=True)
            for _ in coefficients:
                pass
            v.wait_ge(x_loaded, 16 * (B - 1))
            with v.Fori(1, B) as b:
                batch(b)
            for _ in finish(B - 1):
                pass


N_FLAT = D * INTER
N_CTRL = int(D * INTER / 128.9)
RUNS = N_FLAT // P
RC = RUNS // P
QW = 2048
SUB = 512
PARTS = ((0, 0), (0, 1), (0, 2), (1, 0), (1, 1), (2, 0))


def run_orders():
    pos = np.arange(RUNS)
    gate = KD * (pos % INTER) + pos // INTER
    down = KI * (pos % D) + pos // D
    return gate, down


def spline_grid():
    t = np.linspace(0.0, N_CTRL - 1.0, N_FLAT, dtype=np.float64)
    i = np.clip(np.floor(t).astype(np.int64), 0, N_CTRL - 2)
    return t, i


def bf16_round(a):
    u = np.ascontiguousarray(a, dtype=np.float32).view(np.uint32).astype(np.uint64)
    u = (u + 0x7FFF + ((u >> 16) & 1)) & 0xFFFF0000
    return u.astype(np.uint32).view(np.float32)


def spline_constants():
    t, i = spline_grid()
    first = np.arange(RUNS) * P
    phase = t[first] - i[first]
    step = (N_CTRL - 1.0) / (N_FLAT - 1.0)
    basis = 0.5 * np.array([[0, 2, 0, 0], [-1, 0, 1, 0], [2, -5, 4, -1], [-1, 3, -3, 1]], np.float64)
    binom = [[1, 0, 0, 0], [1, 1, 0, 0], [1, 2, 1, 0], [1, 3, 3, 1]]
    coef = np.zeros((2, 4, 4, RUNS))
    for piece in range(2):
        u = phase - piece
        for m in range(4):
            for k in range(4):
                coef[piece, m, k] = sum(binom[l][m] * u ** (l - m) * basis[l, k] for l in range(m, 4))
    starts = (i.reshape(RUNS, P) == i[first][:, None]).sum(1).astype(np.float32)
    orders = run_orders()
    coefs = np.stack([coef[..., o] for o in orders]).reshape(2, 2, 4, 4, P, RC)
    coefs = np.ascontiguousarray(coefs.transpose(4, 0, 1, 2, 3, 5)).astype(np.float32).reshape(P, -1)
    second = [(starts[orders[o]] <= np.arange(P)[:, None]).astype(np.uint8) for o in (0, 0, 1)]
    second = np.ascontiguousarray(np.stack(second)).view(np.int32)
    power = np.stack([(np.arange(P) * step) ** m for m in range(4)])
    parts, rest = [], power
    for _ in range(3):
        parts.append(bf16_round(rest))
        rest = rest - parts[-1]
    powers = np.concatenate([parts[q] for _, q in PARTS]).astype(np.float32)
    return {"spline_coefs": coefs, "spline_second": second, "spline_powers": powers}


def windows(cp):
    _, i = spline_grid()
    base = i[np.arange(RUNS) * P]
    out = []
    for t, a in enumerate(cp):
        order = run_orders()[t // 2]
        at = np.clip(base[order][None, :] - 1 + np.arange(5)[:, None], 0, N_CTRL - 1)
        out.append(np.asarray(a)[at].reshape(5, P, RC).transpose(1, 0, 2))
    return np.ascontiguousarray(np.stack(out, axis=1))


class SplineCoefficients:

    def __init__(self, nc, A, SCL, scratch, stack):
        def sb(name, shape, dt=F32):
            return stack.enter_context(nc.sbuf_tensor(name, shape, dt))

        self.A, self.SCL, self.scratch = A, SCL, scratch
        self.WIN = sb("WIN", [P, 3, 5, RC])
        self.COEF = sb("COEF", [P, 2, 2, 4, 4 * RC])
        self.TMP = sb("TMP", [P, 4, 4, RC])
        self.CF = sb("CF", [P, 6, 4, RC])
        self.PB = sb("PB", [P, 3, 6, 4, RC], BF16)
        self.MX = sb("MX", [P, 3])
        self.MXA = sb("MXA", [P, 3])
        self.SC = sb("SC", [P, 3])
        self.loaded, self.mx_ready, self.all_max, self.parts_ready, self.parts_stored, self.own = (
            nc.alloc_semaphore("k_" + n) for n in ("loaded", "mx", "all_max", "parts", "parts_stored", "own"))

    def load(self, sp):
        sp.dma_start(self.WIN[:, :, :, :], self.A["spline_windows"]).then_inc(self.loaded, 16)
        sp.dma_start(self.COEF[:, :, :, :, :],
                     self.A["spline_coefs"].rearrange("p (o q m f) -> p o q m f", o=2, q=2, m=4)).then_inc(self.loaded, 16)

    def store(self, sp):
        sp.wait_ge(self.parts_ready, 3)
        for part in range(3):
            sp.dma_start(self.scratch[part].rearrange("a m (p c) -> p (a m) c", p=P),
                         self.PB[:, part, :, :, :].rearrange("p a m c -> p (a m) c")).then_inc(self.parts_stored, 16)
        sp.wait_ge(self.parts_stored, 48)

    def largest(self, pool):
        pool.wait_ge(self.mx_ready, 1)
        pool.partition_all_reduce(self.MXA[:, :], self.MX[:, :], P, RMAX).then_inc(self.all_max, 1)

    def vector_steps(self, v):
        WIN, COEF, TMP, CF, PB, MX, MXA, SC, SCL = (
            self.WIN, self.COEF, self.TMP, self.CF, self.PB, self.MX, self.MXA, self.SC, self.SCL)
        own, parts_ready = Tally(v, self.own, 0, 0), self.parts_ready

        def step(ins):
            own.inc(ins)
            own.wait()

        v.wait_ge(self.loaded, 32)
        v.tensor_reduce(MX[:, :], WIN[:, :, :, :].rearrange("p t k c -> p t (k c)"), AX.X, ALU.max,
                        apply_absolute_value=True).then_inc(self.mx_ready, 1)
        for tp in range(6):
            t, piece = divmod(tp, 2)
            step(v.tensor_tensor(TMP[:, :, :, :].rearrange("p m k c -> p m (k c)"),
                                 WIN[:, t, piece:piece + 4, :].rearrange("p k c -> p (k c)").unsqueeze(1).to_broadcast([P, 4, 4 * RC]),
                                 COEF[:, t // 2, piece, :, :], ALU.mult))
            yield
            step(v.tensor_reduce(CF[:, tp, :, :], TMP[:, :, :, :].rearrange("p m k c -> p m c k"), AX.X, ALU.add))
            yield
        yield
        v.wait_ge(self.all_max, 1)
        step(v.tensor_scalar(MXA[:, :], MXA[:, :], 1e-30, None, ALU.max))
        step(v.tensor_scalar(SCL[:, :].bitcast(U32), MXA[:, :].bitcast(U32), 0x7F800000, None, ALU.bitwise_and))
        step(v.reciprocal(SC[:, :], SCL[:, :]))
        step(v.tensor_scalar(SC[:, :], SC[:, :], 8192.0, None, ALU.mult))
        for t in range(3):
            c = CF[:, 2 * t:2 * t + 2, :, :]
            step(v.tensor_scalar(c, c, SC[:, t:t + 1], None, ALU.mult))
        v.tensor_copy(PB[:, 0, :, :, :], CF[:, :, :, :]).then_inc(parts_ready, 1)
        v.wait_ge(parts_ready, 1)
        yield
        step(v.tensor_tensor(CF[:, :, :, :], CF[:, :, :, :], PB[:, 0, :, :, :], ALU.subtract))
        v.tensor_copy(PB[:, 1, :, :, :], CF[:, :, :, :]).then_inc(parts_ready, 1)
        v.wait_ge(parts_ready, 2)
        yield
        step(v.tensor_tensor(CF[:, :, :, :], CF[:, :, :, :], PB[:, 1, :, :, :], ALU.subtract))
        v.tensor_copy(PB[:, 2, :, :, :], CF[:, :, :, :]).then_inc(parts_ready, 1)

def spline_phase(nc, A, WH, WL, scratch, stack):
    def sb(name, shape, dt=F32):
        return stack.enter_context(nc.sbuf_tensor(name, shape, dt))

    sem = nc.alloc_semaphore
    PW = sb("PW", [24, P])
    PWB = sb("PWB", [24, P], BF16)
    RH = sb("RH", [24, 2, 2, QW], BF16)
    MK = sb("MK", [P, 2, QW // 4], I32)
    WF = sb("WF", [P, 4, SUB])
    PS = [stack.enter_context(nc.psum_tensor(f"SP{i}", [P, SUB], F32)) for i in range(8)]
    loaded, pw_ready = sem("b_loaded"), sem("b_pw")
    wl_dve = sem("b_wl_dve")
    rh_loaded = [sem("b_rh0"), sem("b_rh1")]
    pp_ready, wf_copied, wf_selected, wh_ready, wl_ready = (
        sem("b_" + n) for n in ("pp", "wf_copied", "wf_selected", "wh", "wl"))
    passed, pool_passed = sem("b_passed"), sem("b_pool_passed")
    NS = RUNS // SUB
    SEL0 = 8

    with nc.Block() as block:
        @block.sync
        def _(sp):
            sp.dma_start(PW[:, :], A["spline_powers"]).then_inc(loaded, 16)
            with sp.Fori(0, 3) as t:
                for q in range(RUNS // QW):
                    cols = slice(q * QW, (q + 1) * QW)
                    sp.wait_ge(wf_selected, t * NS + 4 * q + SEL0 - 4)
                    for n, (part, _) in enumerate(PARTS):
                        sp.dma_start(RH[4 * n:4 * n + 4, q % 2, :, :],
                                     scratch[part, ds(2 * t, 2), :, cols].rearrange("a m c -> m a c")).then_inc(rh_loaded[q % 2], 16)
                    sp.dma_start(MK[:, q % 2, :], A["spline_second"][ds(t, 1), :, q * QW // 4:(q + 1) * QW // 4].rearrange("a p c -> p (a c)")).then_inc(rh_loaded[q % 2], 16)

        @block.gpsimd
        def _(pool):
            pool.wait_ge(pw_ready, 1)
            with pool.Fori(0, 3) as t:
                for n in range(NS):
                    if n % 4 == 3:
                        continue
                    pool.wait_ge(wh_ready, t * NS + n + 1)
                    pool.sem_inc(pool_passed, 1)
                    pool.tensor_tensor(WL[:, ds(t, 1), n * SUB:(n + 1) * SUB], WF[:, n % 4, :],
                                       WH[:, ds(t, 1), n * SUB:(n + 1) * SUB], ALU.subtract).then_inc(wl_ready, 1)

        @block.scalar
        def _(act):
            with act.Fori(0, 3) as t:
                def high(n):
                    act.wait_ge(wf_selected, t * NS + n + 1 + SEL0)
                    nc.scalar.copy(WH[:, ds(t, 1), n * SUB:(n + 1) * SUB], WF[:, n % 4, :]).then_inc(wh_ready, 1)

                for n in range(NS):
                    act.wait_ge(pp_ready, t * NS + n + 1)
                    if n % 4 == 3:
                        act.wait_ge(wl_dve, t * (NS // 4) + n // 4 + 1)
                    else:
                        act.wait_ge(wl_ready, t * (NS // 4 * 3) + n // 4 * 3 + n % 4 + 1)
                    nc.scalar.copy(WF[:, n % 4, :], PS[2 * (n % 4)][:, :]).then_inc(wf_copied, 1)
                    if n:
                        high(n - 1)
                high(NS - 1)

        @block.tensor
        def _(pe):
            pe.wait_ge(pw_ready, 1)
            with pe.Fori(0, 3) as t:
                for n in range(NS):
                    q = n // 4
                    if n % 4 == 0:
                        pe.wait_ge(rh_loaded[q % 2], t * (2 * 7 * 16) + (q // 2 + 1) * 7 * 16)
                    pe.wait_ge(wf_selected, t * NS + n - 3 + SEL0)
                    for piece in range(2):
                        last = pe.matmul(PS[2 * (n % 4) + piece][:, :], PWB[:, :],
                                         RH[:, q % 2, piece, (n % 4) * SUB:(n % 4 + 1) * SUB], start=True, stop=True)
                    last.then_inc(pp_ready, 1)

        @block.vector
        def _(v):
            v.wait_ge(loaded, 16)
            v.tensor_copy(PWB[:, :], PW[:, :]).then_inc(pw_ready, 1)
            v.sem_inc(wf_selected, SEL0)
            v.sem_inc(wl_ready, 3)
            v.sem_inc(wl_dve, 1)
            with v.Fori(0, 3) as t:
                def low(n):
                    v.wait_ge(wh_ready, t * NS + n + 1)
                    v.tensor_tensor(WL[:, ds(t, 1), n * SUB:(n + 1) * SUB], WF[:, n % 4, :],
                                    WH[:, ds(t, 1), n * SUB:(n + 1) * SUB], ALU.subtract).then_inc(wl_dve, 1)

                for n in range(NS):
                    q = n // 4
                    if n % 4 == 0:
                        v.wait_ge(rh_loaded[q % 2], t * (2 * 7 * 16) + (q // 2 + 1) * 7 * 16)
                        v.sem_inc(passed, 1)
                    v.wait_ge(wf_copied, t * NS + n + 1)
                    v.sem_inc(passed, 1)
                    v.copy_predicated(WF[:, n % 4, :], MK[:, q % 2, :].bitcast(U8)[:, (n % 4) * SUB:(n % 4 + 1) * SUB],
                                      PS[2 * (n % 4) + 1][:, :]).then_inc(wf_selected, 1)
                    if n and n % 4 == 0:
                        low(n - 1)
                low(NS - 1)


BLK = 32
QT = 1024
QTILES = D * INTER // (P * QT)


def rounded(v, own, src, val, mag, inv, nb):
    blocks = lambda a: a.rearrange("p (n k) -> p n k", k=BLK)
    wide = lambda a: a.unsqueeze(2).to_broadcast([P, nb, BLK])
    own.inc(v.tensor_tensor(blocks(val), blocks(src), wide(inv), ALU.mult))
    own.wait()
    yield
    own.inc(v.tensor_scalar(mag.bitcast(U32), val.bitcast(U32), 0x7F800000, None, ALU.bitwise_and))
    own.wait()
    own.inc(v.tensor_scalar(mag, mag, 2.0 ** -6, 1.5 * 2.0 ** 20, ALU.max, ALU.mult))
    own.wait()
    yield
    own.inc(v.tensor_tensor(val, val, mag, ALU.add))
    own.wait()
    own.inc(v.tensor_tensor(val, val, mag, ALU.subtract))
    own.wait()


def quantise(v, own, src, val, mag, inv, scale, nb):
    yield from rounded(v, own, src, val, mag, inv, nb)
    yield
    blocks = val.rearrange("p (n k) -> p n k", k=BLK)
    own.inc(v.tensor_tensor(blocks, blocks, scale.unsqueeze(2).to_broadcast([P, nb, BLK]), ALU.mult))
    own.wait()


def quantised_layout(ws):
    out = []
    for w in ws:
        n, d = w.shape
        rows = w.reshape(n // P, P, d).transpose(1, 0, 2).reshape(P, -1)
        out.append(rows.reshape(P, QTILES, QT).transpose(1, 0, 2))
    return np.ascontiguousarray(np.concatenate(out))


Q_OWN = 14


class WeightQuantiser:

    def __init__(self, nc, A, SCT, store, stack):
        def sb(name, shape, dt=F32):
            return stack.enter_context(nc.sbuf_tensor(name, shape, dt))

        self.nc, self.raw, self.SCT, self.store = nc, A["ffn1_weights"], SCT, store
        self.VAL = sb("VALQ", [P, 2, QT])
        self.MAG = sb("MAGQ", [P, QT])
        self.Q = sb("QQ", [P, 2, 2, QT], F16)
        self.AM = sb("AMQ", [P, 2, QT // BLK])
        self.IV = sb("IVQ", [P, QT // BLK])
        self.MX = sb("MXQ", [P, 1])
        self.MXA = sb("MXAQ", [P, 1])
        self.EX = sb("EXQ", [P, 1])
        self.SC = sb("SCQ", [P, 1])
        sem = nc.alloc_semaphore
        self.raw_loaded, self.stored = ([sem(f"q_{n}{i}") for i in range(2)] for n in ("raw", "stored"))
        (self.mx_ready, self.all_max, self.rounded_ready, self.scale_ready, self.val_ready, self.qh_ready,
         self.ql_ready, self.own, self.sp_passed, self.pool_passed) = (sem("q_" + n) for n in (
             "mx", "all_max", "rounded", "scale", "val", "qh", "ql", "own", "sp_passed", "pool_passed"))

    def transfers(self, sp):
        def load(n, s):
            sp.dma_start(self.VAL[:, s, :], self.raw[ds(n, 1)].rearrange("a p c -> p (a c)")).then_inc(self.raw_loaded[s], 16)

        def save(n, s):
            sp.wait_ge(self.ql_ready, n + 1)
            sp.sem_inc(self.sp_passed, 1)
            sp.dma_start(self.store[ds(n, 1)].rearrange("a p c -> p (a c)"),
                         self.Q[:, s, :, :].rearrange("p a c -> p (a c)")).then_inc(self.stored[s], 16)

        last = 3 * QTILES // 2 - 1
        for s in range(2):
            sp.sem_inc(self.stored[s], 16)
            load(s, s)
        with sp.Fori(0, last) as m:
            for s in range(2):
                save(m * 2 + s, s)
                load(m * 2 + (s + 2), s)
        for s in range(2):
            save(2 * last + s, s)
        for s in range(2):
            sp.wait_ge(self.stored[s], 16 * (last + 2))

    def vector_steps(self, v, m, s):
        own, am, val = Tally(v, self.own, m * 2 + s, Q_OWN), self.AM[:, s, :], self.VAL[:, s, :]

        def step(ins):
            own.inc(ins)
            own.wait()

        v.wait_ge(self.raw_loaded[s], m * 16 + 16)
        step(v.tensor_reduce(am, self.VAL[:, s, :].rearrange("p (m k) -> p m k", k=BLK), AX.X, ALU.max,
                             apply_absolute_value=True))
        v.tensor_reduce(self.MX[:, :], am, AX.X, ALU.max).then_inc(self.mx_ready, 1)
        step(v.tensor_scalar(am, am, 1.0 / 448.0, 1e-30, ALU.mult, ALU.max))
        step(v.reciprocal(self.IV[:, :], am))
        r = rounded(v, own, self.VAL[:, s, :], val, self.MAG[:, :], self.IV[:, :], QT // BLK)
        next(r)
        next(r)
        yield
        for _ in r:
            pass
        v.sem_inc(self.rounded_ready, 1)
        v.wait_ge(self.all_max, m * 2 + (s + 1))
        step(v.tensor_scalar(self.MXA[:, :], self.MXA[:, :], 1e-30, None, ALU.max))
        power = self.MXA[:, :].bitcast(U32), 0x7F800000, None, ALU.bitwise_and
        own.inc(v.tensor_scalar(self.EX[:, :].bitcast(U32), *power))
        step(v.tensor_scalar(self.SCT[:, ds(m * 2 + s, 1)].bitcast(U32), *power))
        step(v.reciprocal(self.SC[:, :], self.EX[:, :]))
        step(v.tensor_scalar(self.SC[:, :], self.SC[:, :], 8192.0, None, ALU.mult))
        step(v.tensor_scalar(am, am, self.SC[:, 0:1], None, ALU.mult))
        v.sem_inc(self.scale_ready, 1)
        own.done()

    def largest(self, pool, m, s):
        pool.wait_ge(self.mx_ready, m * 2 + (s + 1))
        pool.sem_inc(self.pool_passed, 1)
        pool.partition_all_reduce(self.MXA[:, :], self.MX[:, :], P, RMAX).then_inc(self.all_max, 1)

    def scaled(self, pool, m, s):
        val = self.VAL[:, s, :]
        blocks = val.rearrange("p (n k) -> p n k", k=BLK)
        pool.wait_ge(self.rounded_ready, m * 2 + (s + 1))
        pool.sem_inc(self.pool_passed, 1)
        pool.wait_ge(self.scale_ready, m * 2 + (s + 1))
        pool.sem_inc(self.pool_passed, 1)
        pool.tensor_tensor(blocks, blocks, self.AM[:, s, :].unsqueeze(2).to_broadcast([P, QT // BLK, BLK]),
                           ALU.mult).then_inc(self.val_ready, 1)

    def low(self, pool, m, s):
        pool.wait_ge(self.qh_ready, m * 2 + (s + 1))
        pool.sem_inc(self.pool_passed, 1)
        pool.tensor_tensor(self.Q[:, s, 1, :], self.VAL[:, s, :], self.Q[:, s, 0, :], ALU.subtract).then_inc(self.ql_ready, 1)

    def high(self, act, m, s):
        act.wait_ge(self.val_ready, m * 2 + (s + 1))
        act.wait_ge(self.stored[s], m * 16 + 16)
        self.nc.scalar.copy(self.Q[:, s, 0, :], self.VAL[:, s, :]).then_inc(self.qh_ready, 1)


XS = 1024.0


def ffn0_phase(nc, A, X, tg, idf, WH, WL, SCL, quantiser, stack):
    def sb(name, shape, dt=F32):
        return stack.enter_context(nc.sbuf_tensor(name, shape, dt))

    sem = nc.alloc_semaphore
    XN = sb("XN0", [P, NC, D])
    XH = sb("XH0", [P, KD, S], F16)
    XL = sb("XL0", [P, KD, S], F16)
    HH = sb("HH0", [P, KI, S], F16)
    HL = sb("HL0", [P, KI, S], F16)
    SG = sb("SG0", [P, 2, S])
    HM = sb("HM0", [P, 2, S])
    ST = sb("ST0", [P, NC, 6])
    MV = sb("MV0", [P, NC, 2])
    SD = sb("SD0", [P, NC])
    RS = sb("RS0", [P, NC])
    EPS = sb("EPS0", [P, 1])
    DS = sb("DS0", [P, 4])
    T, G, U, DN = ([stack.enter_context(nc.psum_tensor(f"F{n}{i}", [P, 512], F32)) for i in range(2)] for n in "TGUD")
    (mv_ready, sd_ready, xn_ready, t_ready, xh_ready, xl_ready, gu_ready, sg_ready, hm_ready, hh_ready, hl_ready,
     dn_ready, x_added, ds_ready, own_sem) = (sem("c_" + n) for n in (
         "mv", "sd", "xn", "t", "xh", "xl", "gu", "sg", "hm", "hh", "hl", "dn", "x_added", "ds", "own"))
    passed, pe_passed = sem("c_passed"), sem("c_pe_passed")

    with nc.Block() as block:
        @block.sync
        def _(sp):
            quantiser.transfers(sp)

        @block.gpsimd
        def _(pool):
            def batch(b, more):
                with pool.Fori(0, KI // 4) as m:
                    for s in range(2):
                        if more:
                            quantiser.largest(pool, b * (QTILES // 2) + m, s)
                        for w in range(2):
                            i = 4 * m + (2 * s + w)
                            pool.wait_ge(hh_ready, b * KI + i + 1)
                            pool.sem_inc(quantiser.pool_passed, 1)
                            pool.tensor_tensor(HL[:, ds(i, 1), :], HM[:, w, :], HH[:, ds(i, 1), :],
                                               ALU.subtract).then_inc(hl_ready, 1)
                            if more and w == 0:
                                quantiser.scaled(pool, b * (QTILES // 2) + m, s)
                        if more:
                            quantiser.low(pool, b * (QTILES // 2) + m, s)

            with pool.Fori(0, B - 1) as b:
                batch(b, True)
            batch(B - 1, False)

        @block.scalar
        def _(act):
            def norm(b):
                act.wait_ge(mv_ready, b + 1)
                nc.scalar.activation(SD[:, :], MV[:, :, 1], ACT.Sqrt, bias=EPS[:, 0:1]).then_inc(sd_ready, 1)

            def high(b):
                for k in range(KD):
                    act.wait_ge(t_ready, b * KD + k + 1)
                    nc.scalar.activation(XH[:, k, :], T[k % 2][:, :], ACT.Copy, scale=XS).then_inc(xh_ready, 1)

            def batch(b, more):
                with act.Fori(0, KI // 4) as m:
                    for s in range(2):
                        for w in range(2):
                            i = 4 * m + (2 * s + w)
                            act.wait_ge(gu_ready, b * KI + i + 1)
                            act.wait_ge(hm_ready, b * KI + i + 1)
                            nc.scalar.activation(SG[:, w, :], G[w][:, :], ACT.Silu, scale=DS[:, 0:1]).then_inc(sg_ready, 1)
                            act.wait_ge(hm_ready, b * KI + i + 3)
                            nc.scalar.copy(HH[:, ds(i, 1), :], HM[:, w, :]).then_inc(hh_ready, 1)
                        if more:
                            quantiser.high(act, b * (QTILES // 2) + m, s)
                if more:
                    norm(b + 1)
                    high(b + 1)

            act.wait_ge(ds_ready, 6)
            norm(0)
            high(0)
            with act.Fori(0, B - 1) as b:
                batch(b, True)
            batch(B - 1, False)

        @block.tensor
        def _(pe):
            def transposes(b):
                for k in range(KD):
                    pe.wait_ge(xl_ready, b * KD + k + 1)
                    if k == 0:
                        pe.wait_ge(xn_ready, b * NC + NC)
                    for c in range(NC):
                        last = pe.transpose(T[k % 2][:, c * P:(c + 1) * P], XN[:, c, k * P:(k + 1) * P], idf)
                    last.then_inc(t_ready, 1)

            def down(b, u):
                for w in range(2):
                    pe.wait_ge(x_added, b * NC + 2 * u + w + 1)
                    c = 2 * u + w
                    n = 0
                    for i in range(KI):
                        for lhs, rhs in ((HH, WH), (HH, WL), (HL, WH)):
                            n += 1
                            last = pe.matmul(DN[w][:, :], lhs[:, i, c * P:(c + 1) * P], rhs[:, 2, i * D:(i + 1) * D],
                                             start=(n == 1), stop=(n == 3 * KI))
                    last.then_inc(dn_ready, 1)

            def batch(b, more):
                pe.wait_ge(xl_ready, b * KD + KD + 2)
                pe.sem_inc(pe_passed, 1)
                with pe.Fori(0, KI // 2) as u:
                    for w in range(2):
                        pe.wait_ge(hm_ready, b * KI + 2 * u + w + 1)
                        for t, bank in ((0, G[w]), (1, U[w])):
                            n = 0
                            for k in range(KD):
                                cols = ds(u * (2 * P) + (k * INTER + w * P), P)
                                for lhs, rhs in ((WH, XH), (WH, XL), (WL, XH)):
                                    n += 1
                                    last = pe.matmul(bank[:, :], lhs[:, t, cols], rhs[:, k, :],
                                                     start=(n == 1), stop=(n == 3 * KD))
                        last.then_inc(gu_ready, 1)
                pe.wait_ge(hl_ready, b * KI + KI + 2)
                pe.sem_inc(pe_passed, 1)
                down(b, 0)
                if more:
                    transposes(b + 1)
                down(b, 1)

            transposes(0)
            with pe.Fori(0, B - 1) as b:
                batch(b, True)
            batch(B - 1, False)

        @block.vector
        def _(v):
            n_own = [0]

            def step(ins):
                n_own[0] += 1
                ins.then_inc(ds_ready, 1)
                v.wait_ge(ds_ready, n_own[0])

            step(v.memset(EPS[:, :], 1e-5))
            step(v.tensor_scalar(DS[:, 0:1], SCL[:, 0:1], 2.0 ** -23, None, ALU.mult))
            step(v.reciprocal(DS[:, 1:2], SCL[:, 0:1]))
            step(v.tensor_scalar(DS[:, 1:2], DS[:, 1:2], 2.0 ** -29, None, ALU.mult))
            step(v.tensor_scalar(DS[:, 2:3], SCL[:, 0:1], SCL[:, 1:2], SCL[:, 2:3], ALU.mult, ALU.mult))
            step(v.tensor_scalar(DS[:, 2:3], DS[:, 2:3], tg[:, 2:3], 2.0 ** -7, ALU.mult, ALU.mult))
            v.sem_inc(xl_ready, 2)
            v.sem_inc(hm_ready, 2)
            v.sem_inc(hl_ready, 2)
            v.sem_inc(x_added, 2)

            def norm(b):
                for c in range(NC):
                    v.bn_stats(ST[:, c, :], X[:, ds(b * NC + c, 1), :]).then_inc(own_sem, 1)
                v.wait_ge(own_sem, b * (2 * NC) + NC)
                v.sem_inc(passed, 1)
                for c in range(NC):
                    v.bn_aggr(MV[:, c, :], ST[:, c, :]).then_inc(*((own_sem, 1) if c < NC - 1 else (mv_ready, 1)))
                v.wait_ge(sd_ready, b + 1)
                v.reciprocal(RS[:, :], SD[:, :]).then_inc(own_sem, 1)
                v.wait_ge(own_sem, b * (2 * NC) + 2 * NC)
                for c in range(NC):
                    v.tensor_scalar(XN[:, c, :], X[:, ds(b * NC + c, 1), :], MV[:, c, 0:1], RS[:, c:c + 1],
                                    ALU.subtract, ALU.mult).then_inc(xn_ready, 1)

            def low(b):
                for k in range(KD):
                    v.wait_ge(xh_ready, b * KD + k + 1)
                    v.scalar_tensor_tensor(out=XL[:, k, :], in0=T[k % 2][:, :], scalar=XS, in1=XH[:, k, :],
                                           op0=ALU.mult, op1=ALU.subtract).then_inc(xl_ready, 1)

            def add(b, u):
                for w in range(2):
                    c = 2 * u + w
                    v.wait_ge(dn_ready, b * NC + c + 1)
                    x = X[:, ds(b * NC + c, 1), :]
                    v.scalar_tensor_tensor(out=x, in0=DN[w][:, :], scalar=DS[:, 2:3], in1=x,
                                           op0=ALU.mult, op1=ALU.add).then_inc(x_added, 1)

            def batch(b, more):
                with v.Fori(0, KI // 4) as m:
                    for s in range(2):
                        tile = quantiser.vector_steps(v, b * (QTILES // 2) + m, s) if more else iter(())
                        next(tile, None)
                        for w in range(2):
                            i = 4 * m + (2 * s + w)
                            v.wait_ge(sg_ready, b * KI + i + 1)
                            v.wait_ge(hl_ready, b * KI + i + 1)
                            v.scalar_tensor_tensor(out=HM[:, w, :], in0=U[w][:, :], scalar=DS[:, 1:2], in1=SG[:, w, :],
                                                   op0=ALU.mult, op1=ALU.mult).then_inc(hm_ready, 1)
                            if w == 0:
                                next(tile, None)
                if more:
                    norm(b + 1)
                add(b, 0)
                if more:
                    low(b + 1)
                add(b, 1)

            norm(0)
            low(0)
            with v.Fori(0, B - 1) as b:
                batch(b, True)
            batch(B - 1, False)


AH, AC = 8, 64
UNITS = AH * NC


def attention_phase(nc, A, X, tg, idf, stack):
    def sb(name, shape, dt=F32):
        return stack.enter_context(nc.sbuf_tensor(name, shape, dt))

    sem = nc.alloc_semaphore
    XN = sb("XN2", [P, NC, S])
    CTX = sb("CTX2", [P, NC, S])
    QH = sb("QH2", [P, NC, S], F16)
    QL = sb("QL2", [P, NC, S], F16)
    KH = sb("KH2", [P, NC, 2, S], F16)
    KL = sb("KL2", [P, NC, 2, S], F16)
    VH = sb("VH2", [P, NC, D], F16)
    VL = sb("VL2", [P, NC, D], F16)
    PR = sb("PR2", [P, 2, S])
    PH = sb("PH2", [P, 3, S], F16)
    PL = sb("PL2", [P, 3, S], F16)
    OT = sb("OT2", [P, NC, D])
    NM = sb("NM2", [P, 2, UNITS])
    SM = sb("SM2", [P, UNITS])
    RC_ = sb("RC2", [P, UNITS])
    ST = sb("ST2", [P, NC, 6])
    MV = sb("MV2", [P, NC, 2])
    SD = sb("SD2", [P, NC])
    RS = sb("RS2", [P, NC])
    EPS = sb("EPS2", [P, 1])
    CM = sb("CM2", [P, 8])
    SB = [stack.enter_context(nc.psum_tensor(f"A_S{i}", [P, 512], F32)) for i in range(3)]
    PB = [stack.enter_context(nc.psum_tensor(f"A_P{i}", [P, 512], F32)) for i in range(2)]
    OB = [stack.enter_context(nc.psum_tensor(f"A_O{i}", [P, 512], F32)) for i in range(2)]
    TB = stack.enter_context(nc.psum_tensor("A_T", [P, 512], F32))
    (ctx_loaded, mv_ready, sd_ready, xn_ready, t_ready, t_taken, s_ready, max_ready, p_ready, pt_ready, ph_ready,
     pl_ready, o_ready, ot_ready, own_sem, passed, pre_ready, cm_ready, cm_all, cs_ready, vh_ready,
     vl_ready, kh_ready, kl_ready, qh_ready, ql_ready, rc_ready, norm_own) = (sem("d_" + n) for n in (
         "ctx", "mv", "sd", "xn", "t", "t_taken", "s", "max", "p", "pt", "ph", "pl", "o", "ot", "own", "passed", "pre", "cm", "cm_all", "cs", "vh", "vl", "kh", "kl", "qh", "ql", "rc", "norm_own"))
    NT = 2 * NC
    TT = 1 + NC
    OWN, OWN_NORM = 2 + UNITS, 2 * NC + 4
    ctx = A["ctx_2048"].rearrange("b (c p) d -> b p c d", p=P)
    half = [slice(0, AC), slice(AC, P)]

    with nc.Block() as block:
        @block.sync
        def _(sp):
            sp.dma_start(CTX[:, :, :], ctx[0]).then_inc(ctx_loaded, 16)
            with sp.Fori(1, B) as b:
                sp.wait_ge(t_ready, b * NT + (NC - NT))
                sp.sem_inc(passed, 1)
                sp.wait_ge(kl_ready, b * 2)
                sp.sem_inc(passed, 1)
                sp.wait_ge(kh_ready, b * 2)
                sp.sem_inc(passed, 1)
                sp.dma_start(CTX[:, :, :], ctx[ds(b, 1)].rearrange("a p c d -> p (a c) d")).then_inc(ctx_loaded, 16)

        @block.gpsimd
        def _(pool):
            pool.memset(KH[:, :, :, :], 0.0).then_inc(pre_ready, 1)
            pool.memset(KL[:, :, :, :], 0.0).then_inc(pre_ready, 1)
            with pool.Fori(0, B) as b:
                pool.wait_ge(cm_ready, b + 1)
                pool.sem_inc(passed, 1)
                pool.partition_all_reduce(CM[:, 1:2], CM[:, 0:1], P, RMAX).then_inc(cm_all, 1)

        @block.scalar
        def _(act):
            act.wait_ge(pre_ready, 3)
            def split(b):
                act.wait_ge(mv_ready, b + 1)
                nc.scalar.activation(SD[:, :], MV[:, :, 1], ACT.Sqrt, bias=EPS[:, 0:1]).then_inc(sd_ready, 1)
                act.wait_ge(cs_ready, b + 1)
                for par in range(2):
                    nc.scalar.activation(KH[half[par], :, par, :], CTX[half[par], :, :], ACT.Copy,
                                         scale=CM[half[par], 4:5]).then_inc(kh_ready, 1)
                act.wait_ge(xn_ready, b * NC + NC)
                nc.scalar.copy(QH[:, :, :], XN[:, :, :]).then_inc(qh_ready, 1)

            def batch(b, more):
                for k in range(NC):
                    act.wait_ge(t_ready, b * NT + k + 1)
                    nc.scalar.activation(VH[:, k, :], (SB + [TB])[k][:, :], ACT.Copy, scale=CM[:, 4:5]).then_inc(vh_ready, 1)

                def high(u):
                    act.wait_ge(pt_ready, b * UNITS + u + 1)
                    nc.scalar.activation(PH[:, u % 3, :], PB[u % 2][:, :], ACT.Copy, scale=XS).then_inc(ph_ready, 1)

                def scale(u):
                    h, q = divmod(u, NC)
                    act.wait_ge(o_ready, b * UNITS + u + 1)
                    act.wait_ge(rc_ready, b * UNITS + u + 1)
                    nc.scalar.activation(OT[:, q, h * AC:(h + 1) * AC], OB[u % 2][:, 0:AC], ACT.Copy,
                                         scale=RC_[:, u:u + 1]).then_inc(ot_ready, 1)

                for u in range(UNITS):
                    act.wait_ge(max_ready, b * UNITS + u + 1)
                    if u >= 2:
                        act.wait_ge(pt_ready, b * UNITS + u - 1)
                    nc.scalar.activation(PR[:, u % 2, :], SB[u % 3][:, :], ACT.Exp, bias=NM[:, 1, u:u + 1],
                                         scale=CM[:, 5:6], accum_out=SM[:, u:u + 1]).then_inc(p_ready, 1)
                    if u >= 1:
                        high(u - 1)
                    if u >= 3:
                        scale(u - 3)
                high(UNITS - 1)
                for u in range(UNITS - 3, UNITS):
                    scale(u)
                if more:
                    split(b + 1)

            split(0)
            with act.Fori(0, B - 1) as b:
                batch(b, True)
            batch(B - 1, False)

        @block.tensor
        def _(pe):
            with pe.Fori(0, B) as b:
                def scores(u):
                    h, q = divmod(u, NC)
                    c, par = divmod(h, 2)
                    if u >= 3:
                        pe.wait_ge(p_ready, b * UNITS + u - 2)
                    cols = slice(q * P, (q + 1) * P)
                    for i, (lhs, rhs) in enumerate(((QH, KH), (QH, KL), (QL, KH))):
                        last = pe.matmul(SB[u % 3][:, :], lhs[:, c, cols], rhs[:, c, par, :], start=(i == 0), stop=(i == 2))
                    last.then_inc(s_ready, 1)

                def turn(u):
                    pe.wait_ge(p_ready, b * UNITS + u + 1)
                    if u >= 2:
                        pe.wait_ge(pl_ready, b * UNITS + u - 1)
                    for k in range(NC):
                        last = pe.transpose(PB[u % 2][:, k * P:(k + 1) * P], PR[:, u % 2, k * P:(k + 1) * P], idf)
                    last.then_inc(pt_ready, 1)

                def weigh(u):
                    h = u // NC
                    pe.wait_ge(pl_ready, b * UNITS + u + 1)
                    if u >= 2:
                        pe.wait_ge(ot_ready, b * UNITS + u - 1)
                    n = 0
                    for k in range(NC):
                        for lhs, rhs in ((PH, VH), (PH, VL), (PL, VH)):
                            n += 1
                            last = pe.matmul(OB[u % 2][:, 0:AC], lhs[:, u % 3, k * P:(k + 1) * P],
                                             rhs[:, k, h * AC:(h + 1) * AC], start=(n == 1), stop=(n == 3 * NC))
                    last.then_inc(o_ready, 1)

                def back(c):
                    pe.wait_ge(ot_ready, b * UNITS + (c + 1) * 2 * NC)
                    pe.wait_ge(t_taken, b * TT + c + 2)
                    for k in range(NC):
                        last = pe.transpose(TB[:, k * P:(k + 1) * P], OT[:, k, c * P:(c + 1) * P], idf)
                    last.then_inc(t_ready, 1)

                pe.wait_ge(ctx_loaded, b * 16 + 16)
                for k in range(NC):
                    if k == NC - 1:
                        pe.wait_ge(t_taken, b * TT + 1)
                    for c in range(NC):
                        last = pe.transpose((SB + [TB])[k][:, c * P:(c + 1) * P], CTX[:, c, k * P:(k + 1) * P], idf)
                    last.then_inc(t_ready, 1)
                pe.wait_ge(kh_ready, b * 2 + 2)
                pe.wait_ge(kl_ready, b * 2 + 2)
                pe.wait_ge(ql_ready, b + 1)
                pe.wait_ge(vl_ready, b * (NC - 1) + NC - 1)
                pe.wait_ge(t_taken, b * TT + 2)
                scores(0)
                scores(1)
                for u in range(UNITS + 5):
                    if u + 2 < UNITS:
                        scores(u + 2)
                    if u < UNITS:
                        turn(u)
                    if 2 <= u < UNITS + 2:
                        weigh(u - 2)
                    if u >= 2 * NC + 4 and (u - 4) % (2 * NC) == 0:
                        back((u - 4) // (2 * NC) - 1)

        @block.vector
        def _(v):
            v.memset(EPS[:, :], 1e-5).then_inc(pre_ready, 1)
            v.sem_inc(t_taken, 1)
            v.wait_ge(pre_ready, 3)
            def norm(b):
                own = Tally(v, norm_own, b, OWN_NORM)
                v.wait_ge(ctx_loaded, b * 16 + 16)
                v.tensor_reduce(CM[:, 0:1], CTX[:, :, :].rearrange("p c d -> p (c d)"), AX.X, ALU.max,
                                apply_absolute_value=True).then_inc(cm_ready, 1)
                for c in range(NC):
                    own.inc(v.bn_stats(ST[:, c, :], X[:, ds(b * NC + c, 1), :]))
                own.wait()
                v.sem_inc(passed, 1)
                for c in range(NC):
                    ins = v.bn_aggr(MV[:, c, :], ST[:, c, :])
                    if c < NC - 1:
                        own.inc(ins)
                ins.then_inc(mv_ready, 1)
                v.wait_ge(cm_all, b + 1)
                own.inc(v.tensor_scalar(CM[:, 1:2], CM[:, 1:2], 1e-30, None, ALU.max))
                own.wait()
                own.inc(v.tensor_scalar(CM[:, 2:3].bitcast(U32), CM[:, 1:2].bitcast(U32), 0x7F800000, None, ALU.bitwise_and))
                own.wait()
                own.inc(v.reciprocal(CM[:, 3:4], CM[:, 2:3]))
                own.wait()
                v.tensor_scalar(CM[:, 4:5], CM[:, 3:4], 8192.0, None, ALU.mult).then_inc(cs_ready, 1)
                v.wait_ge(sd_ready, b + 1)
                own.inc(v.reciprocal(RS[:, :], SD[:, :]))
                own.wait()
                own.inc(v.tensor_scalar(RS[:, :], RS[:, :], XS, None, ALU.mult))
                own.wait()
                for c in range(NC):
                    v.tensor_scalar(XN[:, c, :], X[:, ds(b * NC + c, 1), :], MV[:, c, 0:1], RS[:, c:c + 1],
                                    ALU.subtract, ALU.mult).then_inc(xn_ready, 1)
                own.done()

            def batch(b, more):
                own = Tally(v, own_sem, b, OWN)
                own.inc(v.tensor_scalar(CM[:, 5:6], CM[:, 2:3], 2.0 ** -23 / AC, None, ALU.mult))
                own.inc(v.tensor_scalar(CM[:, 6:7], CM[:, 2:3], tg[:, 1:2], 2.0 ** -23, ALU.mult, ALU.mult))
                v.wait_ge(cs_ready, b + 1)
                for par in range(2):
                    v.wait_ge(kh_ready, b * 2 + par + 1)
                    v.scalar_tensor_tensor(out=KL[half[par], :, par, :], in0=CTX[half[par], :, :], scalar=CM[half[par], 4:5],
                                           in1=KH[half[par], :, par, :], op0=ALU.mult, op1=ALU.subtract).then_inc(kl_ready, 1)
                v.wait_ge(qh_ready, b + 1)
                v.wait_ge(xn_ready, b * NC + NC)
                v.tensor_tensor(QL[:, :, :], XN[:, :, :], QH[:, :, :], ALU.subtract).then_inc(ql_ready, 1)
                for k in range(NC):
                    v.wait_ge(vh_ready, b * NC + k + 1)
                    v.scalar_tensor_tensor(out=VL[:, k, :], in0=(SB + [TB])[k][:, :], scalar=CM[:, 4:5], in1=VH[:, k, :],
                                           op0=ALU.mult, op1=ALU.subtract).then_inc(vl_ready if k < NC - 1 else t_taken, 1)

                def top(u):
                    v.wait_ge(s_ready, b * UNITS + u + 1)
                    own.inc(v.tensor_reduce(NM[:, 0, u:u + 1], SB[u % 3][:, :], AX.X, ALU.max, negate=True))
                    own.wait()
                    v.tensor_scalar(NM[:, 1, u:u + 1], NM[:, 0, u:u + 1], CM[:, 5:6], None, ALU.mult).then_inc(max_ready, 1)

                def low(u):
                    v.wait_ge(ph_ready, b * UNITS + u + 1)
                    v.scalar_tensor_tensor(out=PL[:, u % 3, :], in0=PB[u % 2][:, :], scalar=XS, in1=PH[:, u % 3, :],
                                           op0=ALU.mult, op1=ALU.subtract).then_inc(pl_ready, 1)

                def over_sum(u):
                    v.wait_ge(p_ready, b * UNITS + u + 1)
                    v.reciprocal(RC_[:, u:u + 1], SM[:, u:u + 1]).then_inc(rc_ready, 1)

                def add(c):
                    v.wait_ge(t_ready, b * NT + NC + c + 1)
                    x = X[:, ds(b * NC + c, 1), :]
                    v.scalar_tensor_tensor(out=x, in0=TB[:, :], scalar=CM[:, 6:7], in1=x,
                                           op0=ALU.mult, op1=ALU.add).then_inc(t_taken, 1)

                top(0)
                for u in range(UNITS + 6):
                    if u + 1 < UNITS:
                        top(u + 1)
                    if 1 <= u <= UNITS:
                        low(u - 1)
                    if u < UNITS:
                        over_sum(u)
                    if u == UNITS + 1 and more:
                        norm(b + 1)
                    if u >= 2 * NC + 5 and (u - 5) % (2 * NC) == 0:
                        add((u - 5) // (2 * NC) - 1)
                v.wait_ge(t_taken, b * TT + TT + 1)
                v.sem_inc(passed, 1)
                own.done()

            norm(0)
            with v.Fori(0, B - 1) as b:
                batch(b, True)
            batch(B - 1, False)


def weights_phase(nc, SCT, store, WH, WL, SCL, idh, stack):
    def sb(name, shape, dt=F32):
        return stack.enter_context(nc.sbuf_tensor(name, shape, dt))

    sem = nc.alloc_semaphore
    GROUPS = 3 * QTILES // 2
    IN = 4
    Q = sb("QW", [P, IN, 2, 2, QT], F16)
    RT = sb("RTW", [P, 3 * QTILES])
    RS = sb("RSW", [P, 3])
    TH, TL = ([stack.enter_context(nc.psum_tensor(f"W_{n}{i}", [P, 2, NC, P], F16)) for i in range(4)] for n in "HL")
    q_loaded = [sem(f"e_q{i}") for i in range(IN)]
    tw_ready, hi_taken, lo_taken, rt_ready = (sem("e_" + n) for n in ("tw", "hi_taken", "lo_taken", "rt"))

    def dest(W, n, j):
        t, g = divmod(n, QTILES // 2)
        if t < 2:
            return W[:, t, :].rearrange("p (k i) -> p k i", k=KD)[:, :, (4 * g + j) * P:(4 * g + j + 1) * P]
        return W[:, t, :].rearrange("p (i h) -> p i h", i=KI)[:, 4 * j:4 * j + 4, g * P:(g + 1) * P]

    def ratio(n, j):
        tile = 2 * n + j // 2
        return RT[:, tile:tile + 1]

    with nc.Block() as block:
        @block.sync
        def _(sp):
            for n in range(GROUPS):
                if n >= IN:
                    sp.wait_ge(tw_ready, 4 * (n - IN + 1))
                sp.dma_start(Q[:, n % IN, :, :, :].rearrange("p t a c -> p t (a c)"),
                             store[2 * n:2 * n + 2].rearrange("t p c -> p t c")).then_inc(q_loaded[n % IN], 16)

        @block.scalar
        def _(act):
            act.wait_ge(rt_ready, 7)
            for n in range(GROUPS):
                for j in range(4):
                    act.wait_ge(tw_ready, 4 * n + j + 1)
                    nc.scalar.activation(dest(WH, n, j), TH[j][:, 0, :, :], ACT.Copy, scale=ratio(n, j)).then_inc(hi_taken, 1)

        @block.tensor
        def _(pe):
            for n in range(GROUPS):
                pe.wait_ge(q_loaded[n % IN], 16 * (n // IN + 1))
                for j in range(4):
                    if n:
                        pe.wait_ge(hi_taken, 4 * (n - 1) + j + 1)
                        pe.wait_ge(lo_taken, 4 * (n - 1) + j + 1)
                    for bank, part in ((TH[j], 0), (TL[j], 1)):
                        for k in range(NC):
                            at = (j % 2) * D + k * P
                            last = pe.transpose(bank[:, 0, k, :], Q[:, n % IN, j // 2, part, at:at + P], idh)
                    last.then_inc(tw_ready, 1)

        @block.vector
        def _(v):
            for t in range(3):
                v.tensor_reduce(SCL[:, t:t + 1], SCT[:, t * QTILES:(t + 1) * QTILES], AX.X, ALU.max).then_inc(rt_ready, 1)
            v.wait_ge(rt_ready, 3)
            v.reciprocal(RS[:, :], SCL[:, :]).then_inc(rt_ready, 1)
            v.wait_ge(rt_ready, 4)
            for t in range(3):
                tiles = slice(t * QTILES, (t + 1) * QTILES)
                v.tensor_scalar(RT[:, tiles], SCT[:, tiles], RS[:, t:t + 1], None, ALU.mult).then_inc(rt_ready, 1)
            v.wait_ge(rt_ready, 7)
            for n in range(GROUPS):
                for j in range(4):
                    v.wait_ge(tw_ready, 4 * n + j + 1)
                    v.tensor_scalar(dest(WL, n, j), TL[j][:, 0, :, :], ratio(n, j), None, ALU.mult).then_inc(lo_taken, 1)


def ffn1_phase(nc, A, X, tg, idh, WH, WL, SCL, orr, stored, stack):
    def sb(name, shape, dt=F32):
        return stack.enter_context(nc.sbuf_tensor(name, shape, dt))

    sem = nc.alloc_semaphore
    XN = sb("XN3", [P, D])
    XV = sb("XV3", [P, D])
    XM = sb("XM3", [P, D])
    XQ = sb("XQ3", [P, 2, D], F16)
    XT = sb("XT3", [P, 2, KD, P], F16)
    H = sb("H3", [P, INTER])
    V = sb("V3", [P, INTER])
    M = sb("M3", [P, INTER])
    HQ = sb("HQ3", [P, 2, INTER], F16)
    HT = sb("HT3", [P, 4, 2, 4, P], F16)
    SG = sb("SG3", [P, 2, 512])
    XA = sb("XA3", [P, D // BLK])
    XI = sb("XI3", [P, D // BLK])
    HA = sb("HA3", [P, INTER // BLK])
    HI = sb("HI3", [P, INTER // BLK])
    HX = sb("HX3", [P, 4])
    RSC = sb("RSC3", [P, 1])
    ST = sb("ST3", [P, 6])
    MV = sb("MV3", [P, 2])
    SD = sb("SD3", [P, 1])
    EPS = sb("EPS3", [P, 1])
    DS = sb("DS3", [P, 4])
    G, U, DN = ([stack.enter_context(nc.psum_tensor(f"H{n}{i}", [P, 512], F32)) for i in range(2)] for n in "GUD")
    T = [stack.enter_context(nc.psum_tensor(f"HT{i}", [P, 2, 4, P], F16)) for i in range(2)]
    (mv_ready, sd_ready, xv_ready, xh_ready, xl_ready, xt_ready, xt_taken, gu_ready, sg_ready, h_ready, hv_ready,
     hh_ready, hl_ready, ht_ready, ht_taken, dn_ready, x_added, ds_ready, x_own, s_own, h_own) = (sem("f_" + n) for n in (
         "mv", "sd", "xv", "xh", "xl", "xt", "xt_taken", "gu", "sg", "h", "hv", "hh", "hl", "ht", "ht_taken", "dn",
         "x_added", "ds", "x_own", "s_own", "h_own"))
    passed, passed_sp = sem("f_passed"), sem("f_passed_sp")
    IC = INTER // 512

    with nc.Block() as block:
        @block.sync
        def _(sp):
            with sp.Fori(0, TILES) as tt:
                sp.wait_ge(x_added, tt + 2)
                sp.sem_inc(passed_sp, 1)
                sp.dma_start(orr[:, ds(tt, 1), :], X[:, ds(tt, 1), :]).then_inc(stored, 16)
            sp.wait_ge(stored, 16 * TILES)

        @block.scalar
        def _(act):
            def deviation(tt):
                act.wait_ge(mv_ready, tt + 1)
                nc.scalar.activation(SD[:, :], MV[:, 1:2], ACT.Sqrt, bias=EPS[:, 0:1]).then_inc(sd_ready, 1)

            def prepare(tt):
                act.wait_ge(xv_ready, tt + 1)
                nc.scalar.copy(XQ[:, 0, :], XV[:, :]).then_inc(xh_ready, 1)

            def stage(tt, gate_up=True, quant=True, down=True, more=True):
                if gate_up:
                    act.wait_ge(xt_ready, tt + 1)
                    nc.scalar.copy(XT[:, :, :, :], T[0][:, :, :, :]).then_inc(xt_taken, 1)
                    if more:
                        deviation(tt + 1)

                def silu(i):
                    if gate_up:
                        act.wait_ge(gu_ready, tt * IC + i + 1)
                        act.wait_ge(h_ready, tt * IC + i + 1)
                        nc.scalar.activation(SG[:, i % 2, :], G[i % 2][:, :], ACT.Silu, scale=DS[:, 0:1]).then_inc(sg_ready, 1)

                silu(0)
                if down:
                    for q in range(4):
                        act.wait_ge(ht_ready, (tt - 2) * 4 + q + 1)
                        nc.scalar.copy(HT[:, q, :, :, :], T[q % 2][:, :, :, :]).then_inc(ht_taken, 1)
                if quant:
                    act.wait_ge(hv_ready, tt)
                    nc.scalar.copy(HQ[:, 0, :], V[:, :]).then_inc(hh_ready, 1)
                silu(1)
                if gate_up and more:
                    prepare(tt + 1)
                silu(2)
                silu(3)

            act.wait_ge(ds_ready, N_DS)
            deviation(0)
            prepare(0)
            stage(0, quant=False, down=False)
            stage(1, down=False)
            with act.Fori(2, TILES - 1) as tt:
                stage(tt)
            stage(TILES - 1, more=False)
            stage(TILES, gate_up=False)
            stage(TILES + 1, gate_up=False, quant=False)

        @block.tensor
        def _(pe):
            def products(bank, terms):
                for i, (lhs, rhs) in enumerate(terms):
                    ins = pe.matmul(bank[:, :], lhs, rhs, start=(i == 0), stop=(i == len(terms) - 1))
                return ins

            def gate_up_products(tt, i):
                pe.wait_ge(h_ready, tt * IC + i + 1)
                for t, bank in ((0, G[i % 2]), (1, U[i % 2])):
                    ins = products(bank, [(XT[:, lp, k, :], W[:, t, k * INTER + i * 512:k * INTER + (i + 1) * 512])
                                          for k in range(KD) for lp, W in ((0, WH), (0, WL), (1, WH))])
                ins.then_inc(gu_ready, 1)

            def down_products(n):
                pe.wait_ge(hl_ready, n + 1)
                for q in range(4):
                    if q >= 2:
                        pe.wait_ge(ht_taken, n * 4 + q - 1)
                    for part in range(2):
                        for k in range(4):
                            at = q * 512 + k * P
                            ins = pe.transpose(T[q % 2][:, part, k, :], HQ[:, part, at:at + P], idh)
                    ins.then_inc(ht_ready, 1)
                pe.wait_ge(x_added, n + 1)
                for q in range(4):
                    pe.wait_ge(ht_taken, n * 4 + q + 1)
                    for k in range(4):
                        for lp, W in ((0, WH), (0, WL), (1, WH)):
                            i = 4 * q + k
                            ins = pe.matmul(DN[0][:, :], HT[:, q, lp, k, :], W[:, 2, i * D:(i + 1) * D],
                                            start=(i == 0 and lp == 0 and W is WH), stop=(i == KI - 1 and lp == 1))
                ins.then_inc(dn_ready, 1)

            def stage(tt, gate_up=True, down=True):
                if gate_up:
                    pe.wait_ge(xl_ready, tt + 1)
                    pe.wait_ge(xh_ready, tt + 1)
                    for part in range(2):
                        for k in range(KD):
                            ins = pe.transpose(T[0][:, part, k, :], XQ[:, part, k * P:(k + 1) * P], idh)
                    ins.then_inc(xt_ready, 1)
                    pe.wait_ge(xt_taken, tt + 1)
                    gate_up_products(tt, 0)
                if down:
                    down_products(tt - 2)
                if gate_up:
                    for i in range(1, IC):
                        gate_up_products(tt, i)

            stage(0, down=False)
            stage(1, down=False)
            with pe.Fori(2, TILES) as tt:
                stage(tt)
            stage(TILES, gate_up=False)
            stage(TILES + 1, gate_up=False)

        @block.vector
        def _(v):
            n_ds = [0]

            def step(ins):
                n_ds[0] += 1
                ins.then_inc(ds_ready, 1)
                v.wait_ge(ds_ready, n_ds[0])

            step(v.memset(EPS[:, :], 1e-5))
            step(v.tensor_scalar(DS[:, 0:2], SCL[:, 0:2], 2.0 ** -23, None, ALU.mult))
            step(v.tensor_scalar(DS[:, 2:3], SCL[:, 2:3], tg[:, 3:4], 2.0 ** -26, ALU.mult, ALU.mult))
            assert n_ds[0] == N_DS
            v.sem_inc(h_ready, 2)
            v.sem_inc(x_added, 1)

            def moments(tt):
                own = Tally(v, s_own, tt, S_OWN)
                own.inc(v.bn_stats(ST[:, :], X[:, ds(tt, 1), :]))
                own.wait()
                v.sem_inc(passed, 1)
                v.bn_aggr(MV[:, :], ST[:, :]).then_inc(mv_ready, 1)
                own.done()

            def prepare(tt):
                own = Tally(v, x_own, tt, X_OWN)
                x = X[:, ds(tt, 1), :]
                v.wait_ge(sd_ready, tt + 1)
                own.inc(v.reciprocal(SD[:, :], SD[:, :]))
                own.wait()
                own.inc(v.tensor_scalar(XN[:, :], x, MV[:, 0:1], SD[:, 0:1], ALU.subtract, ALU.mult))
                own.wait()
                own.inc(v.tensor_reduce(XA[:, :], XN[:, :].rearrange("p (n k) -> p n k", k=BLK), AX.X, ALU.max,
                                        apply_absolute_value=True))
                own.wait()
                own.inc(v.tensor_scalar(XA[:, :], XA[:, :], 1.0 / 448.0, 1e-30, ALU.mult, ALU.max))
                own.wait()
                own.inc(v.reciprocal(XI[:, :], XA[:, :]))
                own.inc(v.tensor_scalar(XA[:, :], XA[:, :], XS, None, ALU.mult))
                own.wait()
                for _ in quantise(v, own, XN[:, :], XV[:, :], XM[:, :], XI[:, :], XA[:, :], D // BLK):
                    pass
                v.sem_inc(xv_ready, 1)
                v.wait_ge(xh_ready, tt + 1)
                v.tensor_tensor(XQ[:, 1, :], XV[:, :], XQ[:, 0, :], ALU.subtract).then_inc(xl_ready, 1)
                own.done()

            def gated(tt, i):
                v.wait_ge(sg_ready, tt * IC + i + 1)
                v.scalar_tensor_tensor(out=H[:, i * 512:(i + 1) * 512], in0=U[i % 2][:, :], scalar=DS[:, 1:2],
                                       in1=SG[:, i % 2, :], op0=ALU.mult, op1=ALU.mult).then_inc(h_ready, 1)

            def quant(tt):
                own = Tally(v, h_own, tt, H_OWN)
                v.wait_ge(h_ready, tt * IC + IC + 2)
                own.inc(v.tensor_reduce(HA[:, :], H[:, :].rearrange("p (n k) -> p n k", k=BLK), AX.X, ALU.max,
                                        apply_absolute_value=True))
                own.wait()
                own.inc(v.tensor_reduce(HX[:, 0:1], HA[:, :], AX.X, ALU.max))
                own.wait()
                own.inc(v.tensor_scalar(HX[:, 0:1], HX[:, 0:1], 1e-30, None, ALU.max))
                own.inc(v.tensor_scalar(HA[:, :], HA[:, :], 1.0 / 448.0, 1e-30, ALU.mult, ALU.max))
                own.wait()
                own.inc(v.reciprocal(HI[:, :], HA[:, :]))
                own.inc(v.tensor_scalar(HX[:, 1:2].bitcast(U32), HX[:, 0:1].bitcast(U32), 0x7F800000, None, ALU.bitwise_and))
                own.wait()
                own.inc(v.reciprocal(HX[:, 2:3], HX[:, 1:2]))
                own.wait()
                own.inc(v.tensor_scalar(HA[:, :], HA[:, :], HX[:, 2:3], 8192.0, ALU.mult, ALU.mult))
                own.wait()
                yield from quantise(v, own, H[:, :], V[:, :], M[:, :], HI[:, :], HA[:, :], INTER // BLK)
                v.sem_inc(hv_ready, 1)
                yield
                v.wait_ge(x_added, tt + 1)
                own.inc(v.tensor_scalar(RSC[:, :], HX[:, 1:2], DS[:, 2:3], None, ALU.mult))
                v.wait_ge(hh_ready, tt + 1)
                v.tensor_tensor(HQ[:, 1, :], V[:, :], HQ[:, 0, :], ALU.subtract).then_inc(hl_ready, 1)
                v.wait_ge(hl_ready, tt + 1)
                own.wait()
                own.done()

            def add(tt):
                v.wait_ge(dn_ready, tt + 1)
                x = X[:, ds(tt, 1), :]
                v.scalar_tensor_tensor(out=x, in0=DN[0][:, :], scalar=RSC[:, 0:1], in1=x,
                                       op0=ALU.mult, op1=ALU.add).then_inc(x_added, 1)

            def stage(tt, gate_up=True, quantised=True, down=True, more=True):
                if gate_up and more:
                    moments(tt + 1)
                parts = quant(tt - 1) if quantised else iter(())
                next(parts, None)
                if gate_up:
                    gated(tt, 0)
                for _ in range(3):
                    next(parts, None)
                if down:
                    add(tt - 2)
                next(parts, None)
                if gate_up:
                    gated(tt, 1)
                    if more:
                        prepare(tt + 1)
                    gated(tt, 2)
                    gated(tt, 3)

            moments(0)
            prepare(0)
            stage(0, quantised=False, down=False)
            stage(1, down=False)
            with v.Fori(2, TILES - 1) as tt:
                stage(tt)
            stage(TILES - 1, more=False)
            stage(TILES, gate_up=False)
            stage(TILES + 1, gate_up=False, quantised=False)
            v.wait_ge(x_added, TILES + 1)


N_DS = 3
S_OWN = 1
X_OWN = 12
H_OWN = 15


def extra_inputs(z):
    out = {"shape_constants": shape_constants(), **spline_constants()}
    out["spline_windows"] = windows([z[f"L0_ffn_{n}_cp"] for n in ("gate", "up", "down")])
    out["ffn1_weights"] = quantised_layout([z[f"L1_ffn_{n}_w"] for n in ("gate", "up", "down")])
    return out


PRE_DVE = 11
DVE_OWN_A = 31
WARM_START = 12
WARM_HEAD = 1
FIN_OWN_A = 10
ACT_OWN_A = 2


def build_program(nc, A, out):
    with ExitStack() as top:
        X = top.enter_context(nc.sbuf_tensor("X", [P, TILES, D], F32))
        CST = top.enter_context(nc.sbuf_tensor("CST", [P, CST_W], F32))
        IDB = top.enter_context(nc.sbuf_tensor("IDB", [P, P], BF16))
        IDH = top.enter_context(nc.sbuf_tensor("IDH", [P, P], F16))
        SCL = top.enter_context(nc.sbuf_tensor("SCL", [P, 3], F32))
        SCT = top.enter_context(nc.sbuf_tensor("SCT", [P, 3 * QTILES], F32))
        store = nc.dram_tensor("quantised_weights", [3 * QTILES, P, 2 * QT], F16).ap()
        scratch = nc.dram_tensor("spline_scratch", [3, 6, 4, RUNS], BF16).ap()
        TG = top.enter_context(nc.sbuf_tensor("TG", [P, 4], F32))
        loaded, ready, stored = nc.alloc_semaphore("loaded"), nc.alloc_semaphore("consts_ready"), nc.alloc_semaphore("stored")
        orr = out.rearrange("b (c p) d -> p (b c) d", p=P)
        xr = A["x"].rearrange("b (c p) d -> p (b c) d", p=P)
        x_loaded = nc.alloc_semaphore("x_loaded")
        with nc.Block() as block:
            @block.sync
            def _(sp):
                sp.dma_start(CST[:, :], A["shape_constants"]).then_inc(loaded, 16)
                for q, name in enumerate(("g_xattn", "g_ffn")):
                    sp.dma_start(TG[:, 2 * q:2 * q + 2], A[name].rearrange("(a n) -> a n", a=1).to_broadcast([P, 2])).then_inc(loaded, 16)
                for b in range(B):
                    sp.dma_start(X[:, b * NC:(b + 1) * NC, :], xr[:, b * NC:(b + 1) * NC, :]).then_inc(x_loaded if b else loaded, 16)

            @block.vector
            def _(v):
                v.wait_ge(loaded, 4 * 16)
                v.tensor_copy(IDB[:, :], CST[:, 0:P]).then_inc(ready, 1)
                v.tensor_copy(IDH[:, :], CST[:, 0:P]).then_inc(ready, 1)

            @block.scalar
            def _(act):
                act.wait_ge(loaded, 4 * 16)
                nc.scalar.activation(TG[:, :], TG[:, :], ACT.Tanh).then_inc(ready, 1)
                act.wait_ge(ready, 3)

        with ExitStack() as stack:
            spline = SplineCoefficients(nc, A, SCL, scratch, stack)
            mlstm_phase(nc, A, X, TG, CST, CST[:, 0:P], IDB[:, :], spline, x_loaded, stack)
        with ExitStack() as weights:
            WH = weights.enter_context(nc.sbuf_tensor("W0H", [P, 3, RUNS], F16))
            WL = weights.enter_context(nc.sbuf_tensor("W0L", [P, 3, RUNS], F16))
            with ExitStack() as stack:
                spline_phase(nc, A, WH, WL, scratch, stack)
            with ExitStack() as stack:
                ffn0_phase(nc, A, X, TG, CST[:, 0:P], WH, WL, SCL, WeightQuantiser(nc, A, SCT, store, stack), stack)
        with ExitStack() as stack:
            attention_phase(nc, A, X, TG, CST[:, 0:P], stack)
        with ExitStack() as weights:
            WH = weights.enter_context(nc.sbuf_tensor("W1H", [P, 3, RUNS], F16))
            WL = weights.enter_context(nc.sbuf_tensor("W1L", [P, 3, RUNS], F16))
            with ExitStack() as stack:
                weights_phase(nc, SCT, store, WH, WL, SCL, IDH[:, :], stack)
            with ExitStack() as stack:
                ffn1_phase(nc, A, X, TG, IDH[:, :], WH, WL, SCL, orr, stored, stack)


_INS = ["x", "ctx_2048", "g_xattn", "g_ffn", "L0_xattn_Wi", "L0_xattn_bi", "L0_xattn_Wf", "L0_xattn_bf",
        "L0_xattn_ln_scale"]


def kernel(**inputs):
    import numpy as _np
    import concourse.bacc as _bacc
    from concourse import mybir as _mybir
    from concourse.bass_utils import run_bass_kernel_spmd as _run

    nc = _bacc.Bacc("TRN2", target_bir_lowering=False, num_devices=1)
    given = {name: _np.asarray(a) for name, a in inputs.items()}
    arrays = {name: _np.ascontiguousarray(given[name]) for name in _INS}
    arrays.update(extra_inputs(given))
    arrays = {f"in_{name}_dram": a for name, a in arrays.items()}
    args = {}
    for name, a in arrays.items():
        args[name[3:-5]] = nc.dram_tensor(name, a.shape, _mybir.dt.from_np(a.dtype), kind="ExternalInput").ap()
    out = nc.dram_tensor("out_0_dram", (B, S, D), _mybir.dt.float32, kind="ExternalOutput").ap()
    build_program(nc, args, out)
    r = _run(nc, [arrays], core_ids=[0])
    return r.results[0]["out_0_dram"]
```
